# Optimizing a Trainium2 kernel written in Bass

```python
import numpy as np
import jax
import jax.numpy as jnp

def _softmax(x, axis=-1):
    return jax.nn.softmax(x, axis=axis)

def _gelu(x):
    return jax.nn.gelu(x, approximate=True)

def _silu(x):
    return jax.nn.silu(x)

def _sigmoid(x):
    return jax.nn.sigmoid(x)

def _layernorm(x, axis=-1, eps=1e-05):
    m = jnp.mean(x, axis=axis, keepdims=True)
    v = jnp.var(x, axis=axis, keepdims=True)
    return (x - m) / jnp.sqrt(v + eps)

def _scatter_add(tgt, idx, src, axis=0):
    return tgt.at[idx].add(src)

def _segment_sum(src, seg, n):
    return jax.ops.segment_sum(src, seg, n)
kernel_name = 'mk_seq_postln_d1_jaxref_r8_ec8872'

def setup_inputs(seed: int=0):
    np.random.seed(seed)
    _w = jnp.asarray

    def _L0_attn_setup():
        import jax, jax.numpy as jnp
        from jax import lax
        import numpy as np
        D_MODEL, D_INNER, D_STATE, D_CONV, DT_RANK = (256, 512, 16, 4, 128)
        B, L = (2, 128)
        key = jax.random.key(seed)
        ks = jax.random.split(key, 10)
        s = 0.02
        x = jax.random.normal(ks[0], (B, L, D_MODEL), jnp.float32)
        W_in = jax.random.normal(ks[1], (2 * D_INNER, D_MODEL), jnp.float32) * s
        conv_w = jax.random.normal(ks[2], (D_INNER, D_CONV), jnp.float32) * s
        conv_b = jax.random.normal(ks[3], (D_INNER,), jnp.float32) * s
        W_x = jax.random.normal(ks[4], (DT_RANK + 2 * D_STATE, D_INNER), jnp.float32) * s
        W_dt = jax.random.normal(ks[5], (D_INNER, DT_RANK), jnp.float32) * s
        b_dt = jax.random.normal(ks[6], (D_INNER,), jnp.float32) * s
        A_log = jnp.log(jnp.broadcast_to(jnp.arange(1, D_STATE + 1, dtype=jnp.float32), (D_INNER, D_STATE)))
        Dp = jnp.ones((D_INNER,), jnp.float32)
        W_out = jax.random.normal(ks[7], (D_MODEL, D_INNER), jnp.float32) * s
        return {'x': x, 'W_in': W_in, 'conv_w': conv_w, 'conv_b': conv_b, 'W_x': W_x, 'W_dt': W_dt, 'b_dt': b_dt, 'A_log': A_log, 'Dp': Dp, 'W_out': W_out}
    _L0_attn_in = _L0_attn_setup()

    def _L0_ffn_setup():
        import jax, jax.numpy as jnp
        import numpy as np
        H = 256
        NH = 16
        NOPE = 128
        ROPE = 64
        VD = 128
        QHD = NOPE + ROPE
        E = 16
        I = 176
        TOPK = 4
        NSH = 2
        SHI = I * NSH
        EPS = 1e-06
        B, S = (2, 128)

        def rmsnorm(x, w):
            return x * jax.lax.rsqrt(jnp.mean(x * x, axis=-1, keepdims=True) + EPS) * w
        key = jax.random.key(seed)
        ks = jax.random.split(key, 12)
        sd = lambda fan_in: 1.0 / np.sqrt(fan_in)
        return {'hidden_states': jax.random.normal(ks[0], (B, S, H), jnp.float32), 'positions': jnp.broadcast_to(jnp.arange(S, dtype=jnp.int32), (B, S)), 'ln1_w': jnp.ones((H,), jnp.float32), 'ln2_w': jnp.ones((H,), jnp.float32), 'q_w': jax.random.normal(ks[1], (NH * QHD, H), jnp.float32) * sd(H), 'kv_w': jax.random.normal(ks[2], (NH * (NOPE + VD) + ROPE, H), jnp.float32) * sd(H), 'o_w': jax.random.normal(ks[3], (H, NH * VD), jnp.float32) * sd(NH * VD), 'gate_w': jax.random.normal(ks[4], (E, H), jnp.float32) * sd(H), 'w1': jax.random.normal(ks[5], (E, 2 * I, H), jnp.float32) * sd(H), 'w2': jax.random.normal(ks[6], (E, H, I), jnp.float32) * sd(I), 'sh_gu_w': jax.random.normal(ks[7], (2 * SHI, H), jnp.float32) * sd(H), 'sh_down_w': jax.random.normal(ks[8], (H, SHI), jnp.float32) * sd(SHI)}
    _L0_ffn_in = _L0_ffn_setup()
    _d = {'L0_attn_x': _L0_attn_in['x'], 'L0_attn_W_in': _L0_attn_in['W_in'], 'L0_attn_conv_w': _L0_attn_in['conv_w'], 'L0_attn_conv_b': _L0_attn_in['conv_b'], 'L0_attn_W_x': _L0_attn_in['W_x'], 'L0_attn_W_dt': _L0_attn_in['W_dt'], 'L0_attn_b_dt': _L0_attn_in['b_dt'], 'L0_attn_A_log': _L0_attn_in['A_log'], 'L0_attn_Dp': _L0_attn_in['Dp'], 'L0_attn_W_out': _L0_attn_in['W_out'], 'L0_ffn_positions': _L0_ffn_in['positions'], 'L0_ffn_ln1_w': _L0_ffn_in['ln1_w'], 'L0_ffn_ln2_w': _L0_ffn_in['ln2_w'], 'L0_ffn_q_w': _L0_ffn_in['q_w'], 'L0_ffn_kv_w': _L0_ffn_in['kv_w'], 'L0_ffn_o_w': _L0_ffn_in['o_w'], 'L0_ffn_gate_w': _L0_ffn_in['gate_w'], 'L0_ffn_w1': _L0_ffn_in['w1'], 'L0_ffn_w2': _L0_ffn_in['w2'], 'L0_ffn_sh_gu_w': _L0_ffn_in['sh_gu_w'], 'L0_ffn_sh_down_w': _L0_ffn_in['sh_down_w']}
    _x0 = _d['L0_attn_x']
    _d['L0_attn_x'] = jax.random.normal(jax.random.fold_in(jax.random.key(seed), 1), (4, 256, 256), dtype=_x0.dtype)
    del _x0
    return _d

def reference(L0_attn_x, L0_attn_W_in, L0_attn_conv_w, L0_attn_conv_b, L0_attn_W_x, L0_attn_W_dt, L0_attn_b_dt, L0_attn_A_log, L0_attn_Dp, L0_attn_W_out, L0_ffn_positions, L0_ffn_ln1_w, L0_ffn_ln2_w, L0_ffn_q_w, L0_ffn_kv_w, L0_ffn_o_w, L0_ffn_gate_w, L0_ffn_w1, L0_ffn_w2, L0_ffn_sh_gu_w, L0_ffn_sh_down_w):

    def _L0_attn_ref(x, W_in, conv_w, conv_b, W_x, W_dt, b_dt, A_log, Dp, W_out):
        import jax, jax.numpy as jnp
        from jax import lax
        import numpy as np
        D_MODEL, D_INNER, D_STATE, D_CONV, DT_RANK = (256, 512, 16, 4, 128)
        B, L = (2, 128)
        b, l, _ = x.shape
        d_inner, d_state = A_log.shape
        dt_rank = W_dt.shape[1]
        d_conv = conv_w.shape[1]
        xz = jnp.einsum('bld,ed->ble', x, W_in)
        xp, z = jnp.split(xz, 2, axis=-1)
        xpad = jnp.pad(xp, ((0, 0), (d_conv - 1, 0), (0, 0)))
        xc = conv_b + sum((xpad[:, k:k + l, :] * conv_w[:, k] for k in range(d_conv)))
        xc = jax.nn.silu(xc)
        dbc = jnp.einsum('ble,fe->blf', xc, W_x)
        dt = dbc[..., :dt_rank]
        Bm = dbc[..., dt_rank:dt_rank + d_state]
        Cm = dbc[..., dt_rank + d_state:]
        delta = jax.nn.softplus(jnp.einsum('blr,er->ble', dt, W_dt) + b_dt)
        A = -jnp.exp(A_log)
        dA = jnp.exp(delta[..., None] * A)
        dBx = delta[..., None] * Bm[:, :, None, :] * xc[..., None]

        def step(h, inp):
            dA_t, dBx_t = inp
            h = dA_t * h + dBx_t
            return (h, h)
        h0 = jnp.zeros((b, d_inner, d_state), x.dtype)
        _, hs = lax.scan(step, h0, (jnp.swapaxes(dA, 0, 1), jnp.swapaxes(dBx, 0, 1)))
        hs = jnp.swapaxes(hs, 0, 1)
        y = jnp.einsum('bles,bls->ble', hs, Cm) + xc * Dp
        y = y * jax.nn.silu(z)
        return jnp.einsum('ble,de->bld', y, W_out)

    def _L0_ffn_ref(hidden_states, positions, ln1_w, ln2_w, q_w, kv_w, o_w, gate_w, w1, w2, sh_gu_w, sh_down_w):
        import jax, jax.numpy as jnp
        import numpy as np
        H = 256
        NH = 16
        NOPE = 128
        ROPE = 64
        VD = 128
        QHD = NOPE + ROPE
        E = 16
        I = 176
        TOPK = 4
        NSH = 2
        SHI = I * NSH
        EPS = 1e-06
        B, S = (2, 128)

        def rmsnorm(x, w):
            return x * jax.lax.rsqrt(jnp.mean(x * x, axis=-1, keepdims=True) + EPS) * w
        b, s, h = hidden_states.shape
        x = rmsnorm(hidden_states, ln1_w)
        q = jnp.einsum('bsh,dh->bsd', x, q_w).reshape(b, s, NH, QHD)[..., :NOPE]
        kv = jnp.einsum('bsh,dh->bsd', x, kv_w)
        k = kv[..., :NH * NOPE].reshape(b, s, NH, NOPE)
        v = kv[..., NH * NOPE:NH * (NOPE + VD)].reshape(b, s, NH, VD)
        scale = QHD ** (-0.5)
        scores = jnp.einsum('bqnd,bknd->bnqk', q, k) * scale
        causal = jnp.tril(jnp.ones((s, s), bool))
        scores = jnp.where(causal, scores, -1000000000.0)
        p = jax.nn.softmax(scores, axis=-1)
        attn = jnp.einsum('bnqk,bknd->bqnd', p, v).reshape(b, s, NH * VD)
        attn_out = jnp.einsum('bsd,hd->bsh', attn, o_w)
        hid = hidden_states + attn_out
        x2 = rmsnorm(hid, ln2_w).reshape(-1, h)
        logits = x2 @ gate_w.T
        probs = jax.nn.softmax(logits, axis=-1)
        top_w, top_i = jax.lax.top_k(probs, TOPK)
        top_w = top_w / jnp.sum(top_w, axis=-1, keepdims=True)
        wfull = jnp.sum(jax.nn.one_hot(top_i, E, dtype=x2.dtype) * top_w[..., None], axis=1)
        gu = jnp.einsum('th,eih->tei', x2, w1)
        g, u = (gu[..., :I], gu[..., I:])
        act = jax.nn.silu(g) * u
        down = jnp.einsum('tei,ehi->teh', act, w2)
        routed = jnp.einsum('te,teh->th', wfull, down)
        sgu = x2 @ sh_gu_w.T
        sg, su = (sgu[..., :SHI], sgu[..., SHI:])
        shared = jax.nn.silu(sg) * su @ sh_down_w.T
        return hid + (routed + shared).reshape(b, s, h)
    x = L0_attn_x
    x = _layernorm(x + _L0_attn_ref(x, L0_attn_W_in, L0_attn_conv_w, L0_attn_conv_b, L0_attn_W_x, L0_attn_W_dt, L0_attn_b_dt, L0_attn_A_log, L0_attn_Dp, L0_attn_W_out), axis=-1)
    x = _layernorm(x + _L0_ffn_ref(x, L0_ffn_positions, L0_ffn_ln1_w, L0_ffn_ln2_w, L0_ffn_q_w, L0_ffn_kv_w, L0_ffn_o_w, L0_ffn_gate_w, L0_ffn_w1, L0_ffn_w2, L0_ffn_sh_gu_w, L0_ffn_sh_down_w), axis=-1)
    return x

_drawn_inputs = setup_inputs


def setup_inputs(seed=0):
    import zlib

    import numpy as np

    out = dict(_drawn_inputs(seed))
    spreads = {'L0_attn_Dp': (1.0, 0.6), 'L0_ffn_ln1_w': (1.0, 0.2), 'L0_ffn_ln2_w': (1.0, 0.2)}
    factors = {'L0_attn_W_in': 8.0,
     'L0_attn_conv_w': 8.0,
     'L0_attn_conv_b': 8.0,
     'L0_attn_W_x': 8.0,
     'L0_attn_W_dt': 8.0,
     'L0_attn_b_dt': 8.0,
     'L0_attn_A_log': 8.0,
     'L0_attn_W_out': 8.0}
    for name, (base, spread) in spreads.items():
        noise = np.random.default_rng([zlib.crc32(name.encode()), seed]).standard_normal(out[name].shape)
        drawn = base * np.exp(spread * noise) if base else spread * noise
        out[name] = jnp.asarray(drawn.astype(out[name].dtype))
    for name, factor in factors.items():
        out[name] = (out[name] * factor).astype(out[name].dtype)
    return out
```

```python
from contextlib import ExitStack

import numpy as np
import concourse.bass as bass
from concourse import mybir

F32 = mybir.dt.float32
F32R = mybir.dt.float32r
BF16 = mybir.dt.bfloat16
ALU = mybir.AluOpType
ACT = mybir.ActivationFunctionType
AX = mybir.AxisListType

P = 128
BATCH, SEQ, D = 4, 256, 256
T = BATCH * SEQ
TT = T // P
DC = D // P
HALF = T // 2
E_IN = 512
EC = E_IN // P
NS = 16
NTAP = 4
DT_RANK = 128
CH = NTAP + 3 + NS
NH, HD, ROPE = 16, 128, 64
QSCALE = float(HD + ROPE) ** -0.5
GH = 4
NG = NH // GH
PACK = 1024
NE, EI, TOPK, NSH = 16, 176, 4, 2
SHI = NSH * EI
NEA = NE + NSH
ROWS = NE * EI + SHI
NM = (ROWS + P - 1) // P
GM = 5
NMG = NM // GM
NW = 32
FPACK = 3 * D
LN_EPS, RMS_EPS = 1e-5, 1e-6
MASKED = -1.0e30


def banks(ps, first, n=1):
    return ps[:, first:first + n, :].rearrange("p b n -> p (b n)")


def mamba_block(nc, ctx, d, keep, ps):
    def sb(name, shape, dt=F32):
        return ctx.enter_context(nc.sbuf_tensor(name, shape, dt))

    def sem(name):
        return ctx.enter_context(nc.semaphore(name))

    x1, ident, stats = keep["x1"], keep["ident"], keep["stats"]
    xT = sb("m_xT", [P, DC, T])
    w_in = sb("m_w_in", [P, DC, 2 * E_IN])
    w_x = sb("m_w_x", [P, EC, 2 * P])
    w_dt = sb("m_w_dt", [P, E_IN])
    w_out = sb("m_w_out", [P, EC, D])
    chan = sb("m_chan", [P, EC, CH])
    xpad = sb("m_xpad", [P, EC, BATCH, SEQ + NTAP - 1])
    conv = sb("m_conv", [P, EC, T])
    xc = sb("m_xc", [P, EC, T])
    z = sb("m_z", [P, EC, T])
    delta = sb("m_delta", [P, EC, T])
    du = sb("m_du", [P, EC, T])
    dt = sb("m_dt", [P, T])
    spa = sb("m_spa", [P, 2, T])
    spl = sb("m_spl", [P, 2, T])
    negA = sb("m_negA", [P, EC, NS])
    bcp = sb("m_bcp", [P, T], BF16)
    sel = sb("m_sel", [P, 2 * NS, P], BF16)
    zero = sb("m_zero", [P, HALF], BF16)
    b_sb = sb("m_b_sb", [P, 2, HALF])
    dA = sb("m_dA", [P, EC, HALF])
    dbx = sb("m_dbx", [P, EC, HALF])
    h = sb("m_h", [P, EC, HALF])
    hc = sb("m_hc", [P, EC, HALF])
    spu = hc[:].rearrange("p (a c) t -> p a (c t)", a=2)
    spt = h[:].rearrange("p (a c) t -> p a (c t)", a=2)
    bcr = du[:, 0, :]
    yT = conv

    ld_chan, ld_x, ld_w1, ld_w2, ld_wx, ld_wdt, ld_xt, ld_wo = (
        sem(f"m_ld_{n}") for n in ("chan", "x", "w1", "w2", "wx", "wdt", "xt", "wo"))
    pads_ready = sem("m_pads_ready")
    sel_zero, sel_ready = sem("m_sel_zero"), sem("m_sel_ready")
    xp_ready = sem("m_xp_ready")
    xp_free = sem("m_xp_free")
    conv_step = sem("m_conv_step")
    xc_ready = sem("m_xc_ready")
    dt_ready, dt_sb_ready = sem("m_dt_ready"), sem("m_dt_sb_ready")
    bc_ready, bc_step = sem("m_bc_ready"), sem("m_bc_step")
    dl_ready, dl_free = sem("m_dl_ready"), sem("m_dl_free")
    v_ready, e_ready, e_step = sem("m_v_ready"), sem("m_e_ready"), sem("m_e_step")
    u_ready, l_ready, t_ready = sem("m_u_ready"), sem("m_l_ready"), sem("m_t_ready")
    lt_ready, delta_ready, du_ready = sem("m_lt_ready"), sem("m_delta_ready"), sem("m_du_ready")
    a_exp, a_ready = sem("m_a_exp"), sem("m_a_ready")
    zero_ready = sem("m_zero_ready")
    y_zeroed = sem("m_y_zeroed")
    b_ready, b_sb_ready, c_ready = sem("m_b_ready"), sem("m_b_sb_ready"), sem("m_c_ready")
    dA_ready, dbx_ready = sem("m_dA_ready"), sem("m_dbx_ready")
    scan_free = sem("m_scan_free")
    h_ready = sem("m_h_ready")
    hc_ready = sem("m_hc_ready")
    hc_free = sem("m_hc_free")
    z_ready, z_raw, z_done = sem("m_z_ready"), sem("m_z_raw"), sem("m_z_done")
    y_lin, y_done = sem("m_y_lin"), sem("m_y_done")
    o_ready, o_free = sem("m_o_ready"), sem("m_o_free")
    st, ag, sq, rc, nw, ln = (sem(f"m_ln_{n}") for n in ("stat", "aggr", "sqrt", "rec", "newton", "out"))

    NCH = EC
    PER_HALF = NS * EC

    def out_bank(i):
        return 7 if i < TT // 2 else (7, 4, 5, 6)[i - TT // 2]

    def taps(c, k):
        return chan[:, c, k:k + 1]

    conv_b, b_dt, d_p = ([chan[:, c, NTAP + k:NTAP + k + 1] for c in range(EC)] for k in range(3))

    with nc.Block() as block:
        @block.sync
        def _(sp):
            sp.dma_start(xT[:], d["xT"]).then_inc(ld_x, 16)
            sp.dma_start(w_in[:, :, 0:E_IN], d["w_in"][:, :, 0:E_IN]).then_inc(ld_w1, 16)
            sp.dma_start(chan[:], d["chan"]).then_inc(ld_chan, 16)
            sp.dma_start(w_x[:], d["w_x"]).then_inc(ld_wx, 16)
            sp.dma_start(w_dt[:], d["w_dt"]).then_inc(ld_wdt, 16)
            sp.dma_start(w_in[:, :, E_IN:], d["w_in"][:, :, E_IN:]).then_inc(ld_w2, 16)
            sp.dma_start(x1[:], d["x_tok"]).then_inc(ld_xt, 16)
            sp.dma_start(w_out[:], d["w_out"]).then_inc(ld_wo, 16)

        @block.gpsimd
        def _(pool):
            nc.gpsimd.memset(xpad[:, :, :, 0:NTAP - 1], 0.0).then_inc(pads_ready, 1)
            nc.gpsimd.memset(sel[:], 0.0).then_inc(sel_zero, 1)
            nc.gpsimd.memset(zero[:], 0.0).then_inc(zero_ready, 1)
            pool.wait_ge(sel_zero, 1)
            pool.wait_ge(zero_ready, 1)
            for n, q in enumerate((0, 2, 3)):
                if n:
                    pool.wait_ge(sel_ready, n)
                v = sel[32 * q:32 * q + 32, :, :]
                nc.gpsimd.affine_select(out=v, in_=v, compare_op=ALU.not_equal, fill=1.0, base=0,
                                        pattern=[[-1, 2 * NS], [0, P]], channel_multiplier=1
                                        ).then_inc(sel_ready, 1)
            pool.wait_ge(sel_ready, 3)
            for c in range(EC):
                pool.wait_ge(l_ready, c + 1)
                pool.wait_ge(t_ready, c + 1)
                nc.gpsimd.tensor_tensor(spl[:, c % 2, :], spl[:, c % 2, :], spt[:, c % 2, :],
                                        ALU.subtract).then_inc(lt_ready, 1)
                pool.wait_ge(delta_ready, c + 1)
                nc.gpsimd.tensor_tensor(du[:, c, :], delta[:, c, :], xc[:, c, :], ALU.mult).then_inc(du_ready, 1)

            def dbx_of(half, n, s_done, s2, c):
                if c == 0:
                    pool.wait_ge(b_sb_ready, s_done + 1)
                pool.wait_ge(scan_free, n + 1)
                nc.gpsimd.tensor_tensor(dbx[:, c, :], du[:, c, half * HALF:(half + 1) * HALF], b_sb[:, s2, :],
                                        ALU.mult).then_inc(dbx_ready, 1)

            pool.wait_ge(du_ready, EC)
            for half in range(2):
                with pool.Fori(0, NS // 2) as i:
                    for s2 in range(2):
                        for c in range(EC):
                            dbx_of(half, i * (2 * EC) + (half * PER_HALF + s2 * EC + c),
                                   i * 2 + (half * NS + s2), s2, c)

        @block.tensor
        def _(pe):
            pe.wait_ge(ld_x, 16)
            pe.wait_ge(ld_w1, 16)
            for c in range(EC):
                if c >= 2:
                    pe.wait_ge(xp_free, c - 1)
                for th in range(2):
                    for k in range(DC):
                        mm = nc.tensor.matmul(ps[:, 2 * (c % 2) + th, :], w_in[:, k, c * P:(c + 1) * P],
                                              xT[:, k, th * HALF:(th + 1) * HALF], start=(k == 0), stop=(k == DC - 1))
                mm.then_inc(xp_ready, 1)
            pe.wait_ge(ld_wx, 16)
            for c in range(EC):
                pe.wait_ge(xc_ready, c + 1)
                for o in range(2):
                    for th in range(2):
                        mm = nc.tensor.matmul(ps[:, 4 + 2 * o + th, :], w_x[:, c, o * P:(o + 1) * P],
                                              xc[:, c, th * HALF:(th + 1) * HALF], start=(c == 0), stop=(c == EC - 1))
                    if c == EC - 1:
                        mm.then_inc(dt_ready if o == 0 else bc_ready, 1)
            pe.wait_ge(ld_wdt, 16)
            pe.wait_ge(dt_sb_ready, 1)
            pe.wait_ge(xp_free, EC)
            for c in range(EC):
                if c >= 2:
                    pe.wait_ge(dl_free, c - 1)
                for th in range(2):
                    mm = nc.tensor.matmul(ps[:, 2 * (c % 2) + th, :], w_dt[:, c * P:(c + 1) * P],
                                          dt[:, th * HALF:(th + 1) * HALF], start=True, stop=True)
                mm.then_inc(dl_ready, 1)

            def zero_y(half):
                if half:
                    pe.wait_ge(y_done, EC)
                else:
                    pe.wait_ge(zero_ready, 1)
                    pe.wait_ge(dl_free, EC)
                    pe.wait_ge(bc_step, 5)
                    pe.wait_ge(sel_ready, 3)
                for c in range(EC):
                    mm = nc.tensor.matmul(ps[:, c, :], zero[:, 0:P], zero[:, :], start=True, stop=False,
                                          skip_group_check=True)
                    if half == 0:
                        mm.then_inc(hc_free, 1)

            def row_of(s):
                return sel[:, bass.ds(s, 1), :].rearrange("p a n -> p (a n)")

            def broadcast_b(half, s, s_done):
                if not (isinstance(s_done, int) and s_done == 0):
                    pe.wait_ge(b_sb_ready, s_done)
                nc.tensor.matmul(ps[:, 4, :], row_of(s), bcp[:, half * HALF:(half + 1) * HALF],
                                 start=True, stop=True).then_inc(b_ready, 1)

            def broadcast_c(half, s, s2):
                nc.tensor.matmul(ps[:, 5 + s2, :], row_of(s + NS), bcp[:, half * HALF:(half + 1) * HALF],
                                 start=True, stop=True).then_inc(c_ready, 1)

            def sum_y(n, c):
                pe.wait_ge(hc_ready, n + 1)
                nc.tensor.matmul(ps[:, c, :], ident[:, :], hc[:, c, :], start=False, stop=False,
                                 skip_group_check=True).then_inc(hc_free, 1)

            def z_unit(u):
                c, th = u // 2, u % 2
                if u == 0:
                    pe.wait_ge(ld_w2, 16)
                else:
                    pe.wait_ge(z_raw, u)
                for k in range(DC):
                    mm = nc.tensor.matmul(ps[:, 7, :], w_in[:, k, E_IN + c * P:E_IN + (c + 1) * P],
                                          xT[:, k, th * HALF:(th + 1) * HALF], start=(k == 0), stop=(k == DC - 1))
                mm.then_inc(z_ready, 1)

            def out_tile(i):
                if i == 0:
                    pe.wait_ge(ld_wo, 16)
                if 1 <= i <= TT // 2:
                    pe.wait_ge(o_free, i)
                pe.wait_ge(y_done, EC if i < TT // 2 else 2 * EC)
                if i == 0:
                    pe.wait_ge(z_raw, 2 * EC)
                for c in range(EC):
                    mm = nc.tensor.matmul(ps[:, out_bank(i), 0:D], yT[:, c, i * P:(i + 1) * P],
                                          w_out[:, c, :], start=(c == 0), stop=(c == EC - 1))
                mm.then_inc(o_ready, 1)

            def state(half, s, s2):
                known = isinstance(s, int)
                if not (known and s == NS - 1):
                    broadcast_c(half, s + 1, 1 - s2)
                elif half == 0:
                    broadcast_c(1, 0, 0)
                for c in range(EC):
                    if known and half == 0 and s < 2:
                        z_unit(s * EC + c)
                    if known and half == 1 and s == 0:
                        out_tile(c)
                    if c == 2:
                        if not (known and s >= NS - 2):
                            broadcast_b(half, s + 2, s + (half * NS + 2))
                        elif half == 0:
                            broadcast_b(1, s + 2 - NS, s + 2)
                    sum_y(s * EC + (half * PER_HALF + c), c)

            for half in range(2):
                zero_y(half)
                if half == 0:
                    broadcast_b(0, 0, 0)
                    broadcast_c(0, 0, 0)
                    broadcast_b(0, 1, 1)
                state(half, 0, 0)
                state(half, 1, 1)
                with pe.Fori(1, NS // 2 - 1) as i:
                    state(half, i * 2, 0)
                    state(half, i * 2 + 1, 1)
                state(half, NS - 2, 0)
                state(half, NS - 1, 1)
            for i in range(TT // 2, TT):
                out_tile(i)

        @block.scalar
        def _(act):
            act.wait_ge(ld_chan, 16)
            nc.scalar.activation(negA[:], chan[:, :, NTAP + 3:], ACT.Exp).then_inc(a_exp, 1)
            act.wait_ge(pads_ready, 1)

            def copy_xp(c):
                act.wait_ge(xp_ready, c + 1)
                nc.scalar.activation(xpad[:, c, :, NTAP - 1:], banks(ps, 2 * (c % 2), 2).rearrange(
                    "p (b t) -> p b t", b=BATCH), ACT.Copy).then_inc(xp_free, 1)

            def silu_xc(c):
                act.wait_ge(conv_step, NTAP * (c + 1))
                nc.scalar.activation(xc[:, c, :], conv[:, c, :], ACT.Silu).then_inc(xc_ready, 1)

            copy_xp(0)
            copy_xp(1)
            copy_xp(2)
            silu_xc(0)
            copy_xp(3)
            for c in range(1, EC):
                silu_xc(c)
            act.wait_ge(dt_ready, 1)
            nc.scalar.activation(dt[:], banks(ps, 4, 2), ACT.Copy).then_inc(dt_sb_ready, 1)
            nc.scalar.preload_act_table_set("natural_log_exp_and_others")
            for c in range(EC + 1):
                if c < EC:
                    act.wait_ge(dl_ready, c + 1)
                    if c >= 2:
                        act.wait_ge(t_ready, c - 1)
                    pre = banks(ps, 2 * (c % 2), 2)
                    nc.scalar.activation(spa[:, c % 2, :], pre, ACT.Abs, bias=b_dt[c]).then_inc(e_step, 1)
                    nc.scalar.activation(conv[:, c, :], pre, ACT.Identity, bias=b_dt[c]).then_inc(dl_free, 1)
                    act.wait_ge(e_step, c + 1)
                    nc.scalar.activation(spa[:, c % 2, :], spa[:, c % 2, :], ACT.Exp, scale=-1.0).then_inc(e_ready, 1)
                if c >= 1:
                    act.wait_ge(u_ready, c)
                    if c >= 3:
                        act.wait_ge(delta_ready, c - 2)
                    nc.scalar.activation(spl[:, (c - 1) % 2, :], spu[:, (c - 1) % 2, :], ACT.Ln).then_inc(l_ready, 1)

            def copy_b(s_done, s2):
                act.wait_ge(b_ready, s_done + 1)
                if not (isinstance(s_done, int) and s_done < 2):
                    act.wait_ge(dbx_ready, s_done * EC - EC)
                nc.scalar.activation(b_sb[:, s2, :], ps[:, 4, :], ACT.Copy).then_inc(b_sb_ready, 1)

            def state(half, s, s2):
                for c in range(EC):
                    act.wait_ge(scan_free, s * EC + (half * PER_HALF + c + 1))
                    nc.scalar.activation(
                        dA[:, c, :].rearrange("p (b t) -> p b t", b=2)[:, :, 1:],
                        delta[:, c, half * HALF:(half + 1) * HALF].rearrange("p (b t) -> p b t", b=2)[:, :, 1:],
                        ACT.Exp, scale=negA[:, c, bass.ds(s, 1)]).then_inc(dA_ready, 1)
                    if c == 1 and not (isinstance(s, int) and half == 1 and s == NS - 1):
                        copy_b(s + (half * NS + 1), 1 - s2)
                    if isinstance(s, int) and half == 0 and s < 2:
                        u = s * EC + c
                        act.wait_ge(z_ready, u + 1)
                        nc.scalar.activation(z[:, u // 2, (u % 2) * HALF:(u % 2 + 1) * HALF], ps[:, 7, :],
                                             ACT.Copy).then_inc(z_raw, 1)

            act.wait_ge(delta_ready, EC)
            act.wait_ge(a_ready, 1)
            copy_b(0, 0)
            for half in range(2):
                state(half, 0, 0)
                state(half, 1, 1)
                with act.Fori(1, NS // 2 - 1) as i:
                    state(half, i * 2, 0)
                    state(half, i * 2 + 1, 1)
                state(half, NS - 2, 0)
                state(half, NS - 1, 1)
                if half == 0:
                    act.wait_ge(z_raw, 2 * EC)
                    nc.scalar.activation(z[:], z[:], ACT.Silu).then_inc(z_done, 1)
            act.wait_ge(ag, TT)
            nc.scalar.activation(stats[:, :, 2], stats[:, :, 1], ACT.Sqrt, bias=keep["eps"][:, 0:1]).then_inc(sq, 1)

        @block.vector
        def _(dve):
            nc.vector.memset(dA[:].rearrange("p c (b t) -> p c b t", b=2)[:, :, :, 0:1], 0.0).then_inc(scan_free, EC)
            dve.wait_ge(a_exp, 1)
            nc.vector.tensor_scalar(negA[:], negA[:], -1.0, None, ALU.mult).then_inc(a_ready, 1)
            for c in range(EC):
                dve.wait_ge(xp_free, c + 1)
                out = conv[:, c, :].rearrange("p (b t) -> p b t", b=BATCH)
                nc.vector.tensor_scalar(out, xpad[:, c, :, NTAP - 1:], taps(c, NTAP - 1), conv_b[c],
                                        ALU.mult, ALU.add).then_inc(conv_step, 1)
                for k in range(NTAP - 1):
                    dve.wait_ge(conv_step, NTAP * c + k + 1)
                    nc.vector.scalar_tensor_tensor(out=out, in0=xpad[:, c, :, k:k + SEQ], scalar=taps(c, k), in1=out,
                                                   op0=ALU.mult, op1=ALU.add).then_inc(conv_step, 1)
            bc = banks(ps, 6, 2)
            dve.wait_ge(bc_ready, 1)
            nc.vector.tensor_copy(bcp[:], bc).then_inc(bc_step, 1)
            dve.wait_ge(bc_step, 1)
            nc.vector.tensor_tensor(bcr[64:P, :], bc[64:P, :], bcp[64:P, :], ALU.subtract).then_inc(bc_step, 1)
            dve.wait_ge(bc_step, 2)
            nc.vector.tensor_copy(bcp[64:P, :], bcr[64:P, :]).then_inc(bc_step, 1)
            dve.wait_ge(bc_step, 3)
            nc.vector.tensor_tensor(bcr[96:P, :], bcr[96:P, :], bcp[96:P, :], ALU.subtract).then_inc(bc_step, 1)
            dve.wait_ge(bc_step, 4)
            nc.vector.tensor_copy(bcp[96:P, :], bcr[96:P, :]).then_inc(bc_step, 1)
            for c in range(EC + 1):
                if c < EC:
                    dve.wait_ge(e_ready, c + 1)
                    if c >= 2:
                        dve.wait_ge(l_ready, c - 1)
                    nc.vector.tensor_scalar(spu[:, c % 2, :], spa[:, c % 2, :], 1.0, None, ALU.add).then_inc(u_ready, 1)
                if c >= 1:
                    dve.wait_ge(lt_ready, c)
                    dve.wait_ge(dl_free, c)
                    nc.vector.scalar_tensor_tensor(out=delta[:, c - 1, :], in0=conv[:, c - 1, :], scalar=0.0,
                                                   in1=spl[:, (c - 1) % 2, :], op0=ALU.max,
                                                   op1=ALU.add).then_inc(delta_ready, 1)
                if c < EC:
                    dve.wait_ge(u_ready, c + 1)
                    if c >= 2:
                        dve.wait_ge(lt_ready, c - 1)
                    nc.vector.scalar_tensor_tensor(out=spt[:, c % 2, :], in0=spu[:, c % 2, :], scalar=-1.0,
                                                   in1=spa[:, c % 2, :], op0=ALU.add,
                                                   op1=ALU.subtract).then_inc(t_ready, 1)

            def scan(n, c):
                dve.wait_ge(dA_ready, n + 1)
                dve.wait_ge(dbx_ready, n + 1)
                nc.vector.tensor_tensor_scan(h[:, c, :], dA[:, c, :], dbx[:, c, :], 0.0, ALU.mult,
                                             ALU.add).then_inc(scan_free, 1)

            def times_c(n, s_done, s2, c):
                if c == 0:
                    dve.wait_ge(c_ready, s_done + 1)
                dve.wait_ge(scan_free, EC + n + 1)
                dve.wait_ge(hc_free, n + 1)
                nc.vector.tensor_tensor(hc[:, c, :], h[:, c, :], ps[:, 5 + s2, :], ALU.mult).then_inc(hc_ready, 1)

            def finish_y(half, c):
                toks = slice(half * HALF, (half + 1) * HALF)
                if c == 0:
                    dve.wait_ge(z_done, 1)
                dve.wait_ge(hc_free, EC + (half + 1) * PER_HALF - EC + c + 1)
                nc.vector.scalar_tensor_tensor(out=yT[:, c, toks], in0=xc[:, c, toks], scalar=d_p[c],
                                               in1=ps[:, c, :], op0=ALU.mult, op1=ALU.add).then_inc(y_lin, 1)
                dve.wait_ge(y_lin, half * EC + c + 1)
                nc.vector.tensor_tensor(yT[:, c, toks], yT[:, c, toks], z[:, c, toks], ALU.mult).then_inc(y_done, 1)

            def add_x(i):
                dve.wait_ge(o_ready, i + 1)
                if i == 0:
                    dve.wait_ge(ld_xt, 16)
                nc.vector.tensor_tensor(x1[:, i, :], x1[:, i, :], ps[:, out_bank(i), 0:D],
                                        ALU.add).then_inc(o_free, 1)

            for half in range(2):
                n0, s0 = half * PER_HALF, half * NS
                for s in (0, 1):
                    for c in range(EC):
                        scan(n0 + s * EC + c, c)
                        if c >= 1:
                            times_c(n0 + s * EC + c - 1, s0 + s, s, c - 1)
                        if half == 1 and s == 0 and c >= 2:
                            add_x(c - 2)
                    times_c(n0 + s * EC + EC - 1, s0 + s, s, EC - 1)
                    if half == 1 and s == 0:
                        add_x(2)
                        add_x(3)
                with dve.Fori(1, NS // 2) as i:
                    for s2 in range(2):
                        n = i * (2 * EC) + (n0 + s2 * EC)
                        for c in range(EC):
                            scan(n + c, c)
                            if c >= 1:
                                times_c(n + (c - 1), i * 2 + (s0 + s2), s2, c - 1)
                        times_c(n + (EC - 1), i * 2 + (s0 + s2), s2, EC - 1)
                for c in range(EC):
                    finish_y(half, c)
            for i in range(TT // 2, TT):
                add_x(i)
            layernorm(nc, dve, x1, x1, keep, lambda i: (o_free, i + 1), st, ag, sq, rc, nw, ln)


def layernorm(nc, dve, src, dst, keep, ready, st, ag, sq, rc, nw, ln):
    bn, stats = keep["bn"], keep["stats"]
    for i in range(TT):
        dve.wait_ge(*ready(i))
        nc.vector.bn_stats(bn[:, i, :], src[:, i, :]).then_inc(st, 1)
        if i >= 1:
            dve.wait_ge(st, i)
            nc.vector.bn_aggr(stats[:, i - 1, 0:2], bn[:, i - 1, :]).then_inc(ag, 1)
    dve.wait_ge(st, TT)
    nc.vector.bn_aggr(stats[:, TT - 1, 0:2], bn[:, TT - 1, :]).then_inc(ag, 1)
    dve.wait_ge(sq, 1)
    inverse_root(nc, dve, stats, 1, LN_EPS, 1.0, rc, nw)
    dve.wait_ge(nw, 4)
    for i in range(TT):
        nc.vector.tensor_scalar(dst[:, i, :], src[:, i, :], stats[:, i, 0:1], stats[:, i, 3:4],
                                ALU.subtract, ALU.mult).then_inc(ln, 1)


def inverse_root(nc, dve, stats, col, eps, scale, rc, nw):
    v, r, t, w = stats[:, :, col], stats[:, :, 3], stats[:, :, 4], stats[:, :, 5]
    nc.vector.tensor_scalar(w, v, scale, eps, ALU.mult, ALU.add).then_inc(nw, 1)
    nc.vector.reciprocal(r, stats[:, :, 2]).then_inc(rc, 1)
    dve.wait_ge(rc, 1)
    dve.wait_ge(nw, 1)
    nc.vector.tensor_tensor(t, r, r, ALU.mult).then_inc(nw, 1)
    dve.wait_ge(nw, 2)
    nc.vector.tensor_tensor(t, t, w, ALU.mult).then_inc(rc, 1)
    dve.wait_ge(rc, 2)
    nc.vector.tensor_scalar(t, t, -0.5, 1.5, ALU.mult, ALU.add).then_inc(nw, 1)
    dve.wait_ge(nw, 3)
    nc.vector.tensor_tensor(r, r, t, ALU.mult).then_inc(nw, 1)

def three_passes(nc, out, lhs, rhs, start, stop):
    (lh, ll), (rh, rl) = lhs, rhs
    nc.tensor.matmul(out, lh, rh, start=start, stop=False, skip_group_check=True)
    nc.tensor.matmul(out, lh, rl, start=False, stop=False, skip_group_check=True)
    return nc.tensor.matmul(out, ll, rh, start=False, stop=stop, skip_group_check=True)


def rms_plan(nc, ctx, keep, ps, src, ln_w, name, first_bank):
    def sem(n):
        return ctx.enter_context(nc.semaphore(f"{name}_{n}"))

    stats = keep["stats"]
    xr = ctx.enter_context(nc.sbuf_tensor(f"{name}_xr", [P, TT, D], F32))
    hi = ctx.enter_context(nc.sbuf_tensor(f"{name}_hi", [P, DC, T], F32R))
    lo = ctx.enter_context(nc.sbuf_tensor(f"{name}_lo", [P, DC, T], F32R))
    sq_done, root, rc, nw = sem("squares"), sem("root"), sem("rec"), sem("newton")
    scaled, turned, hi_done, lo_done = sem("scaled"), sem("turned"), sem("hi"), sem("lo")
    per_bank = 512 // P

    def bank(u):
        return ps[:, first_bank + u % 4, :]

    def scalar(act):
        for i in range(TT):
            nc.scalar.activation(xr[:, i, :], src[:, i, :], ACT.Square, accum_out=stats[:, i, 0:1]).then_inc(sq_done, 1)
        act.wait_ge(sq_done, TT)
        nc.scalar.activation(stats[:, :, 2], stats[:, :, 0], ACT.Sqrt, scale=1.0 / D,
                             bias=keep["eps"][:, 1:2]).then_inc(root, 1)
        for u in range(2 * DC):
            act.wait_ge(turned, u + 1)
            nc.scalar.activation(hi[:, u // 2, (u % 2) * HALF:(u % 2 + 1) * HALF], bank(u), ACT.Copy,
                                 scale=ln_w[:, u // 2:u // 2 + 1]).then_inc(hi_done, 1)

    def vector(dve):
        dve.wait_ge(root, 1)
        inverse_root(nc, dve, stats, 0, RMS_EPS, 1.0 / D, rc, nw)
        dve.wait_ge(nw, 4)
        for i in range(TT):
            nc.vector.tensor_scalar(xr[:, i, :], src[:, i, :], stats[:, i, 3:4], None, ALU.mult).then_inc(scaled, 1)
        for u in range(2 * DC):
            toks = slice((u % 2) * HALF, (u % 2 + 1) * HALF)
            dve.wait_ge(hi_done, u + 1)
            nc.vector.scalar_tensor_tensor(out=lo[:, u // 2, toks], in0=bank(u), scalar=ln_w[:, u // 2:u // 2 + 1],
                                           in1=hi[:, u // 2, toks].bitcast(F32), op0=ALU.mult,
                                           op1=ALU.subtract).then_inc(lo_done, 1)

    def tensor(pe):
        for u in range(2 * DC):
            for k in range(per_bank):
                i = (u % 2) * per_bank + k
                pe.wait_ge(scaled, i + 1)
                mm = nc.tensor.transpose(bank(u)[:, k * P:(k + 1) * P], xr[:, i, (u // 2) * P:(u // 2 + 1) * P],
                                         keep["ident"][:])
            mm.then_inc(turned, 1)

    return scalar, vector, tensor, (hi, lo), lo_done


def attention_block(nc, ctx, d, keep, ps):
    def sb(name, shape, dt=F32):
        return ctx.enter_context(nc.sbuf_tensor(name, shape, dt))

    def sem(name):
        return ctx.enter_context(nc.semaphore(f"a_{name}"))

    def split(name, shape):
        return sb(f"a_{name}h", shape, F32R), sb(f"a_{name}l", shape, F32R)

    x1, hid, ident, identb, mask = (keep[k] for k in ("x1", "hid", "ident", "identb", "mask"))
    lnw = sb("a_lnw", [P, DC])
    raw = sb("a_raw", [P, GH, PACK])
    w = split("w", [P, GH, PACK])
    q, k_ = split("q", [P, 2, T]), split("k", [P, 2, T])
    v = split("v", [P, 2, TT, 2 * HD])
    p = sb("a_p", [P, 2, 3 * P])
    pT = split("pT", [P, 2, 3 * P])
    o = split("o", [P, GH, T])
    nmax, sums, rs = (sb(f"a_{n}", [P, 4, 2]) for n in ("nmax", "sums", "rs"))

    ld_ln = sem("ld_ln")
    ld_w = [sem(f"ld_w{j}") for j in range(GH)]
    wh_done, w_done = sem("wh_done"), sem("w_done")
    hid_ready = sem("hid_ready")
    r_ready, rh_done, r_free = sem("r_ready"), sem("rh_done"), sem("r_free")
    s_ready, max_done, exp_done = sem("s_ready"), sem("max_done"), sem("exp_done")
    rs_done, norm_done = sem("rs_done"), sem("norm_done")
    pT_ready, ph_done, pl_done = sem("pT_ready"), sem("ph_done"), sem("pl_done")
    o_ready, oh_done, ol_done = sem("o_ready"), sem("oh_done"), sem("ol_done")

    rms_scalar, rms_vector, rms_tensor, xn, xn_done = rms_plan(nc, ctx, keep, ps, x1, lnw, "a_rms", 2)

    FIRST = 8
    PER_GROUP = 6 * GH + TT

    def unit(g, j, u):
        return g * PER_GROUP + (FIRST + 6 * j + u)

    def units_of(g, j):
        last = isinstance(g, int) and g == NG - 1
        return range(0) if last and j == GH - 1 else range(4) if last and j == GH - 2 else range(6)

    def out_unit(g, i):
        return unit(g, 0, i + 6 * GH - (8 if isinstance(g, int) and g == NG - 1 else 0))

    def ring(u):
        return ps[:, u % 2, :]

    def target(j_next, pair_next, tile0, u, part):
        if u < 4:
            return (q, k_)[u // 2][part][:, j_next % 2, (u % 2) * HALF:(u % 2 + 1) * HALF]
        first = tile0 + 2 * (u - 4)
        return v[part][:, pair_next % 2, first:first + 2, :].rearrange("p t d -> p (t d)")

    def step_target(j, u, part):
        return target(j + 1, j // 2 + 1, 4 * (j % 2), u, part)

    def first_target(u, part):
        return target(0, 0, 0, u, part)

    with nc.Block() as block:
        @block.sync
        def _(sp):
            sp.dma_start(lnw[:], d["ln1"]).then_inc(ld_ln, 16)
            for j in range(GH):
                sp.dma_start(raw[:, j, :], d["attn_w"][j]).then_inc(ld_w[j], 16)
            with sp.Fori(1, NG + 1) as g:
                for j in range(GH):
                    sp.wait_ge(w_done, g * GH + (j + 1 - GH))
                    sp.dma_start(raw[:, j, :], d["attn_w"][bass.ds(g * GH + j, 1)].rearrange("a p n -> (a p) n")
                                 ).then_inc(ld_w[j], 16)

        @block.gpsimd
        def _(pool):
            nc.gpsimd.tensor_copy(hid[:], x1[:]).then_inc(hid_ready, 1)

            def pack(k, j):
                pool.wait_ge(wh_done, k + 1)
                nc.gpsimd.tensor_tensor(w[1][:, j, :], raw[:, j, :], w[0][:, j, :].bitcast(F32),
                                        ALU.subtract).then_inc(w_done, 1)

            with pool.Fori(0, NG + 1) as g:
                for j in range(GH):
                    pack(g * GH + j, j)

        @block.tensor
        def _(pe):
            rms_tensor(pe)
            pe.wait_ge(xn_done, 2 * DC)

            def project(n, u, j_next, pair_next, tile0):
                if not (isinstance(n, int) and n < 2):
                    pe.wait_ge(r_free, n - 1)
                bank = ring(u)
                if u < 4:
                    for c in range(DC):
                        at = ((u // 2) * DC + c) * HD
                        toks = slice((u % 2) * HALF, (u % 2 + 1) * HALF)
                        mm = three_passes(nc, bank, [x[:, j_next % GH, at:at + HD] for x in w],
                                          [x[:, c, toks] for x in xn], c == 0, c == DC - 1)
                else:
                    for half in range(2):
                        i = tile0 + 2 * (u - 4) + half
                        for c in range(DC):
                            j = 2 * (pair_next % 2) + c
                            mm = three_passes(nc, bank[:, half * 2 * HD:(half + 1) * 2 * HD],
                                              [x[:, c, i * P:(i + 1) * P] for x in xn],
                                              [x[:, j, 512:768] for x in w], c == 0, c == DC - 1)
                mm.then_inc(r_ready, 1)

            def scores(n, j, b):
                if not (isinstance(n, int) and n < 2):
                    pe.wait_ge(exp_done, n - 1)
                bank, t0 = ps[:, 2 + b % 2, :], b * SEQ
                for first, keys, cols in ((t0, P, slice(0, P)), (t0 + P, SEQ, slice(P, 3 * P))):
                    three_passes(nc, bank[:, cols], [x[:, j % 2, first:first + P] for x in q],
                                 [x[:, j % 2, t0:t0 + keys] for x in k_], True, False)
                    diag = bank[:, cols.stop - P:cols.stop]
                    mm = nc.tensor.matmul(diag, identb[:], mask[:], start=False, stop=True, skip_group_check=True)
                mm.then_inc(s_ready, 1)

            def turn(n, b):
                pe.wait_ge(norm_done, n + 1)
                if not (isinstance(n, int) and n < 2):
                    pe.wait_ge(pl_done, n - 1)
                for blk in range(3):
                    mm = nc.tensor.transpose(ps[:, 4 + b % 2, blk * P:(blk + 1) * P], p[:, b % 2, blk * P:(blk + 1) * P],
                                             ident[:])
                mm.then_inc(pT_ready, 1)

            def weigh(n, j, b):
                pe.wait_ge(pl_done, n + 1)
                if not (isinstance(n, int) and n < 2):
                    pe.wait_ge(ol_done, n - 1)
                bank, cols = ps[:, 6 + b % 2, :], slice((j % 2) * HD, (j % 2 + 1) * HD)
                vs = [[x[:, j // 2, 2 * b + kt, cols] for x in v] for kt in range(2)]
                three_passes(nc, bank[:, 0:SEQ], vs[0], [x[:, b % 2, 0:2 * P] for x in pT], True, False)
                three_passes(nc, bank[:, P:SEQ], vs[1], [x[:, b % 2, 2 * P:3 * P] for x in pT], False,
                             True).then_inc(o_ready, 1)

            def outputs(g):
                pe.wait_ge(ol_done, g * (GH * BATCH) + GH * BATCH)
                pe.wait_ge(w_done, g * GH + 2 * GH)
                for i in range(TT):
                    pe.wait_ge(r_free, out_unit(g, i) - 1)
                    for j in range(GH):
                        mm = three_passes(nc, ring(i)[:, 0:D], [x[:, j, i * P:(i + 1) * P] for x in o],
                                          [x[:, j, 768:1024] for x in w], j == 0, j == GH - 1)
                    mm.then_inc(r_ready, 1)

            for u in range(4):
                if u == 0:
                    pe.wait_ge(w_done, 1)
                project(u, u, 0, 0, 0)
            pe.wait_ge(w_done, 2)
            for u in range(4, FIRST):
                project(u, u, 0, 0, 0)

            def step(g, j):
                n = g * (GH * BATCH) + j * BATCH
                units = units_of(g, j)

                def fill(u):
                    if u in units:
                        if u == 0:
                            pe.wait_ge(w_done, g * GH + (j + 2))
                        if u == 4:
                            pe.wait_ge(w_done, g * GH + (2 * (j // 2) + 4))
                        project(unit(g, j, u), u, j + 1, j // 2 + 1, 4 * (j % 2))

                pe.wait_ge(r_free, g * PER_GROUP + (4 if j == 0 else FIRST + 6 * j - 2))
                scores(n, j, 0)
                scores(n + 1, j, 1)
                fill(0)
                turn(n, 0)
                scores(n + 2, j, 2)
                fill(1)
                weigh(n, j, 0)
                turn(n + 1, 1)
                scores(n + 3, j, 3)
                fill(2)
                weigh(n + 1, j, 1)
                turn(n + 2, 2)
                fill(3)
                weigh(n + 2, j, 2)
                turn(n + 3, 3)
                fill(4)
                fill(5)
                weigh(n + 3, j, 3)

            for j in range(GH):
                step(0, j)
            outputs(0)
            with pe.Fori(1, NG - 1) as g:
                for j in range(GH):
                    step(g, j)
                outputs(g)
            for j in range(GH):
                step(NG - 1, j)
            outputs(NG - 1)

        @block.scalar
        def _(act):
            act.wait_ge(ld_ln, 16)
            rms_scalar(act)

            def pack(j, loads):
                act.wait_ge(ld_w[j], loads)
                nc.scalar.activation(w[0][:, j, :], raw[:, j, :], ACT.Copy).then_inc(wh_done, 1)

            def high(n, u, out):
                act.wait_ge(r_ready, n + 1)
                nc.scalar.activation(out, ring(u), ACT.Copy, scale=QSCALE if u < 2 else 1.0).then_inc(rh_done, 1)

            def exps(n, b):
                act.wait_ge(max_done, n + 1)
                if not (isinstance(n, int) and n < 2):
                    act.wait_ge(pT_ready, n - 1)
                for t, cols in ((0, slice(0, P)), (1, slice(P, 3 * P))):
                    e = nc.scalar.activation(p[:, b % 2, cols], ps[:, 2 + b % 2, cols], ACT.Exp,
                                             bias=nmax[:, b, t:t + 1], accum_out=sums[:, b, t:t + 1])
                e.then_inc(exp_done, 1)

            def high_p(n, b):
                act.wait_ge(pT_ready, n + 1)
                if not (isinstance(n, int) and n < 2):
                    act.wait_ge(o_ready, n - 1)
                nc.scalar.activation(pT[0][:, b % 2, :], ps[:, 4 + b % 2, 0:3 * P], ACT.Copy).then_inc(ph_done, 1)

            def high_o(n, j, b):
                act.wait_ge(o_ready, n + 1)
                nc.scalar.activation(o[0][:, j, b * SEQ:(b + 1) * SEQ], ps[:, 6 + b % 2, 0:SEQ],
                                     ACT.Copy).then_inc(oh_done, 1)

            for j in range(GH):
                pack(j, 16)
            for u in range(FIRST):
                high(u, u, first_target(u, 0))

            def step(g, j):
                n = g * (GH * BATCH) + j * BATCH
                units = units_of(g, j)

                def fill(u):
                    if u in units:
                        high(unit(g, j, u), u, step_target(j, u, 0))

                exps(n, 0)
                exps(n + 1, 1)
                fill(0)
                high_p(n, 0)
                pack(j, g * 16 + 32)
                exps(n + 2, 2)
                fill(1)
                high_o(n, j, 0)
                high_p(n + 1, 1)
                exps(n + 3, 3)
                fill(2)
                high_o(n + 1, j, 1)
                high_p(n + 2, 2)
                fill(3)
                high_o(n + 2, j, 2)
                high_p(n + 3, 3)
                fill(4)
                fill(5)
                high_o(n + 3, j, 3)

            for j in range(GH):
                step(0, j)
            with act.Fori(1, NG - 1) as g:
                for j in range(GH):
                    step(g, j)
            for j in range(GH):
                step(NG - 1, j)

        @block.vector
        def _(dve):
            rms_vector(dve)

            def low(n, u, out, high):
                dve.wait_ge(rh_done, n + 1)
                bank = ring(u)
                if u < 2:
                    mm = nc.vector.scalar_tensor_tensor(out=out, in0=bank, scalar=QSCALE, in1=high.bitcast(F32),
                                                        op0=ALU.mult, op1=ALU.subtract)
                else:
                    mm = nc.vector.tensor_tensor(out, bank, high.bitcast(F32), ALU.subtract)
                mm.then_inc(r_free, 1)

            def maxes(n, b):
                dve.wait_ge(s_ready, n + 1)
                for t, cols in ((0, slice(0, P)), (1, slice(P, 3 * P))):
                    m = nc.vector.tensor_reduce(nmax[:, b, t:t + 1], ps[:, 2 + b % 2, cols], AX.X, ALU.max, negate=True)
                m.then_inc(max_done, 1)

            def normalize(n, b):
                dve.wait_ge(exp_done, n + 1)
                nc.vector.reciprocal(rs[:, b, :], sums[:, b, :]).then_inc(rs_done, 1)
                dve.wait_ge(rs_done, n + 1)
                for t, cols in ((0, slice(0, P)), (1, slice(P, 3 * P))):
                    m = nc.vector.tensor_scalar(p[:, b % 2, cols], p[:, b % 2, cols], rs[:, b, t:t + 1], None, ALU.mult)
                m.then_inc(norm_done, 1)

            def low_p(n, b):
                dve.wait_ge(ph_done, n + 1)
                nc.vector.tensor_tensor(pT[1][:, b % 2, :], ps[:, 4 + b % 2, 0:3 * P], pT[0][:, b % 2, :].bitcast(F32),
                                        ALU.subtract).then_inc(pl_done, 1)

            def low_o(n, j, b):
                toks = slice(b * SEQ, (b + 1) * SEQ)
                dve.wait_ge(oh_done, n + 1)
                nc.vector.tensor_tensor(o[1][:, j, toks], ps[:, 6 + b % 2, 0:SEQ], o[0][:, j, toks].bitcast(F32),
                                        ALU.subtract).then_inc(ol_done, 1)

            def add_output(g):
                for i in range(TT):
                    dve.wait_ge(r_ready, out_unit(g, i) + 1)
                    nc.vector.tensor_tensor(hid[:, i, :], hid[:, i, :], ring(i)[:, 0:D], ALU.add).then_inc(r_free, 1)

            for u in range(FIRST):
                low(u, u, first_target(u, 1), first_target(u, 0))
            dve.wait_ge(hid_ready, 1)

            def step(g, j):
                n = g * (GH * BATCH) + j * BATCH
                units = units_of(g, j)

                def fill(u):
                    if u in units:
                        low(g * (6 * GH) + (FIRST + 6 * j + u), u, step_target(j, u, 1), step_target(j, u, 0))

                maxes(n, 0)
                maxes(n + 1, 1)
                normalize(n, 0)
                fill(0)
                maxes(n + 2, 2)
                low_p(n, 0)
                normalize(n + 1, 1)
                fill(1)
                low_o(n, j, 0)
                maxes(n + 3, 3)
                low_p(n + 1, 1)
                normalize(n + 2, 2)
                fill(2)
                low_o(n + 1, j, 1)
                low_p(n + 2, 2)
                normalize(n + 3, 3)
                fill(3)
                low_o(n + 2, j, 2)
                low_p(n + 3, 3)
                fill(4)
                fill(5)
                low_o(n + 3, j, 3)

            for j in range(GH):
                step(0, j)
            add_output(0)
            with dve.Fori(1, NG - 1) as g:
                for j in range(GH):
                    step(g, j)
                add_output(g)
            for j in range(GH):
                step(NG - 1, j)
            add_output(NG - 1)


def expert_block(nc, ctx, d, keep, ps, out):
    def sb(name, shape, dt=F32):
        return ctx.enter_context(nc.sbuf_tensor(name, shape, dt))

    def sem(name):
        return ctx.enter_context(nc.semaphore(f"e_{name}"))

    def split(name, shape):
        return sb(f"e_{name}h", shape, F32R), sb(f"e_{name}l", shape, F32R)

    x1, hid, identb = (keep[k] for k in ("x1", "hid", "identb"))
    lnw = sb("e_lnw", [P, DC])
    gate_raw = sb("e_gate_raw", [P, DC, NE])
    gate = split("gate", [P, DC, NE])
    raw = sb("e_raw", [P, GM, FPACK])
    w = split("w", [P, GM, FPACK])
    lg, ex, gt, eq, cum = (sb(f"e_{n}", [P, TT, NE]) for n in ("lg", "ex", "gt", "eq", "cum"))
    top = sb("e_top", [P, TT, 8])
    cnt, tot = sb("e_cnt", [P, TT, 1]), sb("e_tot", [P, TT, 1])
    wf = sb("e_wf", [P, TT, NEA])
    wr = sb("e_wr", [P, TT, NEA])
    wp = sb("e_wp", [P, TT, P], BF16)
    wT = sb("e_wT", [P, T], BF16)
    own = sb("e_own", [P, NM, P], BF16)
    sg = sb("e_sg", [P, 2, HALF])
    aw = sb("e_aw", [P, 2, HALF])
    a = split("a", [P, GM, T])

    rms_scalar, rms_vector, rms_tensor, xn, xn_done = rms_plan(nc, ctx, keep, ps, hid, lnw, "e_rms", 0)

    ld_ln, ld_gate = sem("ld_ln"), sem("ld_gate")
    own_ones, own_done = sem("own_ones"), sem("own_done")
    ld_w = [sem(f"ld_w{j}") for j in range(GM)]
    wh_done, w_done = sem("wh_done"), sem("w_done")
    gh_done, gl_done = sem("gh_done"), sem("gl_done")
    lg_ready, rt, ex_done = sem("lg_ready"), sem("rt"), sem("ex_done")
    wp_clear, wp_done, wT_ready, wT_done = sem("wp_clear"), sem("wp_done"), sem("wT_ready"), sem("wT_done")
    g_ready, u_ready = sem("g_ready"), sem("u_ready")
    sg_done, up_done, aw_done = sem("sg_done"), sem("up_done"), sem("aw_done")
    ah_done, al_done = sem("ah_done"), sem("al_done")
    dn_ready, dn_free = sem("dn_ready"), sem("dn_free")
    x_added = sem("x_added")
    st, ag, sq, rc, nw, ln, stored = (sem(n) for n in ("stat", "aggr", "sqrt", "rec", "newton", "ln", "stored"))

    with nc.Block() as block:
        @block.sync
        def _(sp):
            sp.dma_start(lnw[:], d["ln2"]).then_inc(ld_ln, 16)
            sp.dma_start(gate_raw[:], d["gate"]).then_inc(ld_gate, 16)
            for j in range(GM):
                sp.dma_start(raw[:, j, :], d["expert_w"][j]).then_inc(ld_w[j], 16)
            with sp.Fori(1, NMG + 1) as g:
                for j in range(GM):
                    sp.wait_ge(w_done, g * GM + (j + 1 - GM))
                    sp.dma_start(raw[:, j, :], d["expert_w"][bass.ds(g * GM + j, 1)].rearrange("a p n -> (a p) n")
                                 ).then_inc(ld_w[j], 16)
            for i in range(TT):
                sp.wait_ge(ln, i + 1)
                sp.dma_start(out[:, i, :], hid[:, i, :]).then_inc(stored, 16)
            sp.wait_ge(stored, 16 * TT)

        @block.gpsimd
        def _(pool):
            nc.gpsimd.memset(wp[:], 0.0).then_inc(wp_clear, 1)
            nc.gpsimd.memset(own[:], 1.0).then_inc(own_ones, 1)
            pool.wait_ge(own_ones, 1)
            pool.wait_ge(wp_clear, 1)
            for part in range(3):
                rows = own[NW * part:NW * (part + 1), :, :]
                for sign, base in ((1, 0), (-1, EI - 1)):
                    nc.gpsimd.affine_select(out=rows, in_=rows, compare_op=ALU.is_ge, fill=0.0, base=base,
                                            pattern=[[sign * P, NM], [sign, P]], channel_multiplier=-sign * EI
                                            ).then_inc(own_done, 1)
                    pool.wait_ge(own_done, 2 * part + (1 if sign > 0 else 2))
            pool.wait_ge(gh_done, 1)
            nc.gpsimd.tensor_tensor(gate[1][:], gate_raw[:], gate[0][:].bitcast(F32), ALU.subtract).then_inc(gl_done, 1)
            with pool.Fori(0, NMG + 1) as g:
                for j in range(GM):
                    pool.wait_ge(wh_done, g * GM + (j + 1))
                    nc.gpsimd.tensor_tensor(w[1][:, j, :], raw[:, j, :], w[0][:, j, :].bitcast(F32),
                                            ALU.subtract).then_inc(w_done, 1)

        @block.tensor
        def _(pe):
            rms_tensor(pe)
            pe.wait_ge(xn_done, 2 * DC)
            pe.wait_ge(gl_done, 1)
            for i in range(TT):
                for c in range(DC):
                    mm = three_passes(nc, ps[:, 4, i * NE:(i + 1) * NE], [x[:, c, i * P:(i + 1) * P] for x in xn],
                                      [x[:, c, :] for x in gate], c == 0, c == DC - 1)
            mm.then_inc(lg_ready, 1)

            def gate_up(g, k, th):
                n = g * (2 * GM) + (2 * k + th)
                toks = slice(th * HALF, (th + 1) * HALF)
                first = isinstance(g, int) and g == 0 and k == 0
                if th == 0:
                    pe.wait_ge(w_done, g * GM + (k + 1))
                for o, (free, ready) in enumerate(((sg_done, g_ready), (up_done, u_ready))):
                    if not first:
                        pe.wait_ge(free, n - 1)
                    for c in range(DC):
                        at = o * D + c * P
                        mm = three_passes(nc, ps[:, 2 * o + th, :], [x[:, k, at:at + P] for x in w],
                                          [x[:, c, toks] for x in xn], c == 0, c == DC - 1)
                    if o == 0:
                        mm.then_inc(ready, 1)
                if first and th == 0:
                    turn_weights()
                if not first:
                    pe.wait_ge(aw_done, n - 1)
                rows = own[:, bass.ds(g * GM + k, 1), :].rearrange("p a n -> p (a n)")
                nc.tensor.matmul(ps[:, 4 + th, :], rows, wT[:, toks], start=True, stop=True).then_inc(u_ready, 1)

            def turn_weights():
                pe.wait_ge(wp_done, 1)
                turned = ps[:, 6, :].bitcast(BF16)
                for i in range(TT):
                    mm = nc.tensor.transpose(turned[:, i * P:(i + 1) * P], wp[:, i, :], identb[:])
                mm.then_inc(wT_ready, 1)
                pe.wait_ge(wT_done, 1)
                pe.wait_ge(own_done, 6)

            def down(g, i):
                n = g * TT + i
                if isinstance(g, int) and g == 0 and i < 2:
                    pass
                else:
                    pe.wait_ge(dn_free, n - 1)
                for k in range(GM):
                    if i in (0, TT // 2):
                        pe.wait_ge(al_done, g * (2 * GM) + (2 * k + (i > 0) + 1))
                    mm = three_passes(nc, ps[:, 6 + i % 2, 0:D], [x[:, k, i * P:(i + 1) * P] for x in a],
                                      [x[:, k, 2 * D:3 * D] for x in w], k == 0, k == GM - 1)
                mm.then_inc(dn_ready, 1)

            def group(g):
                for k in range(GM):
                    gate_up(g, k, 0)
                    gate_up(g, k, 1)
                pe.wait_ge(w_done, g * GM + 2 * GM)
                for i in range(TT):
                    down(g, i)

            group(0)
            with pe.Fori(1, NMG) as g:
                group(g)

        @block.scalar
        def _(act):
            act.wait_ge(ld_gate, 16)
            nc.scalar.activation(gate[0][:], gate_raw[:], ACT.Copy).then_inc(gh_done, 1)
            act.wait_ge(ld_ln, 16)

            def pack(j, loads):
                act.wait_ge(ld_w[j], loads)
                nc.scalar.activation(w[0][:, j, :], raw[:, j, :], ACT.Copy).then_inc(wh_done, 1)

            rms_scalar(act)
            for j in range(GM):
                pack(j, 16)
            act.wait_ge(rt, 2)
            nc.scalar.activation(ex[:], ex[:], ACT.Exp).then_inc(ex_done, 1)

            def silu(n, th):
                act.wait_ge(g_ready, n + 1)
                if not (isinstance(n, int) and n < 2):
                    act.wait_ge(aw_done, n - 1)
                nc.scalar.activation(sg[:, th, :], ps[:, th, :], ACT.Silu).then_inc(sg_done, 1)

            def high(n, k, th):
                act.wait_ge(aw_done, n + 1)
                nc.scalar.activation(a[0][:, k, th * HALF:(th + 1) * HALF], aw[:, th, :], ACT.Copy).then_inc(ah_done, 1)

            def group(g):
                for k in range(GM):
                    n = g * (2 * GM) + 2 * k
                    silu(n, 0)
                    silu(n + 1, 1)
                    high(n, k, 0)
                    high(n + 1, k, 1)
                    pack(k, g * 16 + 32)

            group(0)
            with act.Fori(1, NMG) as g:
                group(g)
            act.wait_ge(ag, TT)
            nc.scalar.activation(keep["stats"][:, :, 2], keep["stats"][:, :, 1], ACT.Sqrt,
                                 bias=keep["eps"][:, 0:1]).then_inc(sq, 1)

        @block.vector
        def _(dve):
            rms_vector(dve)
            step = [0]

            def chain(ins):
                step[0] += 1
                ins.then_inc(rt, 1)
                dve.wait_ge(rt, step[0])

            dve.wait_ge(lg_ready, 1)
            chain(nc.vector.tensor_copy(lg[:], ps[:, 4, 0:TT * NE].rearrange("p (t e) -> p t e", e=NE)))
            for i in range(TT):
                m = nc.vector.max(top[:, i, :], lg[:, i, :])
            m.then_inc(ex_done, 1)
            dve.wait_ge(ex_done, 1)
            fourth = top[:, :, TOPK - 1:TOPK].to_broadcast([P, TT, NE])
            chain(nc.vector.tensor_tensor(ex[:], lg[:], top[:, :, 0:1].to_broadcast([P, TT, NE]), ALU.subtract))
            chain(nc.vector.tensor_tensor(gt[:], lg[:], fourth, ALU.is_gt))
            chain(nc.vector.tensor_tensor(eq[:], lg[:], fourth, ALU.is_equal))
            chain(nc.vector.tensor_reduce(cnt[:, :, 0], gt[:], AX.X, ALU.add))
            for i in range(TT):
                m = nc.vector.tensor_tensor_scan(cum[:, i, :], eq[:, i, :], eq[:, i, :], cnt[:, i, 0:1],
                                                 ALU.bypass, ALU.add)
            chain(m)
            chain(nc.vector.tensor_scalar(cum[:], cum[:], float(TOPK), None, ALU.is_le))
            chain(nc.vector.tensor_tensor(eq[:], eq[:], cum[:], ALU.mult))
            chain(nc.vector.tensor_tensor(gt[:], gt[:], eq[:], ALU.add))
            dve.wait_ge(ex_done, 2)
            chain(nc.vector.tensor_tensor(ex[:], ex[:], gt[:], ALU.mult))
            chain(nc.vector.tensor_reduce(tot[:, :, 0], ex[:], AX.X, ALU.add))
            chain(nc.vector.reciprocal(tot[:], tot[:]))
            chain(nc.vector.memset(wf[:, :, NE:], 1.0))
            chain(nc.vector.tensor_tensor(wf[:, :, 0:NE], ex[:], tot[:].to_broadcast([P, TT, NE]), ALU.mult))
            dve.wait_ge(wp_clear, 1)
            chain(nc.vector.tensor_copy(wp[:, :, 0:NEA], wf[:]))
            chain(nc.vector.tensor_tensor(wr[:], wf[:], wp[:, :, 0:NEA], ALU.subtract))
            chain(nc.vector.tensor_copy(wp[:, :, NW:NW + NEA], wr[:]))
            chain(nc.vector.tensor_tensor(wr[:], wr[:], wp[:, :, NW:NW + NEA], ALU.subtract))
            nc.vector.tensor_copy(wp[:, :, 2 * NW:2 * NW + NEA], wr[:]).then_inc(wp_done, 1)
            dve.wait_ge(wT_ready, 1)
            nc.vector.tensor_copy(wT[:], ps[:, 6, :].bitcast(BF16)).then_inc(wT_done, 1)

            def products(n, th):
                dve.wait_ge(u_ready, n + 1)
                dve.wait_ge(sg_done, n + 1)
                nc.vector.tensor_tensor(sg[:, th, :], sg[:, th, :], ps[:, 2 + th, :], ALU.mult).then_inc(up_done, 1)
                dve.wait_ge(up_done, n + 1)
                if not (isinstance(n, int) and n < 2):
                    dve.wait_ge(ah_done, n - 1)
                    dve.wait_ge(al_done, n - 1)
                nc.vector.tensor_tensor(aw[:, th, :], sg[:, th, :], ps[:, 4 + th, :], ALU.mult).then_inc(aw_done, 1)

            def low(n, k, th):
                toks = slice(th * HALF, (th + 1) * HALF)
                dve.wait_ge(ah_done, n + 1)
                nc.vector.tensor_tensor(a[1][:, k, toks], aw[:, th, :], a[0][:, k, toks].bitcast(F32),
                                        ALU.subtract).then_inc(al_done, 1)

            def group(g):
                for k in range(GM):
                    n = g * (2 * GM) + 2 * k
                    products(n, 0)
                    products(n + 1, 1)
                    low(n, k, 0)
                    low(n + 1, k, 1)
                for i in range(TT):
                    dve.wait_ge(dn_ready, g * TT + (i + 1))
                    nc.vector.tensor_tensor(hid[:, i, :], hid[:, i, :], ps[:, 6 + i % 2, 0:D],
                                            ALU.add).then_inc(dn_free, 1)

            group(0)
            with dve.Fori(1, NMG) as g:
                group(g)
            for i in range(TT):
                dve.wait_ge(dn_free, (NMG - 1) * TT + i + 1)
                nc.vector.tensor_tensor(hid[:, i, :], hid[:, i, :], x1[:, i, :], ALU.add).then_inc(x_added, 1)
            layernorm(nc, dve, hid, hid, keep, lambda i: (x_added, i + 1), st, ag, sq, rc, nw, ln)


def constants(nc, ctx):
    def sb(name, shape, dt=F32):
        return ctx.enter_context(nc.sbuf_tensor(name, shape, dt))

    keep = {
        "x1": sb("x1", [P, TT, D]),
        "hid": sb("hid", [P, TT, D]),
        "ident": sb("ident", [P, P]),
        "identb": sb("identb", [P, P], BF16),
        "mask": sb("mask", [P, P], BF16),
        "bn": sb("bn", [P, TT, 6]),
        "stats": sb("stats", [P, TT, 6]),
        "eps": sb("eps", [P, 2]),
    }
    made, shaped = ctx.enter_context(nc.semaphore("c_made")), ctx.enter_context(nc.semaphore("c_shaped"))
    with nc.Block() as block:
        @block.gpsimd
        def _(pool):
            nc.gpsimd.memset(keep["ident"][:], 0.0).then_inc(made, 1)
            nc.gpsimd.memset(keep["identb"][:], 0.0).then_inc(made, 1)
            nc.gpsimd.memset(keep["mask"][:], 0.0).then_inc(made, 1)
            nc.gpsimd.memset(keep["eps"][:, 0:1], LN_EPS).then_inc(made, 1)
            nc.gpsimd.memset(keep["eps"][:, 1:2], RMS_EPS).then_inc(made, 1)
            pool.wait_ge(made, 5)
            for m in ("ident", "identb"):
                nc.gpsimd.affine_select(out=keep[m][:], in_=keep[m][:], compare_op=ALU.not_equal, fill=1.0, base=0,
                                        pattern=[[-1, P]], channel_multiplier=1).then_inc(shaped, 1)
            nc.gpsimd.affine_select(out=keep["mask"][:], in_=keep["mask"][:], compare_op=ALU.is_ge, fill=MASKED, base=0,
                                    pattern=[[-1, P]], channel_multiplier=1).then_inc(shaped, 1)
            pool.wait_ge(shaped, 3)
    return keep


def program(nc, d, out):
    with ExitStack() as ctx:
        ps = ctx.enter_context(nc.psum_tensor("ps", [P, 8, 512], F32))
        keep = constants(nc, ctx)
        with ExitStack() as part:
            mamba_block(nc, part, d, keep, ps)
        with ExitStack() as part:
            attention_block(nc, part, d, keep, ps)
        with ExitStack() as part:
            expert_block(nc, part, d, keep, ps, out)


def layouts(i):
    f = {k: np.asarray(v) for k, v in i.items()}
    x = f["L0_attn_x"].reshape(T, D)

    def t_chunks(w):
        return w.T.reshape(-1, P, w.shape[0]).transpose(1, 0, 2)

    def per_channel(v):
        return v.reshape(EC, P, -1).transpose(1, 0, 2)

    w_x = f["L0_attn_W_x"]
    bc = w_x[DT_RANK:]
    q_w = f["L0_ffn_q_w"].reshape(NH, HD + ROPE, D)[:, :HD]
    kv = f["L0_ffn_kv_w"]
    k_w, v_w = kv[:NH * HD].reshape(NH, HD, D), kv[NH * HD:2 * NH * HD].reshape(NH // 2, 2 * HD, D)
    o_w = f["L0_ffn_o_w"].reshape(D, NH, HD)
    attn_w = np.zeros((NH + GH, P, PACK), np.float32)
    for h in range(NH):
        attn_w[h, :, 0:256] = t_chunks(q_w[h]).reshape(P, -1)
        attn_w[h, :, 256:512] = t_chunks(k_w[h]).reshape(P, -1)
        attn_w[h, :, 512:768] = t_chunks(v_w[h // 2])[:, h % 2]
        attn_w[h + GH, :, 768:1024] = o_w[:, h].T
    w1, sh = f["L0_ffn_w1"], f["L0_ffn_sh_gu_w"]
    rows = np.zeros((3, NM * P, D), np.float32)
    for n in range(2):
        rows[n, :ROWS] = np.concatenate([w1[:, n * EI:(n + 1) * EI].reshape(-1, D), sh[n * SHI:(n + 1) * SHI]])
    rows[2, :ROWS] = np.concatenate([f["L0_ffn_w2"].transpose(0, 2, 1).reshape(-1, D), f["L0_ffn_sh_down_w"].T])
    expert_w = np.zeros((NM + GM, P, FPACK), np.float32)
    for m in range(NM):
        for n in range(2):
            expert_w[m, :, n * D:(n + 1) * D] = t_chunks(rows[n, m * P:(m + 1) * P]).reshape(P, -1)
        expert_w[m + GM, :, 2 * D:] = rows[2, m * P:(m + 1) * P]
    a = {
        "attn_w": attn_w, "expert_w": expert_w,
        "ln1": f["L0_ffn_ln1_w"].reshape(DC, P).T, "ln2": f["L0_ffn_ln2_w"].reshape(DC, P).T,
        "gate": t_chunks(f["L0_ffn_gate_w"]),
        "xT": t_chunks(x),
        "x_tok": x.reshape(TT, P, D).transpose(1, 0, 2),
        "w_in": t_chunks(f["L0_attn_W_in"]),
        "chan": np.concatenate([per_channel(f[k]) for k in (
            "L0_attn_conv_w", "L0_attn_conv_b", "L0_attn_b_dt", "L0_attn_Dp", "L0_attn_A_log")], axis=2),
        "w_x": t_chunks(np.concatenate([w_x[:DT_RANK], bc, bc, bc, bc])),
        "w_dt": f["L0_attn_W_dt"].T,
        "w_out": t_chunks(f["L0_attn_W_out"]),
    }
    return {k: np.ascontiguousarray(v) for k, v in a.items()}


def kernel(**inputs):
    import concourse.bacc as bacc
    from concourse.bass_utils import run_bass_kernel_spmd

    arrays = layouts(inputs)
    nc = bacc.Bacc("TRN2", target_bir_lowering=False, num_devices=1)
    d = {k: nc.dram_tensor(f"in_{k}", v.shape, mybir.dt.from_np(v.dtype), kind="ExternalInput").ap()
         for k, v in arrays.items()}
    out = nc.dram_tensor("out", (P, TT, D), F32, kind="ExternalOutput").ap()
    program(nc, d, out)
    r = run_bass_kernel_spmd(nc, [{f"in_{k}": v for k, v in arrays.items()}], core_ids=[0])
    got = r.results[0]["out"]
    return got.transpose(1, 0, 2).reshape(BATCH, SEQ, D)
```

```python
from contextlib import ExitStack

import numpy as np
import concourse.bass as bass
from concourse import mybir

F32 = mybir.dt.float32
F32R = mybir.dt.float32r
BF16 = mybir.dt.bfloat16
ALU = mybir.AluOpType
ACT = mybir.ActivationFunctionType
AX = mybir.AxisListType

P = 128
BATCH, SEQ, D = 4, 256, 256
T = BATCH * SEQ
TT = T // P
DC = D // P
HALF = T // 2
E_IN = 512
EC = E_IN // P
NS = 16
NTAP = 4
DT_RANK = 128
CH = NTAP + 3 + NS
NH, HD, ROPE = 16, 128, 64
QSCALE = float(HD + ROPE) ** -0.5
GH = 4
NG = NH // GH
PACK = 1024
NE, EI, TOPK, NSH = 16, 176, 4, 2
SHI = NSH * EI
SH_TILES = (SHI + P - 1) // P
NM_R = NE * EI // P
NM = SH_TILES + NM_R
GM = 5
NMG = NM // GM
NW = 32
FPACK = 3 * D
LN_EPS, RMS_EPS = 1e-5, 1e-6
MASKED = -1.0e30


def banks(ps, first, n=1):
    return ps[:, first:first + n, :].rearrange("p b n -> p (b n)")


def mamba_block(nc, ctx, d, keep, ps):
    def sb(name, shape, dt=F32):
        return ctx.enter_context(nc.sbuf_tensor(name, shape, dt))

    def sem(name):
        return ctx.enter_context(nc.semaphore(name))

    x1, ident, stats = keep["x1"], keep["ident"], keep["stats"]
    xT = sb("m_xT", [P, DC, T])
    w_in = sb("m_w_in", [P, DC, 2 * E_IN])
    w_x = sb("m_w_x", [P, EC, 2 * P])
    w_dt = sb("m_w_dt", [P, E_IN])
    w_out = sb("m_w_out", [P, EC, D])
    chan = sb("m_chan", [P, EC, CH])
    xpad = sb("m_xpad", [P, EC, BATCH, SEQ + NTAP - 1])
    conv = sb("m_conv", [P, EC, T])
    xc = sb("m_xc", [P, EC, T])
    z = xpad[:].rearrange("p c b t -> p c (b t)")[:, :, 0:T]
    delta = sb("m_delta", [P, EC, T])
    du = sb("m_du", [P, EC, T])
    dt = sb("m_dt", [P, T])
    spa = sb("m_spa", [P, 2, T])
    spl = sb("m_spl", [P, 2, T])
    negA = sb("m_negA", [P, EC, NS])
    bcp = sb("m_bcp", [P, T], BF16)
    sel = sb("m_sel", [P, 2 * NS, P], BF16)
    dp_diag = sb("m_dp_diag", [P, EC, P])
    b_sb = sb("m_b_sb", [P, 2, HALF])
    dA = sb("m_dA", [P, EC, HALF])
    dbx = sb("m_dbx", [P, EC, HALF])
    h = sb("m_h", [P, EC, HALF])
    hc = sb("m_hc", [P, EC, HALF])
    spu = hc[:].rearrange("p (a c) t -> p a (c t)", a=2)
    spt = h[:].rearrange("p (a c) t -> p a (c t)", a=2)
    bcr = du[:, 0, :]
    yT = conv

    ld_chan, ld_x0, ld_x1, ld_w0, ld_w1, ld_w2, ld_wx, ld_wdt, ld_wo = (
        sem(f"m_ld_{n}") for n in ("chan", "x0", "x1", "w0", "w1", "w2", "wx", "wdt", "wo"))
    pads_ready = sem("m_pads_ready")
    sel_zero, sel_ready = sem("m_sel_zero"), sem("m_sel_ready")
    pair_ready, pair_free = sem("m_pair_ready"), sem("m_pair_free")
    conv_step = sem("m_conv_step")
    xc_ready = sem("m_xc_ready")
    dt_ready, dt_sb_ready = sem("m_dt_ready"), sem("m_dt_sb_ready")
    bc_ready, bc_step = sem("m_bc_ready"), sem("m_bc_step")
    v_ready, abs_ready, e_ready = sem("m_v_ready"), sem("m_abs_ready"), sem("m_e_ready")
    u_ready, l_ready, t_ready = sem("m_u_ready"), sem("m_l_ready"), sem("m_t_ready")
    lt_ready, delta_ready, du_ready = sem("m_lt_ready"), sem("m_delta_ready"), sem("m_du_ready")
    a_exp, a_ready = sem("m_a_exp"), sem("m_a_ready")
    dp_ready = sem("m_dp_ready")
    z_ready = sem("m_z_ready")
    b_ready, b_sb_ready, c_ready = sem("m_b_ready"), sem("m_b_sb_ready"), sem("m_c_ready")
    dA_ready, dbx_ready = sem("m_dA_ready"), sem("m_dbx_ready")
    scan_free = sem("m_scan_free")
    h_ready = sem("m_h_ready")
    hc_ready = sem("m_hc_ready")
    hc_free = sem("m_hc_free")
    y_done = sem("m_y_done")
    o_ready, o_free = sem("m_o_ready"), sem("m_o_free")
    st, ag, sq, rc, nw, ln = (sem(f"m_ln_{n}") for n in ("stat", "aggr", "sqrt", "rec", "newton", "out"))

    DELTA0, Z1 = EC + 1, 2 * EC + 1
    PER_HALF = NS * EC

    def out_bank(i):
        return 7 if i < TT // 2 else (7, 4, 5, 6)[i - TT // 2]

    def taps(c, k):
        return chan[:, c, k:k + 1]

    conv_b, b_dt, d_p = ([chan[:, c, NTAP + k:NTAP + k + 1] for c in range(EC)] for k in range(3))

    with nc.Block() as block:
        @block.sync
        def _(sp):
            sp.dma_start(w_in[:, :, 0:P], d["w_in"][:, :, 0:P]).then_inc(ld_w0, 16)
            sp.dma_start(xT[:, :, 0:HALF], d["xT"][:, :, 0:HALF]).then_inc(ld_x0, 16)
            sp.dma_start(xT[:, :, HALF:], d["xT"][:, :, HALF:]).then_inc(ld_x1, 16)
            sp.dma_start(chan[:], d["chan"]).then_inc(ld_chan, 16)
            sp.dma_start(w_in[:, :, P:E_IN], d["w_in"][:, :, P:E_IN]).then_inc(ld_w1, 16)
            sp.dma_start(w_x[:], d["w_x"]).then_inc(ld_wx, 16)
            sp.dma_start(w_dt[:], d["w_dt"]).then_inc(ld_wdt, 16)
            sp.dma_start(w_in[:, :, E_IN:], d["w_in"][:, :, E_IN:]).then_inc(ld_w2, 16)
            sp.dma_start(w_out[:], d["w_out"]).then_inc(ld_wo, 16)

        @block.gpsimd
        def _(pool):
            nc.gpsimd.memset(xpad[:, :, :, 0:NTAP - 1], 0.0).then_inc(pads_ready, 1)
            nc.gpsimd.memset(sel[:], 0.0).then_inc(sel_zero, 1)
            pool.wait_ge(sel_zero, 1)
            for n, q in enumerate((0, 2, 3)):
                if n:
                    pool.wait_ge(sel_ready, n)
                v = sel[32 * q:32 * q + 32, :, :]
                nc.gpsimd.affine_select(out=v, in_=v, compare_op=ALU.not_equal, fill=1.0, base=0,
                                        pattern=[[-1, 2 * NS], [0, P]], channel_multiplier=1
                                        ).then_inc(sel_ready, 1)
            pool.wait_ge(sel_ready, 3)
            for c in range(EC + 1):
                if c < EC:
                    pool.wait_ge(l_ready, c + 1)
                    pool.wait_ge(t_ready, c + 1)
                    nc.gpsimd.tensor_tensor(spl[:, c % 2, :], spl[:, c % 2, :], spt[:, c % 2, :],
                                            ALU.subtract).then_inc(lt_ready, 1)
                if c >= 1:
                    pool.wait_ge(delta_ready, c)
                    nc.gpsimd.tensor_tensor(du[:, c - 1, :], delta[:, c - 1, :], xc[:, c - 1, :],
                                            ALU.mult).then_inc(du_ready, 1)

            def dbx_of(half, n, s_done, s2, c):
                if c == 0:
                    pool.wait_ge(b_sb_ready, s_done + 1)
                pool.wait_ge(scan_free, n + 1)
                nc.gpsimd.tensor_tensor(dbx[:, c, :], du[:, c, half * HALF:(half + 1) * HALF], b_sb[:, s2, :],
                                        ALU.mult).then_inc(dbx_ready, 1)

            pool.wait_ge(du_ready, EC)
            for half in range(2):
                with pool.Fori(0, NS // 2) as i:
                    for s2 in range(2):
                        for c in range(EC):
                            dbx_of(half, i * (2 * EC) + (half * PER_HALF + s2 * EC + c),
                                   i * 2 + (half * NS + s2), s2, c)

        @block.tensor
        def _(pe):
            def pair(r, steps):
                if r >= 2:
                    pe.wait_ge(pair_free, r - 1)
                for th in range(2):
                    if r == 0 and th == 1:
                        pe.wait_ge(ld_x1, 16)
                    for k, (lhs, rhs) in enumerate(steps):
                        mm = nc.tensor.matmul(ps[:, 2 * (r % 2) + th, :], lhs, rhs[:, th * HALF:(th + 1) * HALF],
                                              start=(k == 0), stop=(k == len(steps) - 1))
                mm.then_inc(pair_ready, 1)

            def project_in(r, c):
                pair(r, [(w_in[:, k, c * P:(c + 1) * P], xT[:, k, :]) for k in range(DC)])

            def project_x(c):
                pe.wait_ge(xc_ready, c + 1)
                for o in range(2):
                    for th in range(2):
                        mm = nc.tensor.matmul(ps[:, 4 + 2 * o + th, :], w_x[:, c, o * P:(o + 1) * P],
                                              xc[:, c, th * HALF:(th + 1) * HALF], start=(c == 0), stop=(c == EC - 1))
                    if c == EC - 1:
                        mm.then_inc(dt_ready if o == 0 else bc_ready, 1)

            pe.wait_ge(ld_w0, 16)
            pe.wait_ge(ld_x0, 16)
            project_in(0, 0)
            pe.wait_ge(ld_w1, 16)
            for c in range(1, EC):
                project_in(c, c)
            pe.wait_ge(ld_w2, 16)
            project_in(EC, EC)
            pe.wait_ge(ld_wx, 16)
            for c in range(EC):
                project_x(c)
            pe.wait_ge(ld_wdt, 16)
            pe.wait_ge(dt_sb_ready, 1)
            for c in range(EC):
                pair(DELTA0 + c, [(w_dt[:, c * P:(c + 1) * P], dt[:])])
            for c in range(1, EC):
                project_in(Z1 + c - 1, EC + c)

            def start_y(half):
                if half == 0:
                    pe.wait_ge(dp_ready, EC)
                    pe.wait_ge(pair_free, 3 * EC)
                    pe.wait_ge(bc_step, 5)
                    pe.wait_ge(sel_ready, 3)
                for c in range(EC):
                    if half:
                        pe.wait_ge(y_done, c + 1)
                    mm = nc.tensor.matmul(ps[:, c, :], dp_diag[:, c, :], xc[:, c, half * HALF:(half + 1) * HALF],
                                          start=True, stop=False, skip_group_check=True)
                    if half == 0:
                        mm.then_inc(hc_free, 1)

            def row_of(s):
                return sel[:, bass.ds(s, 1), :].rearrange("p a n -> p (a n)")

            def broadcast_b(half, s, s_done):
                if not (isinstance(s_done, int) and s_done == 0):
                    pe.wait_ge(b_sb_ready, s_done)
                nc.tensor.matmul(ps[:, 4, :], row_of(s), bcp[:, half * HALF:(half + 1) * HALF],
                                 start=True, stop=True).then_inc(b_ready, 1)

            def broadcast_c(half, s, s2):
                nc.tensor.matmul(ps[:, 5 + s2, :], row_of(s + NS), bcp[:, half * HALF:(half + 1) * HALF],
                                 start=True, stop=True).then_inc(c_ready, 1)

            def sum_y(n, c):
                pe.wait_ge(hc_ready, n + 1)
                nc.tensor.matmul(ps[:, c, :], ident[:, :], hc[:, c, :], start=False, stop=False,
                                 skip_group_check=True).then_inc(hc_free, 1)

            def add_x(i):
                for k in range(DC):
                    nc.tensor.matmul(ps[:, out_bank(i), k * P:(k + 1) * P], xT[:, k, i * P:(i + 1) * P], ident[:, :],
                                     start=(k == 0), stop=False, skip_group_check=True)

            def out_part(i, c):
                mm = nc.tensor.matmul(ps[:, out_bank(i), 0:D], yT[:, c, i * P:(i + 1) * P], w_out[:, c, :],
                                      start=False, stop=(c == EC - 1), skip_group_check=True)
                if c == EC - 1:
                    mm.then_inc(o_ready, 1)

            def out_tile(i):
                if i == 0:
                    pe.wait_ge(ld_wo, 16)
                else:
                    pe.wait_ge(o_free, i)
                add_x(i)
                for c in range(EC):
                    out_part(i, c)

            def state(half, s, s2):
                known = isinstance(s, int)
                if not (known and s == NS - 1):
                    broadcast_c(half, s + 1, 1 - s2)
                elif half == 0:
                    broadcast_c(1, 0, 0)
                for c in range(EC):
                    if known and half == 1 and s == 0:
                        out_tile(c)
                    if c == 2:
                        if not (known and s >= NS - 2):
                            broadcast_b(half, s + 2, s + (half * NS + 2))
                        elif half == 0:
                            broadcast_b(1, s + 2 - NS, s + 2)
                    sum_y(s * EC + (half * PER_HALF + c), c)

            for half in range(2):
                start_y(half)
                if half == 0:
                    broadcast_b(0, 0, 0)
                    broadcast_c(0, 0, 0)
                    broadcast_b(0, 1, 1)
                state(half, 0, 0)
                state(half, 1, 1)
                with pe.Fori(1, NS // 2 - 1) as i:
                    state(half, i * 2, 0)
                    state(half, i * 2 + 1, 1)
                state(half, NS - 2, 0)
                state(half, NS - 1, 1)
            pe.wait_ge(o_free, TT // 2)
            for i in range(TT // 2, TT):
                add_x(i)
            for c in range(EC):
                pe.wait_ge(y_done, EC + c + 1)
                for i in range(TT // 2, TT):
                    out_part(i, c)

        @block.scalar
        def _(act):
            act.wait_ge(ld_chan, 16)
            nc.scalar.activation(negA[:], chan[:, :, NTAP + 3:], ACT.Exp).then_inc(a_exp, 1)
            nc.scalar.preload_act_table_set("silu_and_others")
            act.wait_ge(pads_ready, 1)

            def copy_xp(c):
                act.wait_ge(pair_ready, c + 1)
                nc.scalar.activation(xpad[:, c, :, NTAP - 1:], banks(ps, 2 * (c % 2), 2).rearrange(
                    "p (b t) -> p b t", b=BATCH), ACT.Copy).then_inc(pair_free, 1)

            def silu_xc(c):
                act.wait_ge(conv_step, NTAP * (c + 1))
                nc.scalar.activation(xc[:, c, :], conv[:, c, :], ACT.Silu).then_inc(xc_ready, 1)

            def take_z(c, item, func):
                act.wait_ge(pair_ready, item + 1)
                nc.scalar.activation(z[:, c, :], banks(ps, 2 * (item % 2), 2), func).then_inc(pair_free, 1)

            copy_xp(0)
            copy_xp(1)
            copy_xp(2)
            silu_xc(0)
            copy_xp(3)
            take_z(0, EC, ACT.Silu)
            for c in range(1, EC):
                silu_xc(c)
            nc.scalar.preload_act_table_set("natural_log_exp_and_others")
            act.wait_ge(dt_ready, 1)
            nc.scalar.activation(dt[:], banks(ps, 4, 2), ACT.Copy).then_inc(dt_sb_ready, 1)

            def take_v(c):
                act.wait_ge(pair_ready, DELTA0 + c + 1)
                nc.scalar.activation(conv[:, c, :], banks(ps, 2 * ((DELTA0 + c) % 2), 2), ACT.Identity,
                                     bias=b_dt[c]).then_inc(pair_free, 1)

            def exp_v(c):
                act.wait_ge(abs_ready, c + 1)
                nc.scalar.activation(spa[:, c % 2, :], spa[:, c % 2, :], ACT.Exp).then_inc(e_ready, 1)

            def log_u(c):
                act.wait_ge(u_ready, c + 1)
                if c >= 2:
                    act.wait_ge(delta_ready, c - 1)
                nc.scalar.activation(spl[:, c % 2, :], spu[:, c % 2, :], ACT.Ln).then_inc(l_ready, 1)

            take_v(0)
            take_v(1)
            exp_v(0)
            take_v(2)
            exp_v(1)
            log_u(0)
            take_v(3)
            exp_v(2)
            log_u(1)
            exp_v(3)
            log_u(2)
            take_z(1, Z1, ACT.Copy)
            log_u(3)
            take_z(2, Z1 + 1, ACT.Copy)
            take_z(3, Z1 + 2, ACT.Copy)

            def copy_b(s_done, s2):
                act.wait_ge(b_ready, s_done + 1)
                if not (isinstance(s_done, int) and s_done < 2):
                    act.wait_ge(dbx_ready, s_done * EC - EC)
                nc.scalar.activation(b_sb[:, s2, :], ps[:, 4, :], ACT.Copy).then_inc(b_sb_ready, 1)

            def state(half, s, s2):
                for c in range(EC):
                    act.wait_ge(scan_free, s * EC + (half * PER_HALF + c + 1))
                    nc.scalar.activation(
                        dA[:, c, :].rearrange("p (b t) -> p b t", b=2)[:, :, 1:],
                        delta[:, c, half * HALF:(half + 1) * HALF].rearrange("p (b t) -> p b t", b=2)[:, :, 1:],
                        ACT.Exp, scale=negA[:, c, bass.ds(s, 1)]).then_inc(dA_ready, 1)
                    if half == 1 and isinstance(s, int) and s == 1:
                        take_out(c)
                    if c == 1 and not (isinstance(s, int) and half == 1 and s == NS - 1):
                        copy_b(s + (half * NS + 1), 1 - s2)

            def take_out(i):
                act.wait_ge(o_ready, i + 1)
                nc.scalar.activation(x1[:, i, :], ps[:, out_bank(i), 0:D], ACT.Copy).then_inc(o_free, 1)

            act.wait_ge(delta_ready, EC)
            act.wait_ge(a_ready, 1)
            copy_b(0, 0)
            for half in range(2):
                state(half, 0, 0)
                if half == 0:
                    act.wait_ge(pair_free, 3 * EC)
                    nc.scalar.activation(z[:, 1:, :], z[:, 1:, :], ACT.Silu).then_inc(z_ready, 1)
                    nc.scalar.preload_act_table_set("exp_and_others")
                state(half, 1, 1)
                with act.Fori(1, NS // 2 - 1) as i:
                    state(half, i * 2, 0)
                    state(half, i * 2 + 1, 1)
                state(half, NS - 2, 0)
                state(half, NS - 1, 1)
            for i in range(TT // 2, TT):
                take_out(i)
            act.wait_ge(ag, TT)
            nc.scalar.activation(stats[:, :, 2], stats[:, :, 1], ACT.Sqrt, bias=keep["eps"][:, 0:1]).then_inc(sq, 1)

        @block.vector
        def _(dve):
            nc.vector.memset(dA[:].rearrange("p c (b t) -> p c b t", b=2)[:, :, :, 0:1], 0.0).then_inc(scan_free, EC)
            dve.wait_ge(a_exp, 1)
            nc.vector.tensor_scalar(negA[:], negA[:], -1.0, None, ALU.mult).then_inc(a_ready, 1)
            for c in range(EC):
                nc.vector.tensor_scalar(dp_diag[:, c, :], ident[:], d_p[c], None, ALU.mult).then_inc(dp_ready, 1)
            for c in range(EC):
                dve.wait_ge(pair_free, c + 1)
                out = conv[:, c, :].rearrange("p (b t) -> p b t", b=BATCH)
                nc.vector.tensor_scalar(out, xpad[:, c, :, NTAP - 1:], taps(c, NTAP - 1), conv_b[c],
                                        ALU.mult, ALU.add).then_inc(conv_step, 1)
                for k in range(NTAP - 1):
                    dve.wait_ge(conv_step, NTAP * c + k + 1)
                    nc.vector.scalar_tensor_tensor(out=out, in0=xpad[:, c, :, k:k + SEQ], scalar=taps(c, k), in1=out,
                                                   op0=ALU.mult, op1=ALU.add).then_inc(conv_step, 1)
            bc = banks(ps, 6, 2)
            dve.wait_ge(bc_ready, 1)
            nc.vector.tensor_copy(bcp[:], bc).then_inc(bc_step, 1)
            dve.wait_ge(bc_step, 1)
            nc.vector.tensor_tensor(bcr[64:P, :], bc[64:P, :], bcp[64:P, :], ALU.subtract).then_inc(bc_step, 1)
            dve.wait_ge(bc_step, 2)
            nc.vector.tensor_copy(bcp[64:P, :], bcr[64:P, :]).then_inc(bc_step, 1)
            dve.wait_ge(bc_step, 3)
            nc.vector.tensor_tensor(bcr[96:P, :], bcr[96:P, :], bcp[96:P, :], ALU.subtract).then_inc(bc_step, 1)
            dve.wait_ge(bc_step, 4)
            nc.vector.tensor_copy(bcp[96:P, :], bcr[96:P, :]).then_inc(bc_step, 1)
            def neg_abs(c):
                dve.wait_ge(pair_free, DELTA0 + c + 1)
                if c >= 2:
                    dve.wait_ge(t_ready, c - 1)
                nc.vector.scalar_tensor_tensor(out=spa[:, c % 2, :], in0=conv[:, c, :], scalar=-1.0,
                                               in1=conv[:, c, :], op0=ALU.mult, op1=ALU.min).then_inc(abs_ready, 1)

            def one_plus(c):
                s2 = c % 2
                dve.wait_ge(e_ready, c + 1)
                if c >= 2:
                    dve.wait_ge(t_ready, c - 1)
                    dve.wait_ge(l_ready, c - 1)
                nc.vector.tensor_scalar(spu[:, s2, :], spa[:, s2, :], 1.0, None, ALU.add).then_inc(u_ready, 1)
                dve.wait_ge(u_ready, c + 1)
                if c >= 2:
                    dve.wait_ge(lt_ready, c - 1)
                nc.vector.scalar_tensor_tensor(out=spt[:, s2, :], in0=spu[:, s2, :], scalar=-1.0, in1=spa[:, s2, :],
                                               op0=ALU.add, op1=ALU.subtract).then_inc(t_ready, 1)

            def sum_delta(c):
                dve.wait_ge(lt_ready, c + 1)
                nc.vector.scalar_tensor_tensor(out=delta[:, c, :], in0=conv[:, c, :], scalar=0.0, in1=spl[:, c % 2, :],
                                               op0=ALU.max, op1=ALU.add).then_inc(delta_ready, 1)

            neg_abs(0)
            neg_abs(1)
            for c in range(EC):
                one_plus(c)
                if c + 2 < EC:
                    neg_abs(c + 2)
                if c >= 1:
                    sum_delta(c - 1)
            sum_delta(EC - 1)

            def scan(n, c):
                dve.wait_ge(dA_ready, n + 1)
                dve.wait_ge(dbx_ready, n + 1)
                nc.vector.tensor_tensor_scan(h[:, c, :], dA[:, c, :], dbx[:, c, :], 0.0, ALU.mult,
                                             ALU.add).then_inc(scan_free, 1)

            def times_c(n, s_done, s2, c):
                if c == 0:
                    dve.wait_ge(c_ready, s_done + 1)
                dve.wait_ge(scan_free, EC + n + 1)
                dve.wait_ge(hc_free, n + 1)
                nc.vector.tensor_tensor(hc[:, c, :], h[:, c, :], ps[:, 5 + s2, :], ALU.mult).then_inc(hc_ready, 1)

            def finish_y(half, c):
                toks = slice(half * HALF, (half + 1) * HALF)
                if half == 0 and c == 0:
                    dve.wait_ge(z_ready, 1)
                dve.wait_ge(hc_free, EC + (half + 1) * PER_HALF - EC + c + 1)
                nc.vector.tensor_tensor(yT[:, c, toks], z[:, c, toks], ps[:, c, :], ALU.mult).then_inc(y_done, 1)

            for half in range(2):
                n0, s0 = half * PER_HALF, half * NS
                for s in (0, 1):
                    for c in range(EC):
                        scan(n0 + s * EC + c, c)
                        if half == 1 and s == 0:
                            finish_y(0, c)
                        if c >= 1:
                            times_c(n0 + s * EC + c - 1, s0 + s, s, c - 1)
                    times_c(n0 + s * EC + EC - 1, s0 + s, s, EC - 1)
                with dve.Fori(1, NS // 2) as i:
                    for s2 in range(2):
                        n = i * (2 * EC) + (n0 + s2 * EC)
                        for c in range(EC):
                            scan(n + c, c)
                            if c >= 1:
                                times_c(n + (c - 1), i * 2 + (s0 + s2), s2, c - 1)
                        times_c(n + (EC - 1), i * 2 + (s0 + s2), s2, EC - 1)
            for c in range(EC):
                finish_y(1, c)
            layernorm(nc, dve, x1, x1, keep, lambda i: dve.wait_ge(o_free, i + 1), st, ag, sq, rc, nw, ln)


def layernorm(nc, dve, src, dst, keep, ready, st, ag, sq, rc, nw, ln, parts=1):
    bn, stats, run = keep["bn"], keep["stats"], TT // parts
    for part in range(parts):
        tiles = range(part * run, (part + 1) * run)
        for i in tiles:
            ready(i)
            nc.vector.bn_stats(bn[:, i, :], src[:, i, :]).then_inc(st, 1)
            if i > tiles[0]:
                dve.wait_ge(st, i)
                nc.vector.bn_aggr(stats[:, i - 1, 0:2], bn[:, i - 1, :]).then_inc(ag, 1)
        dve.wait_ge(st, tiles[-1] + 1)
        nc.vector.bn_aggr(stats[:, tiles[-1], 0:2], bn[:, tiles[-1], :]).then_inc(ag, 1)
        dve.wait_ge(sq, part + 1)
        inverse_root(nc, dve, stats[:, tiles[0]:tiles[-1] + 1, :], 1, LN_EPS, 1.0, rc, nw, part)
        for i in tiles:
            nc.vector.tensor_scalar(dst[:, i, :], src[:, i, :], stats[:, i, 0:1], stats[:, i, 3:4],
                                    ALU.subtract, ALU.mult).then_inc(ln, 1)


def inverse_root(nc, dve, stats, col, eps, scale, rc, nw, before=0):
    r0, n0 = 2 * before, 4 * before
    v, r, t, w = stats[:, :, col], stats[:, :, 3], stats[:, :, 4], stats[:, :, 5]
    nc.vector.tensor_scalar(w, v, scale, eps, ALU.mult, ALU.add).then_inc(nw, 1)
    nc.vector.reciprocal(r, stats[:, :, 2]).then_inc(rc, 1)
    dve.wait_ge(rc, r0 + 1)
    dve.wait_ge(nw, n0 + 1)
    nc.vector.tensor_tensor(t, r, r, ALU.mult).then_inc(nw, 1)
    dve.wait_ge(nw, n0 + 2)
    nc.vector.tensor_tensor(t, t, w, ALU.mult).then_inc(rc, 1)
    dve.wait_ge(rc, r0 + 2)
    nc.vector.tensor_scalar(t, t, -0.5, 1.5, ALU.mult, ALU.add).then_inc(nw, 1)
    dve.wait_ge(nw, n0 + 3)
    nc.vector.tensor_tensor(r, r, t, ALU.mult).then_inc(nw, 1)
    dve.wait_ge(nw, n0 + 4)


def three_passes(nc, out, lhs, rhs, start, stop):
    (lh, ll), (rh, rl) = lhs, rhs
    nc.tensor.matmul(out, lh, rh, start=start, stop=False, skip_group_check=True)
    nc.tensor.matmul(out, lh, rl, start=False, stop=False, skip_group_check=True)
    return nc.tensor.matmul(out, ll, rh, start=False, stop=stop, skip_group_check=True)


def squares(nc, act, keep, src, junk, wait, sq_done, root):
    stats = keep["stats"]
    for i in range(TT):
        wait(i)
        nc.scalar.activation(junk(i), src(i), ACT.Square, accum_out=stats[:, i, 0:1]).then_inc(sq_done, 1)
    act.wait_ge(sq_done, TT)
    nc.scalar.activation(stats[:, :, 2], stats[:, :, 0], ACT.Sqrt, scale=1.0 / D,
                         bias=keep["eps"][:, 1:2]).then_inc(root, 1)


def rms_plan(nc, ctx, keep, ps, src, ln_w, name, first_bank, squared=False):
    def sem(n):
        return ctx.enter_context(nc.semaphore(f"{name}_{n}"))

    stats = keep["stats"]
    xr = ctx.enter_context(nc.sbuf_tensor(f"{name}_xr", [P, TT, D], F32))
    hi = ctx.enter_context(nc.sbuf_tensor(f"{name}_hi", [P, DC, T], F32R))
    lo = ctx.enter_context(nc.sbuf_tensor(f"{name}_lo", [P, DC, T], F32R))
    sq_done, root, rc, nw = sem("squares"), sem("root"), sem("rec"), sem("newton")
    scaled, turned, hi_done, lo_done = sem("scaled"), sem("turned"), sem("hi"), sem("lo")
    per_bank = 512 // P

    def bank(u):
        return ps[:, first_bank + u % 4, :]

    def scalar(act):
        if not squared:
            squares(nc, act, keep, lambda i: src[:, i, :], lambda i: xr[:, i, :], lambda i: None, sq_done, root)
        splits(act)

    def splits(act):
        for u in range(2 * DC):
            act.wait_ge(turned, u + 1)
            nc.scalar.activation(hi[:, u // 2, (u % 2) * HALF:(u % 2 + 1) * HALF], bank(u), ACT.Copy,
                                 scale=ln_w[:, u // 2:u // 2 + 1]).then_inc(hi_done, 1)

    def vector(dve):
        if not squared:
            dve.wait_ge(root, 1)
        inverse_root(nc, dve, stats, 0, RMS_EPS, 1.0 / D, rc, nw)
        for i in range(TT):
            nc.vector.tensor_scalar(xr[:, i, :], src[:, i, :], stats[:, i, 3:4], None, ALU.mult).then_inc(scaled, 1)
        for u in range(2 * DC):
            toks = slice((u % 2) * HALF, (u % 2 + 1) * HALF)
            dve.wait_ge(hi_done, u + 1)
            nc.vector.scalar_tensor_tensor(out=lo[:, u // 2, toks], in0=bank(u), scalar=ln_w[:, u // 2:u // 2 + 1],
                                           in1=hi[:, u // 2, toks].bitcast(F32), op0=ALU.mult,
                                           op1=ALU.subtract).then_inc(lo_done, 1)

    def tensor(pe):
        for u in range(2 * DC):
            for k in range(per_bank):
                i = (u % 2) * per_bank + k
                pe.wait_ge(scaled, i + 1)
                mm = nc.tensor.transpose(bank(u)[:, k * P:(k + 1) * P], xr[:, i, (u // 2) * P:(u // 2 + 1) * P],
                                         keep["ident"][:])
            mm.then_inc(turned, 1)

    return scalar, vector, tensor, (hi, lo), lo_done


def shared_buffers(nc, ctx, keep):
    keep["raw"] = ctx.enter_context(nc.sbuf_tensor("raw", [P, GM, PACK], F32))
    keep["own"] = ctx.enter_context(nc.sbuf_tensor("own", [P, NM_R, P], BF16))
    keep["ln2"] = ctx.enter_context(nc.sbuf_tensor("ln2", [P, DC], F32))
    keep["gate"] = ctx.enter_context(nc.sbuf_tensor("gate", [P, DC, NE], F32))
    keep["ld_expert"] = [ctx.enter_context(nc.semaphore(f"ld_expert{j}")) for j in range(GM)]
    keep["ld_small"] = ctx.enter_context(nc.semaphore("ld_small"))


def attention_block(nc, ctx, d, keep, ps):
    def sb(name, shape, dt=F32):
        return ctx.enter_context(nc.sbuf_tensor(name, shape, dt))

    def sem(name):
        return ctx.enter_context(nc.semaphore(f"a_{name}"))

    def split(name, shape):
        return sb(f"a_{name}h", shape, F32R), sb(f"a_{name}l", shape, F32R)

    x1, hid, ident, identb, mask = (keep[k] for k in ("x1", "hid", "ident", "identb", "mask"))
    lnw = sb("a_lnw", [P, DC])
    raw, own = keep["raw"], keep["own"]
    w = split("w", [P, GH, PACK])
    q, k_ = split("q", [P, 2, T]), split("k", [P, 2, T])
    v = split("v", [P, 2, TT, 2 * HD])
    p = sb("a_p", [P, BATCH, 3 * P])
    pT = split("pT", [P, 2, 3 * P])
    o = split("o", [P, GH, T])
    nmax, sums, rs = (sb(f"a_{n}", [P, 4, 2]) for n in ("nmax", "sums", "rs"))

    ld_ln = sem("ld_ln")
    ld_w = [sem(f"ld_w{j}") for j in range(GH)]
    wh_done, w_done = sem("wh_done"), sem("w_done")
    hid_ready = sem("hid_ready")
    own_ones, own_done = sem("own_ones"), sem("own_done")
    sq_done, root = sem("sq_done"), sem("root")
    r_ready, rh_done, r_free = sem("r_ready"), sem("rh_done"), sem("r_free")
    s_ready, max_done, exp_done = sem("s_ready"), sem("max_done"), sem("exp_done")
    rs_done, norm_done = sem("rs_done"), sem("norm_done")
    pT_ready, ph_done, pl_done = sem("pT_ready"), sem("ph_done"), sem("pl_done")
    o_ready, oh_done, ol_done = sem("o_ready"), sem("oh_done"), sem("ol_done")

    rms_scalar, rms_vector, rms_tensor, xn, xn_done = rms_plan(nc, ctx, keep, ps, x1, lnw, "a_rms", 2)

    FIRST = 8
    PER_GROUP = 6 * GH + TT

    def unit(g, j, u):
        return g * PER_GROUP + (FIRST + 6 * j + u)

    def units_of(g, j):
        last = isinstance(g, int) and g == NG - 1
        return range(0) if last and j == GH - 1 else range(4) if last and j == GH - 2 else range(6)

    def out_unit(g, i):
        return unit(g, 0, i + 6 * GH - (8 if isinstance(g, int) and g == NG - 1 else 0))

    def ring(u):
        return ps[:, u % 2, :]

    def target(j_next, pair_next, tile0, u, part):
        if u < 4:
            return (q, k_)[u // 2][part][:, j_next % 2, (u % 2) * HALF:(u % 2 + 1) * HALF]
        first = tile0 + 2 * (u - 4)
        return v[part][:, pair_next % 2, first:first + 2, :].rearrange("p t d -> p (t d)")

    def step_target(j, u, part):
        return target(j + 1, j // 2 + 1, 4 * (j % 2), u, part)

    def first_target(u, part):
        return target(0, 0, 0, u, part)

    with nc.Block() as block:
        @block.sync
        def _(sp):
            sp.dma_start(lnw[:], d["ln1"]).then_inc(ld_ln, 16)
            for j in range(GH):
                sp.dma_start(raw[:, j, :], d["attn_w"][j]).then_inc(ld_w[j], 16)
            with sp.Fori(1, NG + 1) as g:
                for j in range(GH):
                    sp.wait_ge(w_done, g * GH + (j + 1 - GH))
                    sp.dma_start(raw[:, j, :], d["attn_w"][bass.ds(g * GH + j, 1)].rearrange("a p n -> (a p) n")
                                 ).then_inc(ld_w[j], 16)
            sp.dma_start(keep["ln2"][:], d["ln2"]).then_inc(keep["ld_small"], 16)
            sp.dma_start(keep["gate"][:], d["gate"]).then_inc(keep["ld_small"], 16)
            for j in range(GM):
                if j < GH:
                    sp.wait_ge(w_done, NG * GH + j + 1)
                sp.dma_start(raw[:, j, 0:FPACK], d["expert_w"][j]).then_inc(keep["ld_expert"][j], 16)

        @block.gpsimd
        def _(pool):
            nc.gpsimd.tensor_copy(hid[:], x1[:]).then_inc(hid_ready, 1)

            def pack(k, j):
                pool.wait_ge(wh_done, k + 1)
                nc.gpsimd.tensor_tensor(w[1][:, j, :], raw[:, j, :], w[0][:, j, :].bitcast(F32),
                                        ALU.subtract).then_inc(w_done, 1)

            for j in range(GH):
                pack(j, j)
            nc.gpsimd.memset(own[:], 1.0).then_inc(own_ones, 1)
            pool.wait_ge(own_ones, 1)
            for part in range(3):
                rows = own[NW * part:NW * (part + 1), :, :]
                for sign, base in ((1, 0), (-1, EI - 1)):
                    nc.gpsimd.affine_select(out=rows, in_=rows, compare_op=ALU.is_ge, fill=0.0, base=base,
                                            pattern=[[sign * P, NM_R], [sign, P]], channel_multiplier=-sign * EI
                                            ).then_inc(own_done, 1)
                    pool.wait_ge(own_done, 2 * part + (1 if sign > 0 else 2))
            with pool.Fori(1, NG + 1) as g:
                for j in range(GH):
                    pack(g * GH + j, j)

        @block.tensor
        def _(pe):
            rms_tensor(pe)
            pe.wait_ge(xn_done, 2 * DC)

            def project(n, u, j_next, pair_next, tile0):
                if not (isinstance(n, int) and n < 2):
                    pe.wait_ge(r_free, n - 1)
                bank = ring(u)
                if u < 4:
                    for c in range(DC):
                        at = ((u // 2) * DC + c) * HD
                        toks = slice((u % 2) * HALF, (u % 2 + 1) * HALF)
                        mm = three_passes(nc, bank, [x[:, j_next % GH, at:at + HD] for x in w],
                                          [x[:, c, toks] for x in xn], c == 0, c == DC - 1)
                else:
                    for half in range(2):
                        i = tile0 + 2 * (u - 4) + half
                        for c in range(DC):
                            j = 2 * (pair_next % 2) + c
                            mm = three_passes(nc, bank[:, half * 2 * HD:(half + 1) * 2 * HD],
                                              [x[:, c, i * P:(i + 1) * P] for x in xn],
                                              [x[:, j, 512:768] for x in w], c == 0, c == DC - 1)
                mm.then_inc(r_ready, 1)

            def scores(n, j, b):
                if not (isinstance(n, int) and n < 2):
                    pe.wait_ge(exp_done, n - 1)
                bank, t0 = ps[:, 2 + b % 2, :], b * SEQ
                for first, keys, cols in ((t0, P, slice(0, P)), (t0 + P, SEQ, slice(P, 3 * P))):
                    three_passes(nc, bank[:, cols], [x[:, j % 2, first:first + P] for x in q],
                                 [x[:, j % 2, t0:t0 + keys] for x in k_], True, False)
                    diag = bank[:, cols.stop - P:cols.stop]
                    mm = nc.tensor.matmul(diag, identb[:], mask[:], start=False, stop=True, skip_group_check=True)
                mm.then_inc(s_ready, 1)

            def turn(n, b):
                pe.wait_ge(norm_done, n + 1)
                if not (isinstance(n, int) and n < 2):
                    pe.wait_ge(pl_done, n - 1)
                for blk in range(3):
                    mm = nc.tensor.transpose(ps[:, 4 + b % 2, blk * P:(blk + 1) * P], p[:, b, blk * P:(blk + 1) * P],
                                             ident[:])
                mm.then_inc(pT_ready, 1)

            def weigh(n, j, b):
                pe.wait_ge(pl_done, n + 1)
                if not (isinstance(n, int) and n < 2):
                    pe.wait_ge(ol_done, n - 1)
                bank, cols = ps[:, 6 + b % 2, :], slice((j % 2) * HD, (j % 2 + 1) * HD)
                vs = [[x[:, j // 2, 2 * b + kt, cols] for x in v] for kt in range(2)]
                three_passes(nc, bank[:, 0:SEQ], vs[0], [x[:, b % 2, 0:2 * P] for x in pT], True, False)
                three_passes(nc, bank[:, P:SEQ], vs[1], [x[:, b % 2, 2 * P:3 * P] for x in pT], False,
                             True).then_inc(o_ready, 1)

            def outputs(g):
                pe.wait_ge(ol_done, g * (GH * BATCH) + GH * BATCH)
                pe.wait_ge(w_done, g * GH + 2 * GH)
                for i in range(TT):
                    pe.wait_ge(r_free, out_unit(g, i) - 1)
                    for j in range(GH):
                        mm = three_passes(nc, ring(i)[:, 0:D], [x[:, j, i * P:(i + 1) * P] for x in o],
                                          [x[:, j, 768:1024] for x in w], j == 0, j == GH - 1)
                    mm.then_inc(r_ready, 1)

            pe.wait_ge(w_done, 1)
            for u in range(4):
                project(u, u, 0, 0, 0)
            pe.wait_ge(w_done, 2)
            for u in range(4, FIRST):
                project(u, u, 0, 0, 0)
                if u >= FIRST - 2:
                    pe.wait_ge(r_free, 4)
                    scores(u - (FIRST - 2), 0, u - (FIRST - 2))

            def step(g, j):
                n = g * (GH * BATCH) + j * BATCH
                units = units_of(g, j)

                def fill(u):
                    if u in units:
                        if u == 0:
                            pe.wait_ge(w_done, g * GH + (j + 2))
                        if u == 4:
                            pe.wait_ge(w_done, g * GH + (2 * (j // 2) + 4))
                        project(unit(g, j, u), u, j + 1, j // 2 + 1, 4 * (j % 2))

                ahead = len(units) > 0
                fill(0)
                scores(n + 2, j, 2)
                turn(n, 0)
                fill(1)
                weigh(n, j, 0)
                scores(n + 3, j, 3)
                turn(n + 1, 1)
                fill(2)
                weigh(n + 1, j, 1)
                turn(n + 2, 2)
                fill(3)
                weigh(n + 2, j, 2)
                turn(n + 3, 3)
                fill(4)
                if ahead:
                    pe.wait_ge(r_free, unit(g, j, 3) + 1)
                    scores(n + BATCH, j + 1, 0)
                weigh(n + 3, j, 3)
                if ahead:
                    scores(n + (BATCH + 1), j + 1, 1)
                fill(5)

            for j in range(GH):
                step(0, j)
            outputs(0)
            with pe.Fori(1, NG - 1) as g:
                for j in range(GH):
                    step(g, j)
                outputs(g)
            for j in range(GH):
                step(NG - 1, j)
            outputs(NG - 1)

        @block.scalar
        def _(act):
            act.wait_ge(ld_ln, 16)
            rms_scalar(act)

            def pack(j, loads):
                act.wait_ge(ld_w[j], loads)
                nc.scalar.activation(w[0][:, j, :], raw[:, j, :], ACT.Copy).then_inc(wh_done, 1)

            def high(n, u, out):
                act.wait_ge(r_ready, n + 1)
                nc.scalar.activation(out, ring(u), ACT.Copy, scale=QSCALE if u < 2 else 1.0).then_inc(rh_done, 1)

            def exps(n, b):
                act.wait_ge(max_done, n + 1)
                if not (isinstance(n, int) and n < BATCH):
                    act.wait_ge(pT_ready, n + (1 - BATCH))
                for t, cols in ((0, slice(0, P)), (1, slice(P, 3 * P))):
                    e = nc.scalar.activation(p[:, b, cols], ps[:, 2 + b % 2, cols], ACT.Exp,
                                             bias=nmax[:, b, t:t + 1], accum_out=sums[:, b, t:t + 1])
                e.then_inc(exp_done, 1)

            def high_p(n, b):
                act.wait_ge(pT_ready, n + 1)
                if not (isinstance(n, int) and n < 2):
                    act.wait_ge(o_ready, n - 1)
                nc.scalar.activation(pT[0][:, b % 2, :], ps[:, 4 + b % 2, 0:3 * P], ACT.Copy).then_inc(ph_done, 1)

            def high_o(n, j, b):
                act.wait_ge(o_ready, n + 1)
                nc.scalar.activation(o[0][:, j, b * SEQ:(b + 1) * SEQ], ps[:, 6 + b % 2, 0:SEQ],
                                     ACT.Copy).then_inc(oh_done, 1)

            for j in range(GH):
                pack(j, 16)
            for u in range(FIRST):
                high(u, u, first_target(u, 0))
                if u >= FIRST - 2:
                    exps(u - (FIRST - 2), u - (FIRST - 2))

            def step(g, j):
                n = g * (GH * BATCH) + j * BATCH
                units = units_of(g, j)

                def fill(u):
                    if u in units:
                        high(unit(g, j, u), u, step_target(j, u, 0))

                ahead = len(units) > 0
                fill(0)
                high_p(n, 0)
                exps(n + 2, 2)
                fill(1)
                high_o(n, j, 0)
                high_p(n + 1, 1)
                exps(n + 3, 3)
                fill(2)
                high_o(n + 1, j, 1)
                high_p(n + 2, 2)
                pack(j, g * 16 + 32)
                fill(3)
                high_o(n + 2, j, 2)
                high_p(n + 3, 3)
                fill(4)
                if ahead:
                    exps(n + BATCH, 0)
                high_o(n + 3, j, 3)
                if ahead:
                    exps(n + (BATCH + 1), 1)
                fill(5)

            for j in range(GH):
                step(0, j)
            with act.Fori(1, NG - 1) as g:
                for j in range(GH):
                    step(g, j)
            for j in range(GH):
                step(NG - 1, j)
            squares(nc, act, keep, lambda i: hid[:, i, :], lambda i: v[0][:, 0, i, :],
                    lambda i: act.wait_ge(r_free, out_unit(NG - 1, i) + 1), sq_done, root)

        @block.vector
        def _(dve):
            rms_vector(dve)

            def low(n, u, out, high):
                dve.wait_ge(rh_done, n + 1)
                bank = ring(u)
                if u < 2:
                    mm = nc.vector.scalar_tensor_tensor(out=out, in0=bank, scalar=QSCALE, in1=high.bitcast(F32),
                                                        op0=ALU.mult, op1=ALU.subtract)
                else:
                    mm = nc.vector.tensor_tensor(out, bank, high.bitcast(F32), ALU.subtract)
                mm.then_inc(r_free, 1)

            def maxes(n, b):
                dve.wait_ge(s_ready, n + 1)
                for t, cols in ((0, slice(0, P)), (1, slice(P, 3 * P))):
                    m = nc.vector.tensor_reduce(nmax[:, b, t:t + 1], ps[:, 2 + b % 2, cols], AX.X, ALU.max, negate=True)
                m.then_inc(max_done, 1)

            def normalize(n, b):
                dve.wait_ge(exp_done, n + 1)
                nc.vector.reciprocal(rs[:, b, :], sums[:, b, :]).then_inc(rs_done, 1)
                dve.wait_ge(rs_done, n + 1)
                for t, cols in ((0, slice(0, P)), (1, slice(P, 3 * P))):
                    m = nc.vector.tensor_scalar(p[:, b, cols], p[:, b, cols], rs[:, b, t:t + 1], None, ALU.mult)
                m.then_inc(norm_done, 1)

            def low_p(n, b):
                dve.wait_ge(ph_done, n + 1)
                nc.vector.tensor_tensor(pT[1][:, b % 2, :], ps[:, 4 + b % 2, 0:3 * P], pT[0][:, b % 2, :].bitcast(F32),
                                        ALU.subtract).then_inc(pl_done, 1)

            def low_o(n, j, b):
                toks = slice(b * SEQ, (b + 1) * SEQ)
                dve.wait_ge(oh_done, n + 1)
                nc.vector.tensor_tensor(o[1][:, j, toks], ps[:, 6 + b % 2, 0:SEQ], o[0][:, j, toks].bitcast(F32),
                                        ALU.subtract).then_inc(ol_done, 1)

            def add_output(g):
                for i in range(TT):
                    dve.wait_ge(r_ready, out_unit(g, i) + 1)
                    nc.vector.tensor_tensor(hid[:, i, :], hid[:, i, :], ring(i)[:, 0:D], ALU.add).then_inc(r_free, 1)

            for u in range(FIRST):
                low(u, u, first_target(u, 1), first_target(u, 0))
                if u >= FIRST - 2:
                    maxes(u - (FIRST - 2), u - (FIRST - 2))
            normalize(0, 0)
            dve.wait_ge(hid_ready, 1)

            def step(g, j):
                n = g * (GH * BATCH) + j * BATCH
                units = units_of(g, j)

                def fill(u):
                    if u in units:
                        low(g * (6 * GH) + (FIRST + 6 * j + u), u, step_target(j, u, 1), step_target(j, u, 0))

                ahead = len(units) > 0
                maxes(n + 2, 2)
                fill(0)
                low_p(n, 0)
                normalize(n + 1, 1)
                fill(1)
                low_o(n, j, 0)
                maxes(n + 3, 3)
                low_p(n + 1, 1)
                normalize(n + 2, 2)
                fill(2)
                low_o(n + 1, j, 1)
                low_p(n + 2, 2)
                normalize(n + 3, 3)
                fill(3)
                low_o(n + 2, j, 2)
                low_p(n + 3, 3)
                fill(4)
                if ahead:
                    maxes(n + BATCH, 0)
                    maxes(n + (BATCH + 1), 1)
                low_o(n + 3, j, 3)
                if ahead:
                    normalize(n + BATCH, 0)
                fill(5)

            for j in range(GH):
                step(0, j)
            add_output(0)
            with dve.Fori(1, NG - 1) as g:
                for j in range(GH):
                    step(g, j)
                add_output(g)
            for j in range(GH):
                step(NG - 1, j)
            add_output(NG - 1)


def expert_block(nc, ctx, d, keep, ps, out):
    def sb(name, shape, dt=F32):
        return ctx.enter_context(nc.sbuf_tensor(name, shape, dt))

    def sem(name):
        return ctx.enter_context(nc.semaphore(f"e_{name}"))

    def split(name, shape):
        return sb(f"e_{name}h", shape, F32R), sb(f"e_{name}l", shape, F32R)

    x1, hid, ident, identb, raw, own, gate_raw = (keep[k] for k in ("x1", "hid", "ident", "identb", "raw", "own", "gate"))
    ld_w = keep["ld_expert"]
    gate = split("gate", [P, DC, NE])
    w = split("w", [P, GM, FPACK])
    lgT = sb("e_lgT", [NE, T])
    lg, ex, gt, eq, cum = (sb(f"e_{n}", [P, TT, NE]) for n in ("lg", "ex", "gt", "eq", "cum"))
    top = sb("e_top", [P, TT, 8])
    cnt, tot = sb("e_cnt", [P, TT, 1]), sb("e_tot", [P, TT, 1])
    wf = sb("e_wf", [P, TT, NE])
    wr = sb("e_wr", [P, TT, NE])
    wp = sb("e_wp", [P, TT, P], BF16)
    wT = sb("e_wT", [P, T], BF16)
    sg = sb("e_sg", [P, 2, HALF])
    aw = sb("e_aw", [P, 2, HALF])
    a = split("a", [P, GM, T])

    rms_scalar, rms_vector, rms_tensor, xn, xn_done = rms_plan(nc, ctx, keep, ps, hid, keep["ln2"], "e_rms", 0,
                                                               squared=True)

    wh_done, w_done = sem("wh_done"), sem("w_done")
    dh_done, d_done = sem("dh_done"), sem("d_done")
    gh_done, gl_done = sem("gh_done"), sem("gl_done")
    lgT_ready, lgT_done = sem("lgT_ready"), sem("lgT_done")
    lg_ready, rt, ex_done = sem("lg_ready"), sem("rt"), sem("ex_done")
    wp_clear, wp_done, wT_ready, wT_done = sem("wp_clear"), sem("wp_done"), sem("wT_ready"), sem("wT_done")
    g_ready, u_ready = sem("g_ready"), sem("u_ready")
    sg_done, up_done, aw_done = sem("sg_done"), sem("up_done"), sem("aw_done")
    ah_done, al_done = sem("ah_done"), sem("al_done")
    dn_ready, dn_free = sem("dn_ready"), sem("dn_free")
    x_added = sem("x_added")
    st, ag, sq, rc, nw, ln, stored = (sem(n) for n in ("stat", "aggr", "sqrt", "rec", "newton", "ln", "stored"))

    N_SH = 2 * SH_TILES
    LN_PARTS = 2

    with nc.Block() as block:
        @block.sync
        def _(sp):
            with sp.Fori(1, NMG + 1) as g:
                for j in range(GM):
                    sp.wait_ge(w_done, g * GM + (j + 1 - GM))
                    sp.dma_start(raw[:, j, 0:FPACK], d["expert_w"][bass.ds(g * GM + j, 1)].rearrange(
                        "a p n -> (a p) n")).then_inc(ld_w[j], 16)
            for i in range(TT):
                sp.wait_ge(ln, i + 1)
                sp.dma_start(out[:, i, :], hid[:, i, :]).then_inc(stored, 16)
            sp.wait_ge(stored, 16 * TT)

        @block.gpsimd
        def _(pool):
            pool.wait_ge(gh_done, 1)
            nc.gpsimd.tensor_tensor(gate[1][:], gate_raw[:], gate[0][:].bitcast(F32), ALU.subtract).then_inc(gl_done, 1)

            def rest(j, k, cols, high, low):
                pool.wait_ge(high, j + 1)
                nc.gpsimd.tensor_tensor(w[1][:, k, cols], raw[:, k, cols], w[0][:, k, cols].bitcast(F32),
                                        ALU.subtract).then_inc(low, 1)

            for k in range(GM):
                rest(k, k, slice(0, 2 * D), wh_done, w_done)
                if k == 0:
                    nc.gpsimd.memset(wp[:], 0.0).then_inc(wp_clear, 1)
            pool.wait_ge(xn_done, 2 * DC)
            nc.gpsimd.tensor_tensor(hid[:], hid[:], x1[:], ALU.add).then_inc(x_added, 1)
            with pool.Fori(0, NMG) as g:
                for k in range(GM):
                    rest(g * GM + k, k, slice(2 * D, 3 * D), dh_done, d_done)
                    rest(g * GM + (k + GM), k, slice(0, 2 * D), wh_done, w_done)

        @block.tensor
        def _(pe):
            rms_tensor(pe)
            pe.wait_ge(gl_done, 1)
            for c in range(DC):
                for th in range(2):
                    pe.wait_ge(xn_done, 2 * c + th + 1)
                    mm = three_passes(nc, ps[0:NE, 4 + th, :], [x[:, c, :] for x in gate],
                                      [x[:, c, th * HALF:(th + 1) * HALF] for x in xn], c == 0, c == DC - 1)
            mm.then_inc(lgT_ready, 1)

            def gate_up(g, k, th):
                n = g * (2 * GM) + (2 * k + th)
                toks = slice(th * HALF, (th + 1) * HALF)
                known = isinstance(n, int)
                shared = known and n < N_SH
                if th == 0:
                    pe.wait_ge(w_done, g * GM + (k + 1))
                for o, ready in enumerate((g_ready, u_ready)):
                    if not (known and n < 2):
                        if o == 0:
                            pe.wait_ge(sg_done, n - 1)
                        elif known and n - 2 < N_SH:
                            pe.wait_ge(aw_done, n - 1)
                        else:
                            pe.wait_ge(up_done, n - (1 + N_SH))
                    for c in range(DC):
                        at = o * D + c * P
                        mm = three_passes(nc, ps[:, 2 * o + th, :], [x[:, k, at:at + P] for x in w],
                                          [x[:, c, toks] for x in xn], c == 0, c == DC - 1)
                    if o == 0 or shared:
                        mm.then_inc(ready, 1)
                if not shared:
                    if known and n == N_SH:
                        pe.wait_ge(wT_done, 1)
                    pe.wait_ge(aw_done, n - 1)
                    rows = own[:, bass.ds(g * GM + (k - SH_TILES), 1), :].rearrange("p a n -> p (a n)")
                    nc.tensor.matmul(ps[:, 4 + th, :], rows, wT[:, toks], start=True, stop=True).then_inc(u_ready, 1)

            def turn_logits():
                pe.wait_ge(lgT_done, 2)
                for i in range(TT):
                    mm = nc.tensor.transpose(ps[:, 6, i * NE:(i + 1) * NE], lgT[:, i * P:(i + 1) * P],
                                             ident[0:NE, 0:NE])
                mm.then_inc(lg_ready, 1)

            def turn_weights():
                pe.wait_ge(wp_done, 1)
                turned = ps[:, 6, :].bitcast(BF16)
                for i in range(TT):
                    mm = nc.tensor.transpose(turned[:, i * P:(i + 1) * P], wp[:, i, :], identb[:])
                mm.then_inc(wT_ready, 1)

            def down(g, i):
                n = g * TT + i
                if not (isinstance(g, int) and g == 0 and i < 2):
                    pe.wait_ge(dn_free, n - 1)
                for k in range(GM):
                    if i in (0, TT // 2):
                        pe.wait_ge(al_done, g * (2 * GM) + (2 * k + (i > 0) + 1))
                    mm = three_passes(nc, ps[:, 6 + i % 2, 0:D], [x[:, k, i * P:(i + 1) * P] for x in a],
                                      [x[:, k, 2 * D:3 * D] for x in w], k == 0, k == GM - 1)
                mm.then_inc(dn_ready, 1)

            def group(g):
                for k in range(GM):
                    first = isinstance(g, int) and g == 0
                    gate_up(g, k, 0)
                    if first and k == 0:
                        turn_logits()
                    gate_up(g, k, 1)
                    if first and k == SH_TILES - 1:
                        turn_weights()
                pe.wait_ge(d_done, g * GM + GM)
                for i in range(TT):
                    down(g, i)

            group(0)
            with pe.Fori(1, NMG) as g:
                group(g)

        @block.scalar
        def _(act):
            act.wait_ge(keep["ld_small"], 32)
            nc.scalar.activation(gate[0][:], gate_raw[:], ACT.Copy).then_inc(gh_done, 1)

            def high_w(k, loads):
                act.wait_ge(ld_w[k], loads)
                nc.scalar.activation(w[0][:, k, 0:2 * D], raw[:, k, 0:2 * D], ACT.Copy).then_inc(wh_done, 1)

            def high_d(g, k):
                act.wait_ge(ld_w[k], g * 16 + 32)
                if k == 0 and not (isinstance(g, int) and g == 0):
                    act.wait_ge(dn_ready, g * TT)
                nc.scalar.activation(w[0][:, k, 2 * D:3 * D], raw[:, k, 2 * D:3 * D], ACT.Copy).then_inc(dh_done, 1)

            high_w(0, 16)
            rms_scalar(act)
            for k in range(1, GM):
                high_w(k, 16)
            act.wait_ge(rt, 2)
            nc.scalar.activation(ex[:], ex[:], ACT.Exp).then_inc(ex_done, 1)

            def silu(n, th):
                act.wait_ge(g_ready, n + 1)
                if not (isinstance(n, int) and n < 2):
                    act.wait_ge(aw_done, n - 1)
                nc.scalar.activation(sg[:, th, :], ps[:, th, :], ACT.Silu).then_inc(sg_done, 1)

            def high(n, k, th):
                act.wait_ge(aw_done, n + 1)
                nc.scalar.activation(a[0][:, k, th * HALF:(th + 1) * HALF], aw[:, th, :], ACT.Copy).then_inc(ah_done, 1)

            def group(g):
                for k in range(GM):
                    n = g * (2 * GM) + 2 * k
                    silu(n, 0)
                    if k == GM - 1:
                        high(n, k, 0)
                    silu(n + 1, 1)
                    high_d(g, k)
                    if k < GM - 1:
                        high(n, k, 0)
                    high(n + 1, k, 1)
                    high_w(k, g * 16 + 32)

            group(0)
            with act.Fori(1, NMG) as g:
                group(g)
            for part in range(LN_PARTS):
                tiles = slice(part * TT // LN_PARTS, (part + 1) * TT // LN_PARTS)
                act.wait_ge(ag, tiles.stop)
                nc.scalar.activation(keep["stats"][:, tiles, 2], keep["stats"][:, tiles, 1], ACT.Sqrt,
                                     bias=keep["eps"][:, 0:1]).then_inc(sq, 1)

        @block.vector
        def _(dve):
            rms_vector(dve)
            step = [0]

            def chain(ins):
                step[0] += 1
                ins.then_inc(rt, 1)
                dve.wait_ge(rt, step[0])

            for th in range(2):
                dve.wait_ge(lgT_ready, 1)
                nc.vector.tensor_copy(lgT[:, th * HALF:(th + 1) * HALF], ps[0:NE, 4 + th, :]).then_inc(lgT_done, 1)
            fourth = top[:, :, TOPK - 1:TOPK].to_broadcast([P, TT, NE])

            def top_logits():
                dve.wait_ge(lg_ready, 1)
                chain(nc.vector.tensor_copy(lg[:], ps[:, 6, 0:TT * NE].rearrange("p (t e) -> p t e", e=NE)))
                for i in range(TT):
                    m = nc.vector.max(top[:, i, :], lg[:, i, :])
                m.then_inc(ex_done, 1)
                dve.wait_ge(ex_done, 1)
                chain(nc.vector.tensor_tensor(ex[:], lg[:], top[:, :, 0:1].to_broadcast([P, TT, NE]), ALU.subtract))

            def chosen():
                chain(nc.vector.tensor_tensor(gt[:], lg[:], fourth, ALU.is_gt))
                chain(nc.vector.tensor_tensor(eq[:], lg[:], fourth, ALU.is_equal))
                chain(nc.vector.tensor_reduce(cnt[:, :, 0], gt[:], AX.X, ALU.add))
                for i in range(TT):
                    m = nc.vector.tensor_tensor_scan(cum[:, i, :], eq[:, i, :], eq[:, i, :], cnt[:, i, 0:1],
                                                     ALU.bypass, ALU.add)
                chain(m)
                chain(nc.vector.tensor_scalar(cum[:], cum[:], float(TOPK), None, ALU.is_le))
                chain(nc.vector.tensor_tensor(eq[:], eq[:], cum[:], ALU.mult))
                chain(nc.vector.tensor_tensor(gt[:], gt[:], eq[:], ALU.add))

            def routing_weights():
                dve.wait_ge(ex_done, 2)
                chain(nc.vector.tensor_tensor(ex[:], ex[:], gt[:], ALU.mult))
                chain(nc.vector.tensor_reduce(tot[:, :, 0], ex[:], AX.X, ALU.add))
                chain(nc.vector.reciprocal(tot[:], tot[:]))
                chain(nc.vector.tensor_tensor(wf[:], ex[:], tot[:].to_broadcast([P, TT, NE]), ALU.mult))
                dve.wait_ge(wp_clear, 1)
                chain(nc.vector.tensor_copy(wp[:, :, 0:NE], wf[:]))
                chain(nc.vector.tensor_tensor(wr[:], wf[:], wp[:, :, 0:NE], ALU.subtract))
                chain(nc.vector.tensor_copy(wp[:, :, NW:NW + NE], wr[:]))
                chain(nc.vector.tensor_tensor(wr[:], wr[:], wp[:, :, NW:NW + NE], ALU.subtract))
                nc.vector.tensor_copy(wp[:, :, 2 * NW:2 * NW + NE], wr[:]).then_inc(wp_done, 1)

            def products(n, th):
                dve.wait_ge(u_ready, n + 1)
                dve.wait_ge(sg_done, n + 1)
                if isinstance(n, int) and n < N_SH:
                    if n >= 2:
                        dve.wait_ge(ah_done, n - 1)
                        dve.wait_ge(al_done, n - 1)
                    nc.vector.tensor_tensor(aw[:, th, :], sg[:, th, :], ps[:, 2 + th, :], ALU.mult).then_inc(aw_done, 1)
                    return
                nc.vector.tensor_tensor(sg[:, th, :], sg[:, th, :], ps[:, 2 + th, :], ALU.mult).then_inc(up_done, 1)
                dve.wait_ge(up_done, n + (1 - N_SH))
                dve.wait_ge(ah_done, n - 1)
                dve.wait_ge(al_done, n - 1)
                nc.vector.tensor_tensor(aw[:, th, :], sg[:, th, :], ps[:, 4 + th, :], ALU.mult).then_inc(aw_done, 1)

            def low(n, k, th):
                toks = slice(th * HALF, (th + 1) * HALF)
                dve.wait_ge(ah_done, n + 1)
                nc.vector.tensor_tensor(a[1][:, k, toks], aw[:, th, :], a[0][:, k, toks].bitcast(F32),
                                        ALU.subtract).then_inc(al_done, 1)

            def add_down(g, i):
                dve.wait_ge(dn_ready, g * TT + (i + 1))
                nc.vector.tensor_tensor(hid[:, i, :], hid[:, i, :], ps[:, 6 + i % 2, 0:D], ALU.add).then_inc(dn_free, 1)

            def tiles(g):
                for k in range(GM):
                    n = g * (2 * GM) + 2 * k
                    first = isinstance(g, int) and g == 0
                    if first and k == 0:
                        top_logits()
                    if first and k == 1:
                        chosen()
                    if first and k == 2:
                        routing_weights()
                    products(n, 0)
                    if k == GM - 1:
                        low(n, k, 0)
                    products(n + 1, 1)
                    if k < GM - 1:
                        low(n, k, 0)
                    low(n + 1, k, 1)
                    if first and k == SH_TILES - 1:
                        dve.wait_ge(wT_ready, 1)
                        nc.vector.tensor_copy(wT[:], ps[:, 6, :].bitcast(BF16)).then_inc(wT_done, 1)

            tiles(0)
            dve.wait_ge(x_added, 1)
            for i in range(TT):
                add_down(0, i)
            with dve.Fori(1, NMG - 1) as g:
                tiles(g)
                for i in range(TT):
                    add_down(g, i)
            tiles(NMG - 1)

            def last_sum(i):
                add_down(NMG - 1, i)
                dve.wait_ge(dn_free, (NMG - 1) * TT + i + 1)

            layernorm(nc, dve, hid, hid, keep, last_sum, st, ag, sq, rc, nw, ln, LN_PARTS)


def constants(nc, ctx):
    def sb(name, shape, dt=F32):
        return ctx.enter_context(nc.sbuf_tensor(name, shape, dt))

    keep = {
        "x1": sb("x1", [P, TT, D]),
        "hid": sb("hid", [P, TT, D]),
        "ident": sb("ident", [P, P]),
        "identb": sb("identb", [P, P], BF16),
        "mask": sb("mask", [P, P], BF16),
        "bn": sb("bn", [P, TT, 6]),
        "stats": sb("stats", [P, TT, 6]),
        "eps": sb("eps", [P, 2]),
    }
    made, shaped = ctx.enter_context(nc.semaphore("c_made")), ctx.enter_context(nc.semaphore("c_shaped"))
    with nc.Block() as block:
        @block.gpsimd
        def _(pool):
            nc.gpsimd.memset(keep["ident"][:], 0.0).then_inc(made, 1)
            nc.gpsimd.memset(keep["identb"][:], 0.0).then_inc(made, 1)
            nc.gpsimd.memset(keep["mask"][:], 0.0).then_inc(made, 1)
            nc.gpsimd.memset(keep["eps"][:, 0:1], LN_EPS).then_inc(made, 1)
            nc.gpsimd.memset(keep["eps"][:, 1:2], RMS_EPS).then_inc(made, 1)
            pool.wait_ge(made, 5)
            for m in ("ident", "identb"):
                nc.gpsimd.affine_select(out=keep[m][:], in_=keep[m][:], compare_op=ALU.not_equal, fill=1.0, base=0,
                                        pattern=[[-1, P]], channel_multiplier=1).then_inc(shaped, 1)
            nc.gpsimd.affine_select(out=keep["mask"][:], in_=keep["mask"][:], compare_op=ALU.is_ge, fill=MASKED, base=0,
                                    pattern=[[-1, P]], channel_multiplier=1).then_inc(shaped, 1)
            pool.wait_ge(shaped, 3)
    return keep


def program(nc, d, out):
    with ExitStack() as ctx:
        ps = ctx.enter_context(nc.psum_tensor("ps", [P, 8, 512], F32))
        keep = constants(nc, ctx)
        with ExitStack() as part:
            mamba_block(nc, part, d, keep, ps)
        shared_buffers(nc, ctx, keep)
        with ExitStack() as part:
            attention_block(nc, part, d, keep, ps)
        with ExitStack() as part:
            expert_block(nc, part, d, keep, ps, out)


def layouts(i):
    f = {k: np.asarray(v) for k, v in i.items()}
    x = f["L0_attn_x"].reshape(T, D)

    def t_chunks(w):
        return w.T.reshape(-1, P, w.shape[0]).transpose(1, 0, 2)

    def per_channel(v):
        return v.reshape(EC, P, -1).transpose(1, 0, 2)

    w_x = f["L0_attn_W_x"]
    bc = w_x[DT_RANK:]
    q_w = f["L0_ffn_q_w"].reshape(NH, HD + ROPE, D)[:, :HD]
    kv = f["L0_ffn_kv_w"]
    k_w, v_w = kv[:NH * HD].reshape(NH, HD, D), kv[NH * HD:2 * NH * HD].reshape(NH // 2, 2 * HD, D)
    o_w = f["L0_ffn_o_w"].reshape(D, NH, HD)
    attn_w = np.zeros((NH + GH, P, PACK), np.float32)
    for h in range(NH):
        attn_w[h, :, 0:256] = t_chunks(q_w[h]).reshape(P, -1)
        attn_w[h, :, 256:512] = t_chunks(k_w[h]).reshape(P, -1)
        attn_w[h, :, 512:768] = t_chunks(v_w[h // 2])[:, h % 2]
        attn_w[h + GH, :, 768:1024] = o_w[:, h].T
    w1, sh = f["L0_ffn_w1"], f["L0_ffn_sh_gu_w"]
    rows = np.zeros((3, NM * P, D), np.float32)
    routed = SH_TILES * P
    for n in range(2):
        rows[n, :SHI] = sh[n * SHI:(n + 1) * SHI]
        rows[n, routed:] = w1[:, n * EI:(n + 1) * EI].reshape(-1, D)
    rows[2, :SHI] = f["L0_ffn_sh_down_w"].T
    rows[2, routed:] = f["L0_ffn_w2"].transpose(0, 2, 1).reshape(-1, D)
    expert_w = np.zeros((NM + GM, P, FPACK), np.float32)
    for m in range(NM):
        for n in range(2):
            expert_w[m, :, n * D:(n + 1) * D] = t_chunks(rows[n, m * P:(m + 1) * P]).reshape(P, -1)
        expert_w[m + GM, :, 2 * D:] = rows[2, m * P:(m + 1) * P]
    a = {
        "attn_w": attn_w, "expert_w": expert_w,
        "ln1": f["L0_ffn_ln1_w"].reshape(DC, P).T, "ln2": f["L0_ffn_ln2_w"].reshape(DC, P).T,
        "gate": t_chunks(f["L0_ffn_gate_w"]),
        "xT": t_chunks(x),
        "w_in": t_chunks(f["L0_attn_W_in"]),
        "chan": np.concatenate([per_channel(f[k]) for k in (
            "L0_attn_conv_w", "L0_attn_conv_b", "L0_attn_b_dt", "L0_attn_Dp", "L0_attn_A_log")], axis=2),
        "w_x": t_chunks(np.concatenate([w_x[:DT_RANK], bc, bc, bc, bc])),
        "w_dt": f["L0_attn_W_dt"].T,
        "w_out": t_chunks(f["L0_attn_W_out"]),
    }
    return {k: np.ascontiguousarray(v) for k, v in a.items()}


def kernel(**inputs):
    import concourse.bacc as bacc
    from concourse.bass_utils import run_bass_kernel_spmd

    arrays = layouts(inputs)
    nc = bacc.Bacc("TRN2", target_bir_lowering=False, num_devices=1)
    d = {k: nc.dram_tensor(f"in_{k}", v.shape, mybir.dt.from_np(v.dtype), kind="ExternalInput").ap()
         for k, v in arrays.items()}
    out = nc.dram_tensor("out", (P, TT, D), F32, kind="ExternalOutput").ap()
    program(nc, d, out)
    r = run_bass_kernel_spmd(nc, [{f"in_{k}": v for k, v in arrays.items()}], core_ids=[0])
    got = r.results[0]["out"]
    return got.transpose(1, 0, 2).reshape(BATCH, SEQ, D)
```

```python
from contextlib import ExitStack

import numpy as np
import concourse.bass as bass
from concourse import mybir

F32 = mybir.dt.float32
F32R = mybir.dt.float32r
BF16 = mybir.dt.bfloat16
ALU = mybir.AluOpType
ACT = mybir.ActivationFunctionType
AX = mybir.AxisListType

P = 128
BATCH, SEQ, D = 4, 256, 256
T = BATCH * SEQ
TT = T // P
DC = D // P
HALF = T // 2
E_IN = 512
EC = E_IN // P
NS = 16
NTAP = 4
DT_RANK = 128
CH = NTAP + 3 + NS
NH, HD, ROPE = 16, 128, 64
QSCALE = float(HD + ROPE) ** -0.5
GH = 4
NG = NH // GH
PACK = 1024
NE, EI, TOPK, NSH = 16, 176, 4, 2
SHI = NSH * EI
SH_TILES = (SHI + P - 1) // P
NM_R = NE * EI // P
NM = SH_TILES + NM_R
GM = 5
NMG = NM // GM
NW = 32
FPACK = 3 * D
LN_EPS, RMS_EPS = 1e-5, 1e-6
MASKED = -1.0e30


def banks(ps, first, n=1):
    return ps[:, first:first + n, :].rearrange("p b n -> p (b n)")


def mamba_block(nc, ctx, d, keep, ps):
    def sb(name, shape, dt=F32):
        return ctx.enter_context(nc.sbuf_tensor(name, shape, dt))

    def sem(name):
        return ctx.enter_context(nc.semaphore(name))

    x1, ident, stats = keep["x1"], keep["ident"], keep["stats"]
    xT = sb("m_xT", [P, DC, T])
    w_in = sb("m_w_in", [P, DC, 2 * E_IN])
    w_x = sb("m_w_x", [P, EC, 2 * P])
    w_dt = sb("m_w_dt", [P, E_IN])
    w_out = sb("m_w_out", [P, EC, D])
    chan = sb("m_chan", [P, EC, CH])
    xpad = sb("m_xpad", [P, EC, BATCH, SEQ + NTAP - 1])
    conv = sb("m_conv", [P, EC, T])
    xc = sb("m_xc", [P, EC, T])
    z = xpad[:].rearrange("p c b t -> p c (b t)")[:, :, 0:T]
    delta = sb("m_delta", [P, EC, T])
    du = sb("m_du", [P, EC, T])
    dt = sb("m_dt", [P, T])
    negA = sb("m_negA", [P, EC, NS])
    bcp = sb("m_bcp", [P, T], BF16)
    sel = sb("m_sel", [P, 2 * NS, P], BF16)
    dp_diag = sb("m_dp_diag", [P, EC, P])
    b_sb = sb("m_b_sb", [P, 2, HALF])
    dA = sb("m_dA", [P, EC, HALF])
    dbx = sb("m_dbx", [P, EC, HALF])
    h = sb("m_h", [P, EC, HALF])
    hc = sb("m_hc", [P, 2, EC, HALF])
    spa = dbx[:].rearrange("p (a c) t -> p a (c t)", a=2)
    spl = dA[:].rearrange("p (a c) t -> p a (c t)", a=2)
    spu = hc[:, 0, :, :].rearrange("p (a c) t -> p a (c t)", a=2)
    spt = h[:].rearrange("p (a c) t -> p a (c t)", a=2)
    bcr = du[:, 0, :]
    yT = conv

    ld_chan, ld_x0, ld_x1, ld_w0, ld_w1, ld_w2, ld_wx, ld_wdt, ld_wo = (
        sem(f"m_ld_{n}") for n in ("chan", "x0", "x1", "w0", "w1", "w2", "wx", "wdt", "wo"))
    pads_ready = sem("m_pads_ready")
    sel_zero, sel_ready = sem("m_sel_zero"), sem("m_sel_ready")
    pair_ready, pair_free = sem("m_pair_ready"), sem("m_pair_free")
    conv_step = sem("m_conv_step")
    xc_ready = sem("m_xc_ready")
    dt_ready, dt_sb_ready = sem("m_dt_ready"), sem("m_dt_sb_ready")
    bc_ready, bc_step = sem("m_bc_ready"), sem("m_bc_step")
    v_ready, abs_ready, e_ready = sem("m_v_ready"), sem("m_abs_ready"), sem("m_e_ready")
    u_ready, l_ready, t_ready = sem("m_u_ready"), sem("m_l_ready"), sem("m_t_ready")
    lt_ready, delta_ready, du_ready = sem("m_lt_ready"), sem("m_delta_ready"), sem("m_du_ready")
    a_exp, a_ready = sem("m_a_exp"), sem("m_a_ready")
    dp_ready = sem("m_dp_ready")
    ld_xt, x_added = sem("m_ld_xt"), sem("m_x_added")
    z_ready = sem("m_z_ready")
    b_ready, b_sb_ready, c_ready = sem("m_b_ready"), sem("m_b_sb_ready"), sem("m_c_ready")
    dA_ready, dbx_ready = sem("m_dA_ready"), sem("m_dbx_ready")
    dA_zeroed = sem("m_dA_zeroed")
    att_zero, att_shaped = sem("m_att_zero"), sem("m_att_shaped")
    scan_done = sem("m_scan_done")
    h_ready = sem("m_h_ready")
    hc_ready = sem("m_hc_ready")
    hc_free = sem("m_hc_free")
    y_done = sem("m_y_done")
    o_ready, o_free = sem("m_o_ready"), sem("m_o_free")
    st, ag, sq, rc, nw, ln = (sem(f"m_ln_{n}") for n in ("stat", "aggr", "sqrt", "rec", "newton", "out"))
    sq_done, root = sem("m_sq_done"), sem("m_root")

    DELTA0, Z0 = EC, 2 * EC
    Q = EC // 2
    PER_HALF = NS * Q

    CUTS = ([(1, NS // 2 - 1)], [(1, 2), (2, 3), (3, 5), (5, 6), (6, 7)])

    def out_bank(i):
        return 7 if i < TT // 2 else (7, 4, 5, 6)[i - TT // 2]

    def taps(c, k):
        return chan[:, c, k:k + 1]

    conv_b, b_dt, d_p = ([chan[:, c, NTAP + k:NTAP + k + 1] for c in range(EC)] for k in range(3))

    with nc.Block() as block:
        @block.sync
        def _(sp):
            sp.dma_start(w_in[:, :, 0:P], d["w_in"][:, :, 0:P]).then_inc(ld_w0, 16)
            sp.dma_start(xT[:, :, 0:HALF], d["xT"][:, :, 0:HALF]).then_inc(ld_x0, 16)
            sp.dma_start(xT[:, :, HALF:], d["xT"][:, :, HALF:]).then_inc(ld_x1, 16)
            sp.dma_start(chan[:], d["chan"]).then_inc(ld_chan, 16)
            sp.dma_start(w_in[:, :, P:E_IN], d["w_in"][:, :, P:E_IN]).then_inc(ld_w1, 16)
            sp.dma_start(w_x[:], d["w_x"]).then_inc(ld_wx, 16)
            sp.dma_start(w_dt[:], d["w_dt"]).then_inc(ld_wdt, 16)
            sp.dma_start(w_in[:, :, E_IN:], d["w_in"][:, :, E_IN:]).then_inc(ld_w2, 16)
            sp.dma_start(w_out[:], d["w_out"]).then_inc(ld_wo, 16)
            sp.dma_start(x1[:], d["x_tok"]).then_inc(ld_xt, 16)
            sp.dma_start(keep["ln1"][:], d["ln1"]).then_inc(keep["ld_ln1"], 16)
            for j in range(GH):
                sp.dma_start(keep["raw"][:, j, :], d["attn_w"][j]).then_inc(keep["ld_attn"][j], 16)

        @block.gpsimd
        def _(pool):
            nc.gpsimd.memset(xpad[:, :, :, 0:NTAP - 1], 0.0).then_inc(pads_ready, 1)
            nc.gpsimd.memset(sel[:], 0.0).then_inc(sel_zero, 1)
            pool.wait_ge(sel_zero, 1)
            for n, q in enumerate((0, 2, 3)):
                if n:
                    pool.wait_ge(sel_ready, n)
                v = sel[32 * q:32 * q + 32, :, :]
                nc.gpsimd.affine_select(out=v, in_=v, compare_op=ALU.not_equal, fill=1.0, base=0,
                                        pattern=[[-1, 2 * NS], [0, P]], channel_multiplier=1
                                        ).then_inc(sel_ready, 1)
            pool.wait_ge(sel_ready, 3)
            mask, identb = keep["mask"], keep["identb"]
            nc.gpsimd.memset(identb[:], 0.0).then_inc(att_zero, 1)
            nc.gpsimd.memset(mask[:], 0.0).then_inc(att_zero, 1)
            pool.wait_ge(att_zero, 2)
            nc.gpsimd.affine_select(out=identb[:], in_=identb[:], compare_op=ALU.not_equal, fill=1.0, base=0,
                                    pattern=[[-1, P]], channel_multiplier=1).then_inc(att_shaped, 1)
            for at in (0, 2 * P):
                nc.gpsimd.affine_select(out=mask[:, at:at + P], in_=mask[:, at:at + P], compare_op=ALU.is_ge,
                                        fill=MASKED, base=0, pattern=[[-1, P]], channel_multiplier=1
                                        ).then_inc(att_shaped, 1)
            pool.wait_ge(att_shaped, 3)
            for c in range(EC):
                pool.wait_ge(l_ready, c + 1)
                pool.wait_ge(t_ready, c + 1)
                nc.gpsimd.tensor_tensor(spl[:, c % 2, :], spl[:, c % 2, :], spt[:, c % 2, :],
                                        ALU.subtract).then_inc(lt_ready, 1)

            def dbx_state(half, i, s2):
                s_done = i * 2 + (half * NS + s2)
                for q in range(Q):
                    n, known = s_done * Q + q, isinstance(i, int)
                    if q == 0:
                        pool.wait_ge(b_sb_ready, s_done + 1)
                    if known and n < Q:
                        pool.wait_ge(du_ready, 2 * q + 2)
                    else:
                        pool.wait_ge(scan_done, n + (1 - Q))
                    two = slice(2 * q, 2 * q + 2)
                    nc.gpsimd.tensor_tensor(
                        dbx[:, two, :], du[:, two, half * HALF:(half + 1) * HALF],
                        b_sb[:, s2:s2 + 1, :].to_broadcast([P, 2, HALF]), ALU.mult).then_inc(dbx_ready, 1)

            for half in range(2):
                dbx_state(half, 0, 0)
                dbx_state(half, 0, 1)
                with pool.Fori(1, NS // 2) as i:
                    dbx_state(half, i, 0)
                    dbx_state(half, i, 1)

        @block.tensor
        def _(pe):
            def pair(r, steps):
                if r >= 2:
                    pe.wait_ge(pair_free, r - 1)
                for th in range(2):
                    if r == 0 and th == 1:
                        pe.wait_ge(ld_x1, 16)
                    for k, (lhs, rhs) in enumerate(steps):
                        mm = nc.tensor.matmul(ps[:, 2 * (r % 2) + th, :], lhs, rhs[:, th * HALF:(th + 1) * HALF],
                                              start=(k == 0), stop=(k == len(steps) - 1))
                mm.then_inc(pair_ready, 1)

            def project_in(r, c):
                pair(r, [(w_in[:, k, c * P:(c + 1) * P], xT[:, k, :]) for k in range(DC)])

            def row_of(s):
                return sel[:, bass.ds(s, 1), :].rearrange("p a n -> p (a n)")

            def broadcast_b(half, s, s_done):
                if not (isinstance(s_done, int) and s_done == 0):
                    pe.wait_ge(b_sb_ready, s_done)
                nc.tensor.matmul(ps[:, 4, :], row_of(s), bcp[:, half * HALF:(half + 1) * HALF],
                                 start=True, stop=True).then_inc(b_ready, 1)

            def broadcast_c(half, s, s2):
                nc.tensor.matmul(ps[:, 5 + s2, :], row_of(s + NS), bcp[:, half * HALF:(half + 1) * HALF],
                                 start=True, stop=True).then_inc(c_ready, 1)

            def project_x(c):
                pe.wait_ge(xc_ready, c + 1)
                for o in range(2):
                    for th in range(2):
                        mm = nc.tensor.matmul(ps[:, 4 + 2 * o + th, :], w_x[:, c, o * P:(o + 1) * P],
                                              xc[:, c, th * HALF:(th + 1) * HALF], start=(c == 0), stop=(c == EC - 1))
                    if c == EC - 1:
                        mm.then_inc(dt_ready if o == 0 else bc_ready, 1)

            pe.wait_ge(ld_w0, 16)
            pe.wait_ge(ld_x0, 16)
            project_in(0, 0)
            pe.wait_ge(ld_w1, 16)
            for c in range(1, EC):
                project_in(c, c)
            pe.wait_ge(ld_wx, 16)
            for c in range(EC):
                project_x(c)
            pe.wait_ge(ld_wdt, 16)
            pe.wait_ge(dt_sb_ready, 1)
            for c in range(EC):
                pair(DELTA0 + c, [(w_dt[:, c * P:(c + 1) * P], dt[:])])
            pe.wait_ge(bc_step, 5)
            pe.wait_ge(sel_ready, 3)
            broadcast_b(0, 0, 0)
            broadcast_c(0, 0, 0)
            pe.wait_ge(ld_w2, 16)
            for c in range(EC - 1):
                project_in(Z0 + c, EC + c)
            broadcast_b(0, 1, 1)
            project_in(Z0 + EC - 1, 2 * EC - 1)

            def start_y(half):
                if half == 0:
                    pe.wait_ge(dp_ready, EC)
                    pe.wait_ge(pair_free, 3 * EC)
                for c in range(EC):
                    if half:
                        pe.wait_ge(y_done, c + 1)
                    nc.tensor.matmul(ps[:, c, :], dp_diag[:, c, :], xc[:, c, half * HALF:(half + 1) * HALF],
                                     start=True, stop=False, skip_group_check=True)

            def sum_y(n, s2, c):
                if c % 2 == 0:
                    pe.wait_ge(hc_ready, n + 1)
                nc.tensor.matmul(ps[:, c, :], ident[:, :], hc[:, s2, c, :], start=False, stop=False,
                                 skip_group_check=True).then_inc(hc_free, 1)

            def out_part(i, c):
                mm = nc.tensor.matmul(ps[:, out_bank(i), 0:D], yT[:, c, i * P:(i + 1) * P], w_out[:, c, :],
                                      start=(c == 0), stop=(c == EC - 1))
                if c == EC - 1:
                    mm.then_inc(o_ready, 1)

            def out_tile(i):
                if i == 0:
                    pe.wait_ge(ld_wo, 16)
                else:
                    pe.wait_ge(o_free, i)
                for c in range(EC):
                    out_part(i, c)

            def state(half, s, s2):
                known = isinstance(s, int)
                if not (known and s == NS - 1):
                    broadcast_c(half, s + 1, 1 - s2)
                elif half == 0:
                    broadcast_c(1, 0, 0)
                for c in range(EC):
                    if c == 0:
                        if not (known and s >= NS - 2):
                            broadcast_b(half, s + 2, s + (half * NS + 2))
                        elif half == 0:
                            broadcast_b(1, s + 2 - NS, s + 2)
                    sum_y(s * Q + (half * PER_HALF + c // 2), s2, c)

            for half in range(2):
                start_y(half)
                state(half, 0, 0)
                state(half, 1, 1)
                for run, (lo, hi) in enumerate(CUTS[half]):
                    with pe.Fori(lo, hi) as i:
                        state(half, i * 2, 0)
                        state(half, i * 2 + 1, 1)
                    if half == 1 and run < TT // 2:
                        out_tile(run)
                state(half, NS - 2, 0)
                state(half, NS - 1, 1)
            pe.wait_ge(o_free, TT // 2)
            for c in range(EC):
                pe.wait_ge(y_done, EC + c + 1)
                for i in range(TT // 2, TT):
                    out_part(i, c)

        @block.scalar
        def _(act):
            act.wait_ge(ld_chan, 16)
            nc.scalar.activation(negA[:], chan[:, :, NTAP + 3:], ACT.Exp).then_inc(a_exp, 1)
            nc.scalar.preload_act_table_set("silu_and_others")
            act.wait_ge(pads_ready, 1)

            def copy_xp(c):
                act.wait_ge(pair_ready, c + 1)
                nc.scalar.activation(xpad[:, c, :, NTAP - 1:], banks(ps, 2 * (c % 2), 2).rearrange(
                    "p (b t) -> p b t", b=BATCH), ACT.Copy)
                nc.scalar.activation(conv[:, c, :], banks(ps, 2 * (c % 2), 2), ACT.Identity, bias=conv_b[c],
                                     scale=taps(c, NTAP - 1)).then_inc(pair_free, 1)

            def silu_xc(c):
                act.wait_ge(conv_step, (NTAP - 1) * (c + 1))
                nc.scalar.activation(xc[:, c, :], conv[:, c, :], ACT.Silu).then_inc(xc_ready, 1)

            def take_z(c):
                act.wait_ge(pair_ready, Z0 + c + 1)
                nc.scalar.activation(z[:, c, :], banks(ps, 2 * (c % 2), 2), ACT.Copy).then_inc(pair_free, 1)

            copy_xp(0)
            copy_xp(1)
            copy_xp(2)
            silu_xc(0)
            copy_xp(3)
            for c in range(1, EC):
                silu_xc(c)
            nc.scalar.preload_act_table_set("natural_log_exp_and_others")
            act.wait_ge(dt_ready, 1)
            nc.scalar.activation(dt[:], banks(ps, 4, 2), ACT.Copy).then_inc(dt_sb_ready, 1)

            def take_v(c):
                act.wait_ge(pair_ready, DELTA0 + c + 1)
                nc.scalar.activation(conv[:, c, :], banks(ps, 2 * ((DELTA0 + c) % 2), 2), ACT.Identity,
                                     bias=b_dt[c]).then_inc(pair_free, 1)

            def exp_v(c):
                act.wait_ge(abs_ready, c + 1)
                nc.scalar.activation(spa[:, c % 2, :], spa[:, c % 2, :], ACT.Exp).then_inc(e_ready, 1)

            def log_u(c):
                act.wait_ge(u_ready, c + 1)
                if c >= 2:
                    act.wait_ge(delta_ready, c - 1)
                nc.scalar.activation(spl[:, c % 2, :], spu[:, c % 2, :], ACT.Ln).then_inc(l_ready, 1)

            def copy_b(s_done, s2):
                act.wait_ge(b_ready, s_done + 1)
                if not (isinstance(s_done, int) and s_done < 2):
                    act.wait_ge(dbx_ready, s_done * Q - Q)
                nc.scalar.activation(b_sb[:, s2, :], ps[:, 4, :], ACT.Copy).then_inc(b_sb_ready, 1)

            take_v(0)
            take_v(1)
            exp_v(0)
            take_v(2)
            exp_v(1)
            log_u(0)
            take_v(3)
            exp_v(2)
            log_u(1)
            take_z(0)
            exp_v(3)
            log_u(2)
            take_z(1)
            log_u(3)
            copy_b(0, 0)
            take_z(2)
            take_z(3)

            def state(half, s, s2):
                for c in range(EC):
                    if c % 2 == 0 and not (isinstance(s, int) and half == 0 and s == 0):
                        act.wait_ge(scan_done, s * Q + (half * PER_HALF + c // 2 + 1 - Q))
                    nc.scalar.activation(
                        dA[:, c, :].rearrange("p (b t) -> p b t", b=2)[:, :, 1:],
                        delta[:, c, half * HALF:(half + 1) * HALF].rearrange("p (b t) -> p b t", b=2)[:, :, 1:],
                        ACT.Exp, scale=negA[:, c, bass.ds(s, 1)]).then_inc(dA_ready, 1)
                    if c == 1 and not (isinstance(s, int) and half == 1 and s == NS - 1):
                        copy_b(s + (half * NS + 1), 1 - s2)

            def take_out(i):
                act.wait_ge(o_ready, i + 1)
                nc.scalar.activation(keep["hid"][:, i, :], ps[:, out_bank(i), 0:D], ACT.Copy).then_inc(o_free, 1)

            act.wait_ge(delta_ready, EC)
            act.wait_ge(a_ready, 1)
            act.wait_ge(dA_zeroed, 1)
            for half in range(2):
                state(half, 0, 0)
                act.wait_ge(pair_free, 3 * EC)
                z_half = z[:, :, half * HALF:(half + 1) * HALF]
                nc.scalar.activation(z_half, z_half, ACT.Silu).then_inc(z_ready, 1)
                nc.scalar.preload_act_table_set("exp_and_others")
                state(half, 1, 1)
                for run, (lo, hi) in enumerate(CUTS[half]):
                    with act.Fori(lo, hi) as i:
                        state(half, i * 2, 0)
                        state(half, i * 2 + 1, 1)
                    if half == 1 and run:
                        take_out(run - 1)
                state(half, NS - 2, 0)
                state(half, NS - 1, 1)
            nc.scalar.preload_act_table_set("sqrt_and_others")
            for tiles in (slice(0, TT // 2), slice(TT // 2, TT)):
                act.wait_ge(ag, tiles.stop)
                nc.scalar.activation(stats[:, tiles, 2], stats[:, tiles, 1], ACT.Sqrt,
                                     bias=keep["eps"][:, 0:1]).then_inc(sq, 1)
            squares(nc, act, keep, lambda i: x1[:, i, :], lambda i: keep["hid"][:, i, :],
                    lambda i: act.wait_ge(ln, i + 1), sq_done, root)

        @block.vector
        def _(dve):
            dve.wait_ge(a_exp, 1)
            nc.vector.tensor_scalar(negA[:], negA[:], -1.0, None, ALU.mult).then_inc(a_ready, 1)
            for c in range(EC):
                nc.vector.tensor_scalar(dp_diag[:, c, :], ident[:], d_p[c], None, ALU.mult).then_inc(dp_ready, 1)
            for c in range(EC):
                dve.wait_ge(pair_free, c + 1)
                out = conv[:, c, :].rearrange("p (b t) -> p b t", b=BATCH)
                for k in range(NTAP - 1):
                    if k:
                        dve.wait_ge(conv_step, (NTAP - 1) * c + k)
                    nc.vector.scalar_tensor_tensor(out=out, in0=xpad[:, c, :, k:k + SEQ], scalar=taps(c, k), in1=out,
                                                   op0=ALU.mult, op1=ALU.add).then_inc(conv_step, 1)
            bc = banks(ps, 6, 2)
            dve.wait_ge(bc_ready, 1)
            nc.vector.tensor_copy(bcp[:], bc).then_inc(bc_step, 1)
            dve.wait_ge(bc_step, 1)
            nc.vector.tensor_tensor(bcr[64:P, :], bc[64:P, :], bcp[64:P, :], ALU.subtract).then_inc(bc_step, 1)
            dve.wait_ge(bc_step, 2)
            nc.vector.tensor_copy(bcp[64:P, :], bcr[64:P, :]).then_inc(bc_step, 1)
            dve.wait_ge(bc_step, 3)
            nc.vector.tensor_tensor(bcr[96:P, :], bcr[96:P, :], bcp[96:P, :], ALU.subtract).then_inc(bc_step, 1)
            dve.wait_ge(bc_step, 4)
            nc.vector.tensor_copy(bcp[96:P, :], bcr[96:P, :]).then_inc(bc_step, 1)
            def neg_abs(c):
                dve.wait_ge(pair_free, DELTA0 + c + 1)
                if c >= 2:
                    dve.wait_ge(t_ready, c - 1)
                nc.vector.scalar_tensor_tensor(out=spa[:, c % 2, :], in0=conv[:, c, :], scalar=-1.0,
                                               in1=conv[:, c, :], op0=ALU.mult, op1=ALU.min).then_inc(abs_ready, 1)

            def one_plus(c):
                s2 = c % 2
                dve.wait_ge(e_ready, c + 1)
                if c >= 2:
                    dve.wait_ge(t_ready, c - 1)
                    dve.wait_ge(l_ready, c - 1)
                nc.vector.tensor_scalar(spu[:, s2, :], spa[:, s2, :], 1.0, None, ALU.add).then_inc(u_ready, 1)
                dve.wait_ge(u_ready, c + 1)
                if c >= 2:
                    dve.wait_ge(lt_ready, c - 1)
                nc.vector.scalar_tensor_tensor(out=spt[:, s2, :], in0=spu[:, s2, :], scalar=-1.0, in1=spa[:, s2, :],
                                               op0=ALU.add, op1=ALU.subtract).then_inc(t_ready, 1)

            def sum_delta(c):
                dve.wait_ge(lt_ready, c + 1)
                nc.vector.scalar_tensor_tensor(out=delta[:, c, :], in0=conv[:, c, :], scalar=0.0, in1=spl[:, c % 2, :],
                                               op0=ALU.max, op1=ALU.add).then_inc(delta_ready, 1)

            def times_x(c):
                dve.wait_ge(delta_ready, c + 1)
                nc.vector.tensor_tensor(du[:, c, :], delta[:, c, :], xc[:, c, :], ALU.mult).then_inc(du_ready, 1)

            neg_abs(0)
            neg_abs(1)
            one_plus(0)
            neg_abs(2)
            one_plus(1)
            neg_abs(3)
            sum_delta(0)
            one_plus(2)
            sum_delta(1)
            one_plus(3)
            sum_delta(2)
            times_x(0)
            times_x(1)
            sum_delta(3)
            dve.wait_ge(delta_ready, EC)
            nc.vector.memset(dA[:].rearrange("p c (b t) -> p c b t", b=2)[:, :, :, 0:1], 0.0).then_inc(dA_zeroed, 1)
            times_x(2)
            times_x(3)

            def scan(n, q):
                dve.wait_ge(dA_ready, n * 2 + 2)
                dve.wait_ge(dbx_ready, n + 1)
                if not (isinstance(n, int) and n < Q):
                    dve.wait_ge(hc_ready, n + (1 - Q))
                h2, dA2, dbx2 = (x[:, 2 * q:2 * q + 2, :].rearrange("p c t -> p (c t)") for x in (h, dA, dbx))
                nc.vector.tensor_tensor_scan(h2, dA2, dbx2, 0.0, ALU.mult, ALU.add).then_inc(scan_done, 1)

            def times_c(n, s_done, s2, q):
                if q == 0:
                    dve.wait_ge(c_ready, s_done + 1)
                dve.wait_ge(scan_done, n + 1)
                if not (isinstance(n, int) and n < 2 * Q):
                    dve.wait_ge(hc_free, n * 2 - (4 * Q - 2))
                two = slice(2 * q, 2 * q + 2)
                nc.vector.tensor_tensor(hc[:, s2, two, :], h[:, two, :],
                                        ps[:, 5 + s2:6 + s2, :].to_broadcast([P, 2, HALF]),
                                        ALU.mult).then_inc(hc_ready, 1)

            def finish_y(half, c):
                toks = slice(half * HALF, (half + 1) * HALF)
                if c == 0:
                    dve.wait_ge(z_ready, half + 1)
                dve.wait_ge(hc_free, (half + 1) * NS * EC - EC + c + 1)
                nc.vector.tensor_tensor(yT[:, c, toks], z[:, c, toks], ps[:, c, :], ALU.mult).then_inc(y_done, 1)

            def state(half, i, s2):
                s_done = i * 2 + (half * NS + s2)
                first = half == 1 and isinstance(i, int) and s2 == 0
                for q in range(Q):
                    scan(s_done * Q + q, q)
                    if first:
                        finish_y(0, 2 * q)
                        finish_y(0, 2 * q + 1)
                for q in range(Q):
                    times_c(s_done * Q + q, s_done, s2, q)

            for half in range(2):
                state(half, 0, 0)
                state(half, 0, 1)
                with dve.Fori(1, NS // 2) as i:
                    state(half, i, 0)
                    state(half, i, 1)
            for c in range(EC):
                finish_y(1, c)

            def x_added_to(i):
                if i == 0:
                    dve.wait_ge(ld_xt, 16)
                if i < TT // 2:
                    dve.wait_ge(o_free, i + 1)
                else:
                    dve.wait_ge(o_ready, i + 1)
                mixed = keep["hid"][:, i, :] if i < TT // 2 else ps[:, out_bank(i), 0:D]
                nc.vector.tensor_tensor(x1[:, i, :], x1[:, i, :], mixed, ALU.add).then_inc(x_added, 1)
                dve.wait_ge(x_added, i + 1)

            layernorm(nc, dve, x1, x1, keep, x_added_to, st, ag, sq, rc, nw, ln, 2)


def layernorm(nc, dve, src, dst, keep, ready, st, ag, sq, rc, nw, ln, parts=1):
    bn, stats, run = keep["bn"], keep["stats"], TT // parts
    for part in range(parts):
        tiles = range(part * run, (part + 1) * run)
        for i in tiles:
            ready(i)
            nc.vector.bn_stats(bn[:, i, :], src[:, i, :]).then_inc(st, 1)
            if i > tiles[0]:
                dve.wait_ge(st, i)
                nc.vector.bn_aggr(stats[:, i - 1, 0:2], bn[:, i - 1, :]).then_inc(ag, 1)
        dve.wait_ge(st, tiles[-1] + 1)
        nc.vector.bn_aggr(stats[:, tiles[-1], 0:2], bn[:, tiles[-1], :]).then_inc(ag, 1)
        dve.wait_ge(sq, part + 1)
        inverse_root(nc, dve, stats[:, tiles[0]:tiles[-1] + 1, :], 1, LN_EPS, 1.0, rc, nw, part)
        for i in tiles:
            nc.vector.tensor_scalar(dst[:, i, :], src[:, i, :], stats[:, i, 0:1], stats[:, i, 3:4],
                                    ALU.subtract, ALU.mult).then_inc(ln, 1)


def inverse_root(nc, dve, stats, col, eps, scale, rc, nw, before=0):
    r0, n0 = 2 * before, 4 * before
    v, r, t, w = stats[:, :, col], stats[:, :, 3], stats[:, :, 4], stats[:, :, 5]
    nc.vector.tensor_scalar(w, v, scale, eps, ALU.mult, ALU.add).then_inc(nw, 1)
    nc.vector.reciprocal(r, stats[:, :, 2]).then_inc(rc, 1)
    dve.wait_ge(rc, r0 + 1)
    dve.wait_ge(nw, n0 + 1)
    nc.vector.tensor_tensor(t, r, r, ALU.mult).then_inc(nw, 1)
    dve.wait_ge(nw, n0 + 2)
    nc.vector.tensor_tensor(t, t, w, ALU.mult).then_inc(rc, 1)
    dve.wait_ge(rc, r0 + 2)
    nc.vector.tensor_scalar(t, t, -0.5, 1.5, ALU.mult, ALU.add).then_inc(nw, 1)
    dve.wait_ge(nw, n0 + 3)
    nc.vector.tensor_tensor(r, r, t, ALU.mult).then_inc(nw, 1)
    dve.wait_ge(nw, n0 + 4)


def three_passes(nc, out, lhs, rhs, start, stop):
    (lh, ll), (rh, rl) = lhs, rhs
    nc.tensor.matmul(out, lh, rh, start=start, stop=False, skip_group_check=True)
    nc.tensor.matmul(out, lh, rl, start=False, stop=False, skip_group_check=True)
    return nc.tensor.matmul(out, ll, rh, start=False, stop=stop, skip_group_check=True)


def squares(nc, act, keep, src, junk, wait, sq_done, root):
    stats = keep["stats"]
    for i in range(TT):
        wait(i)
        nc.scalar.activation(junk(i), src(i), ACT.Square, accum_out=stats[:, i, 0:1]).then_inc(sq_done, 1)
    act.wait_ge(sq_done, TT)
    nc.scalar.activation(stats[:, :, 2], stats[:, :, 0], ACT.Sqrt, scale=1.0 / D,
                         bias=keep["eps"][:, 1:2]).then_inc(root, 1)


def rms_plan(nc, ctx, keep, ps, src, ln_w, name, first_bank, squared=False):
    def sem(n):
        return ctx.enter_context(nc.semaphore(f"{name}_{n}"))

    stats = keep["stats"]
    xr = ctx.enter_context(nc.sbuf_tensor(f"{name}_xr", [P, TT, D], F32))
    hi = ctx.enter_context(nc.sbuf_tensor(f"{name}_hi", [P, DC, T], F32R))
    lo = ctx.enter_context(nc.sbuf_tensor(f"{name}_lo", [P, DC, T], F32R))
    sq_done, root, rc, nw = sem("squares"), sem("root"), sem("rec"), sem("newton")
    scaled, turned, hi_done, lo_done = sem("scaled"), sem("turned"), sem("hi"), sem("lo")
    per_bank = 512 // P

    def bank(u):
        return ps[:, first_bank + u % 4, :]

    def scalar(act):
        if not squared:
            squares(nc, act, keep, lambda i: src[:, i, :], lambda i: xr[:, i, :], lambda i: None, sq_done, root)
        splits(act)

    def splits(act):
        for u in range(2 * DC):
            act.wait_ge(turned, u + 1)
            nc.scalar.activation(hi[:, u // 2, (u % 2) * HALF:(u % 2 + 1) * HALF], bank(u), ACT.Copy,
                                 scale=ln_w[:, u // 2:u // 2 + 1]).then_inc(hi_done, 1)

    def vector(dve):
        if not squared:
            dve.wait_ge(root, 1)
        inverse_root(nc, dve, stats, 0, RMS_EPS, 1.0 / D, rc, nw)
        for i in range(TT):
            nc.vector.tensor_scalar(xr[:, i, :], src[:, i, :], stats[:, i, 3:4], None, ALU.mult).then_inc(scaled, 1)
        for u in range(2 * DC):
            toks = slice((u % 2) * HALF, (u % 2 + 1) * HALF)
            dve.wait_ge(hi_done, u + 1)
            nc.vector.scalar_tensor_tensor(out=lo[:, u // 2, toks], in0=bank(u), scalar=ln_w[:, u // 2:u // 2 + 1],
                                           in1=hi[:, u // 2, toks].bitcast(F32), op0=ALU.mult,
                                           op1=ALU.subtract).then_inc(lo_done, 1)

    def tensor(pe):
        for u in range(2 * DC):
            for k in range(per_bank):
                i = (u % 2) * per_bank + k
                pe.wait_ge(scaled, i + 1)
                mm = nc.tensor.transpose(bank(u)[:, k * P:(k + 1) * P], xr[:, i, (u // 2) * P:(u // 2 + 1) * P],
                                         keep["ident"][:])
            mm.then_inc(turned, 1)

    return scalar, vector, tensor, (hi, lo), lo_done


def shared_buffers(nc, ctx, keep):
    keep["own"] = ctx.enter_context(nc.sbuf_tensor("own", [P, NM_R, P], BF16))
    keep["ln2"] = ctx.enter_context(nc.sbuf_tensor("ln2", [P, DC], F32))
    keep["gate"] = ctx.enter_context(nc.sbuf_tensor("gate", [P, DC, NE], F32))
    keep["ld_expert"] = [ctx.enter_context(nc.semaphore(f"ld_expert{j}")) for j in range(GM)]
    keep["ld_small"] = ctx.enter_context(nc.semaphore("ld_small"))


def attention_block(nc, ctx, d, keep, ps):
    def sb(name, shape, dt=F32):
        return ctx.enter_context(nc.sbuf_tensor(name, shape, dt))

    def sem(name):
        return ctx.enter_context(nc.semaphore(f"a_{name}"))

    def split(name, shape):
        return sb(f"a_{name}h", shape, F32R), sb(f"a_{name}l", shape, F32R)

    x1, hid, ident, identb, mask = (keep[k] for k in ("x1", "hid", "ident", "identb", "mask"))
    lnw = keep["ln1"]
    raw, own = keep["raw"], keep["own"]
    w = split("w", [P, GH, PACK])
    q, k_ = split("q", [P, 2, T]), split("k", [P, 2, T])
    v = split("v", [P, 2, TT, 2 * HD])
    p = sb("a_p", [P, BATCH, 3 * P])
    pT = split("pT", [P, 2, 3 * P])
    o = split("o", [P, GH, T])
    nmax, sums, rs = (sb(f"a_{n}", [P, 4, 2]) for n in ("nmax", "sums", "rs"))

    ld_w = keep["ld_attn"]
    wh_done, w_done = sem("wh_done"), sem("w_done")
    hid_ready = sem("hid_ready")
    own_ones, own_done = sem("own_ones"), sem("own_done")
    sq_done, root = sem("sq_done"), sem("root")
    r_ready, rh_done, r_free = sem("r_ready"), sem("rh_done"), sem("r_free")
    s_ready, max_done, exp_done = sem("s_ready"), sem("max_done"), sem("exp_done")
    rs_done, norm_done = sem("rs_done"), sem("norm_done")
    pT_ready, ph_done, pl_done = sem("pT_ready"), sem("ph_done"), sem("pl_done")
    o_ready, oh_done, ol_done = sem("o_ready"), sem("oh_done"), sem("ol_done")

    rms_scalar, rms_vector, rms_tensor, xn, xn_done = rms_plan(nc, ctx, keep, ps, x1, lnw, "a_rms", 2, squared=True)

    FIRST = 8
    PER_GROUP = 6 * GH + TT

    def unit(g, j, u):
        return g * PER_GROUP + (FIRST + 6 * j + u)

    def units_of(g, j):
        last = isinstance(g, int) and g == NG - 1
        return range(0) if last and j == GH - 1 else range(4) if last and j == GH - 2 else range(6)

    def out_unit(g, i):
        return unit(g, 0, i + 6 * GH - (8 if isinstance(g, int) and g == NG - 1 else 0))

    def ring(u):
        return ps[:, u % 2, :]

    def target(j_next, pair_next, tile0, u, part):
        if u < 4:
            return (q, k_)[u // 2][part][:, j_next % 2, (u % 2) * HALF:(u % 2 + 1) * HALF]
        first = tile0 + 2 * (u - 4)
        return v[part][:, pair_next % 2, first:first + 2, :].rearrange("p t d -> p (t d)")

    def step_target(j, u, part):
        return target(j + 1, j // 2 + 1, 4 * (j % 2), u, part)

    def first_target(u, part):
        return target(0, 0, 0, u, part)

    with nc.Block() as block:
        @block.sync
        def _(sp):
            with sp.Fori(1, NG + 1) as g:
                for j in range(GH):
                    sp.wait_ge(w_done, g * GH + (j + 1 - GH))
                    sp.dma_start(raw[:, j, :], d["attn_w"][bass.ds(g * GH + j, 1)].rearrange("a p n -> (a p) n")
                                 ).then_inc(ld_w[j], 16)
            sp.dma_start(keep["ln2"][:], d["ln2"]).then_inc(keep["ld_small"], 16)
            sp.dma_start(keep["gate"][:], d["gate"]).then_inc(keep["ld_small"], 16)
            for j in range(GM):
                if j < GH:
                    sp.wait_ge(w_done, NG * GH + j + 1)
                sp.dma_start(raw[:, j, 0:FPACK], d["expert_w"][j]).then_inc(keep["ld_expert"][j], 16)

        @block.gpsimd
        def _(pool):
            def pack(k, j):
                pool.wait_ge(wh_done, k + 1)
                nc.gpsimd.tensor_tensor(w[1][:, j, :], raw[:, j, :], w[0][:, j, :].bitcast(F32),
                                        ALU.subtract).then_inc(w_done, 1)

            for j in range(GH):
                pack(j, j)
            nc.gpsimd.tensor_copy(hid[:], x1[:]).then_inc(hid_ready, 1)
            nc.gpsimd.memset(own[:], 1.0).then_inc(own_ones, 1)
            pool.wait_ge(own_ones, 1)
            for part in range(3):
                rows = own[NW * part:NW * (part + 1), :, :]
                for sign, base in ((1, 0), (-1, EI - 1)):
                    nc.gpsimd.affine_select(out=rows, in_=rows, compare_op=ALU.is_ge, fill=0.0, base=base,
                                            pattern=[[sign * P, NM_R], [sign, P]], channel_multiplier=-sign * EI
                                            ).then_inc(own_done, 1)
                    pool.wait_ge(own_done, 2 * part + (1 if sign > 0 else 2))
            with pool.Fori(1, NG + 1) as g:
                for j in range(GH):
                    pack(g * GH + j, j)

        @block.tensor
        def _(pe):
            rms_tensor(pe)
            pe.wait_ge(xn_done, 2 * DC)

            def project(n, u, j_next, pair_next, tile0):
                if not (isinstance(n, int) and n < 2):
                    pe.wait_ge(r_free, n - 1)
                bank = ring(u)
                if u < 4:
                    for c in range(DC):
                        at = ((u // 2) * DC + c) * HD
                        toks = slice((u % 2) * HALF, (u % 2 + 1) * HALF)
                        mm = three_passes(nc, bank, [x[:, j_next % GH, at:at + HD] for x in w],
                                          [x[:, c, toks] for x in xn], c == 0, c == DC - 1)
                else:
                    for half in range(2):
                        i = tile0 + 2 * (u - 4) + half
                        for c in range(DC):
                            j = 2 * (pair_next % 2) + c
                            mm = three_passes(nc, bank[:, half * 2 * HD:(half + 1) * 2 * HD],
                                              [x[:, c, i * P:(i + 1) * P] for x in xn],
                                              [x[:, j, 512:768] for x in w], c == 0, c == DC - 1)
                mm.then_inc(r_ready, 1)

            def scores(n, j, b):
                if not (isinstance(n, int) and n < 2):
                    pe.wait_ge(exp_done, n - 1)
                bank, t0 = ps[:, 2 + b % 2, :], b * SEQ
                nc.tensor.matmul(bank[:, 0:3 * P], identb[:], mask[:], start=True, stop=False, skip_group_check=True)
                for first, keys, cols in ((t0, P, slice(0, P)), (t0 + P, SEQ, slice(P, 3 * P))):
                    mm = three_passes(nc, bank[:, cols], [x[:, j % 2, first:first + P] for x in q],
                                      [x[:, j % 2, t0:t0 + keys] for x in k_], False, True)
                mm.then_inc(s_ready, 1)

            def turn(n, b):
                pe.wait_ge(norm_done, n + 1)
                if not (isinstance(n, int) and n < 2):
                    pe.wait_ge(pl_done, n - 1)
                for blk in range(3):
                    mm = nc.tensor.transpose(ps[:, 4 + b % 2, blk * P:(blk + 1) * P], p[:, b, blk * P:(blk + 1) * P],
                                             ident[:])
                mm.then_inc(pT_ready, 1)

            def weigh(n, j, b):
                pe.wait_ge(pl_done, n + 1)
                if not (isinstance(n, int) and n < 2):
                    pe.wait_ge(ol_done, n - 1)
                bank, cols = ps[:, 6 + b % 2, :], slice((j % 2) * HD, (j % 2 + 1) * HD)
                vs = [[x[:, j // 2, 2 * b + kt, cols] for x in v] for kt in range(2)]
                three_passes(nc, bank[:, 0:SEQ], vs[0], [x[:, b % 2, 0:2 * P] for x in pT], True, False)
                three_passes(nc, bank[:, P:SEQ], vs[1], [x[:, b % 2, 2 * P:3 * P] for x in pT], False,
                             True).then_inc(o_ready, 1)

            def outputs(g):
                pe.wait_ge(ol_done, g * (GH * BATCH) + GH * BATCH)
                pe.wait_ge(w_done, g * GH + 2 * GH)
                for i in range(TT):
                    pe.wait_ge(r_free, out_unit(g, i) - 1)
                    for j in range(GH):
                        mm = three_passes(nc, ring(i)[:, 0:D], [x[:, j, i * P:(i + 1) * P] for x in o],
                                          [x[:, j, 768:1024] for x in w], j == 0, j == GH - 1)
                    mm.then_inc(r_ready, 1)

            LAST, AHEAD = NG - 1, 4

            def last_output(i, heads):
                bank, cols = ps[:, (i // 2) % 2, :], slice((i % 2) * D, (i % 2 + 1) * D)
                for j in heads:
                    mm = three_passes(nc, bank[:, cols], [x[:, j, i * P:(i + 1) * P] for x in o],
                                      [x[:, j, 768:1024] for x in w], j == 0 and i % 2 == 0, j == GH - 1)
                return mm

            def early_output(i):
                if i == 0:
                    pe.wait_ge(r_free, out_unit(LAST, 0))
                    pe.wait_ge(ol_done, LAST * (GH * BATCH) + (GH - 1) * BATCH)
                    pe.wait_ge(w_done, LAST * GH + 2 * GH - 1)
                last_output(i, range(GH - 1))

            def last_outputs():
                pe.wait_ge(ol_done, (LAST + 1) * (GH * BATCH))
                pe.wait_ge(w_done, LAST * GH + 2 * GH)
                for i in range(0, TT, 2):
                    if i >= AHEAD:
                        pe.wait_ge(r_free, out_unit(LAST, i - AHEAD + 1) + 1)
                    last_output(i, [GH - 1] if i < AHEAD else range(GH))
                    last_output(i + 1, [GH - 1] if i < AHEAD else range(GH)).then_inc(r_ready, 2)

            pe.wait_ge(w_done, 1)
            for u in range(4):
                project(u, u, 0, 0, 0)
            pe.wait_ge(w_done, 2)
            for u in range(4, FIRST):
                project(u, u, 0, 0, 0)
                if u >= FIRST - 2:
                    pe.wait_ge(r_free, 4)
                    scores(u - (FIRST - 2), 0, u - (FIRST - 2))

            def step(g, j):
                n = g * (GH * BATCH) + j * BATCH
                units = units_of(g, j)

                def fill(u):
                    if u in units:
                        if u == 0:
                            pe.wait_ge(w_done, g * GH + (j + 2))
                        if u == 4:
                            pe.wait_ge(w_done, g * GH + (2 * (j // 2) + 4))
                        project(unit(g, j, u), u, j + 1, j // 2 + 1, 4 * (j % 2))

                if not units:
                    scores(n + 2, j, 2)
                    turn(n, 0)
                    scores(n + 3, j, 3)
                    turn(n + 1, 1)
                    early_output(0)
                    weigh(n, j, 0)
                    turn(n + 2, 2)
                    early_output(1)
                    weigh(n + 1, j, 1)
                    turn(n + 3, 3)
                    early_output(2)
                    weigh(n + 2, j, 2)
                    early_output(3)
                    weigh(n + 3, j, 3)
                    return
                fill(0)
                scores(n + 2, j, 2)
                turn(n, 0)
                fill(1)
                weigh(n, j, 0)
                scores(n + 3, j, 3)
                turn(n + 1, 1)
                fill(2)
                weigh(n + 1, j, 1)
                turn(n + 2, 2)
                fill(3)
                weigh(n + 2, j, 2)
                turn(n + 3, 3)
                fill(4)
                pe.wait_ge(r_free, unit(g, j, 3) + 1)
                scores(n + BATCH, j + 1, 0)
                weigh(n + 3, j, 3)
                scores(n + (BATCH + 1), j + 1, 1)
                fill(5)

            for j in range(GH):
                step(0, j)
            outputs(0)
            with pe.Fori(1, NG - 1) as g:
                for j in range(GH):
                    step(g, j)
                outputs(g)
            for j in range(GH):
                step(NG - 1, j)
            last_outputs()

        @block.scalar
        def _(act):
            def pack(j, loads):
                act.wait_ge(ld_w[j], loads)
                nc.scalar.activation(w[0][:, j, :], raw[:, j, :], ACT.Copy).then_inc(wh_done, 1)

            def high(n, u, out):
                act.wait_ge(r_ready, n + 1)
                nc.scalar.activation(out, ring(u), ACT.Copy, scale=QSCALE if u < 2 else 1.0).then_inc(rh_done, 1)

            def exps(n, b):
                act.wait_ge(max_done, n + 1)
                if not (isinstance(n, int) and n < BATCH):
                    act.wait_ge(pT_ready, n + (1 - BATCH))
                for t, cols in ((0, slice(0, P)), (1, slice(P, 3 * P))):
                    e = nc.scalar.activation(p[:, b, cols], ps[:, 2 + b % 2, cols], ACT.Exp,
                                             bias=nmax[:, b, t:t + 1], accum_out=sums[:, b, t:t + 1])
                e.then_inc(exp_done, 1)

            def high_p(n, b):
                act.wait_ge(pT_ready, n + 1)
                if not (isinstance(n, int) and n < 2):
                    act.wait_ge(o_ready, n - 1)
                nc.scalar.activation(pT[0][:, b % 2, :], ps[:, 4 + b % 2, 0:3 * P], ACT.Copy).then_inc(ph_done, 1)

            def high_o(n, j, b):
                act.wait_ge(o_ready, n + 1)
                nc.scalar.activation(o[0][:, j, b * SEQ:(b + 1) * SEQ], ps[:, 6 + b % 2, 0:SEQ],
                                     ACT.Copy).then_inc(oh_done, 1)

            act.wait_ge(keep["ld_ln1"], 16)
            pack(0, 16)
            pack(1, 16)
            rms_scalar(act)
            pack(2, 16)
            pack(3, 16)
            nc.scalar.preload_act_table_set("exp_and_others")
            for u in range(FIRST):
                high(u, u, first_target(u, 0))
                if u >= FIRST - 2:
                    exps(u - (FIRST - 2), u - (FIRST - 2))

            def step(g, j):
                n = g * (GH * BATCH) + j * BATCH
                units = units_of(g, j)

                def fill(u):
                    if u in units:
                        high(unit(g, j, u), u, step_target(j, u, 0))

                if not units:
                    high_p(n, 0)
                    exps(n + 2, 2)
                    high_p(n + 1, 1)
                    exps(n + 3, 3)
                    high_o(n, j, 0)
                    high_p(n + 2, 2)
                    high_o(n + 1, j, 1)
                    high_p(n + 3, 3)
                    high_o(n + 2, j, 2)
                    pack(j, g * 16 + 32)
                    high_o(n + 3, j, 3)
                    return
                fill(0)
                high_p(n, 0)
                exps(n + 2, 2)
                fill(1)
                high_o(n, j, 0)
                high_p(n + 1, 1)
                exps(n + 3, 3)
                fill(2)
                high_o(n + 1, j, 1)
                high_p(n + 2, 2)
                pack(j, g * 16 + 32)
                fill(3)
                high_o(n + 2, j, 2)
                high_p(n + 3, 3)
                fill(4)
                exps(n + BATCH, 0)
                high_o(n + 3, j, 3)
                exps(n + (BATCH + 1), 1)
                fill(5)

            for j in range(GH):
                step(0, j)
            with act.Fori(1, NG - 1) as g:
                for j in range(GH):
                    step(g, j)
            for j in range(GH):
                step(NG - 1, j)
            nc.scalar.preload_act_table_set("sqrt_and_others")
            squares(nc, act, keep, lambda i: hid[:, i, :], lambda i: v[0][:, 0, i, :],
                    lambda i: act.wait_ge(r_free, out_unit(NG - 1, i) + 1), sq_done, root)

        @block.vector
        def _(dve):
            rms_vector(dve)

            def low(n, u, out, high):
                dve.wait_ge(rh_done, n + 1)
                bank = ring(u)
                if u < 2:
                    mm = nc.vector.scalar_tensor_tensor(out=out, in0=bank, scalar=QSCALE, in1=high.bitcast(F32),
                                                        op0=ALU.mult, op1=ALU.subtract)
                else:
                    mm = nc.vector.tensor_tensor(out, bank, high.bitcast(F32), ALU.subtract)
                mm.then_inc(r_free, 1)

            def maxes(n, b):
                dve.wait_ge(s_ready, n + 1)
                for t, cols in ((0, slice(0, P)), (1, slice(P, 3 * P))):
                    m = nc.vector.tensor_reduce(nmax[:, b, t:t + 1], ps[:, 2 + b % 2, cols], AX.X, ALU.max, negate=True)
                m.then_inc(max_done, 1)

            def normalize(n, b):
                dve.wait_ge(exp_done, n + 1)
                nc.vector.reciprocal(rs[:, b, :], sums[:, b, :]).then_inc(rs_done, 1)
                dve.wait_ge(rs_done, n + 1)
                for t, cols in ((0, slice(0, P)), (1, slice(P, 3 * P))):
                    m = nc.vector.tensor_scalar(p[:, b, cols], p[:, b, cols], rs[:, b, t:t + 1], None, ALU.mult)
                m.then_inc(norm_done, 1)

            def low_p(n, b):
                dve.wait_ge(ph_done, n + 1)
                nc.vector.tensor_tensor(pT[1][:, b % 2, :], ps[:, 4 + b % 2, 0:3 * P], pT[0][:, b % 2, :].bitcast(F32),
                                        ALU.subtract).then_inc(pl_done, 1)

            def low_o(n, j, b):
                toks = slice(b * SEQ, (b + 1) * SEQ)
                dve.wait_ge(oh_done, n + 1)
                nc.vector.tensor_tensor(o[1][:, j, toks], ps[:, 6 + b % 2, 0:SEQ], o[0][:, j, toks].bitcast(F32),
                                        ALU.subtract).then_inc(ol_done, 1)

            def add_output(g):
                if isinstance(g, int) and g == 0:
                    dve.wait_ge(hid_ready, 1)
                for i in range(TT):
                    dve.wait_ge(r_ready, out_unit(g, i) + 1)
                    last = isinstance(g, int) and g == NG - 1
                    mixed = ps[:, (i // 2) % 2, (i % 2) * D:(i % 2 + 1) * D] if last else ring(i)[:, 0:D]
                    nc.vector.tensor_tensor(hid[:, i, :], hid[:, i, :], mixed, ALU.add).then_inc(r_free, 1)

            for u in range(FIRST):
                low(u, u, first_target(u, 1), first_target(u, 0))
                if u >= FIRST - 2:
                    maxes(u - (FIRST - 2), u - (FIRST - 2))
            normalize(0, 0)

            def step(g, j):
                n = g * (GH * BATCH) + j * BATCH
                units = units_of(g, j)

                def fill(u):
                    if u in units:
                        low(g * (6 * GH) + (FIRST + 6 * j + u), u, step_target(j, u, 1), step_target(j, u, 0))

                if not units:
                    maxes(n + 2, 2)
                    low_p(n, 0)
                    normalize(n + 1, 1)
                    maxes(n + 3, 3)
                    low_p(n + 1, 1)
                    normalize(n + 2, 2)
                    low_o(n, j, 0)
                    low_p(n + 2, 2)
                    normalize(n + 3, 3)
                    low_o(n + 1, j, 1)
                    low_p(n + 3, 3)
                    low_o(n + 2, j, 2)
                    low_o(n + 3, j, 3)
                    return
                maxes(n + 2, 2)
                fill(0)
                low_p(n, 0)
                normalize(n + 1, 1)
                fill(1)
                low_o(n, j, 0)
                maxes(n + 3, 3)
                low_p(n + 1, 1)
                normalize(n + 2, 2)
                fill(2)
                low_o(n + 1, j, 1)
                low_p(n + 2, 2)
                normalize(n + 3, 3)
                fill(3)
                low_o(n + 2, j, 2)
                low_p(n + 3, 3)
                fill(4)
                maxes(n + BATCH, 0)
                maxes(n + (BATCH + 1), 1)
                low_o(n + 3, j, 3)
                normalize(n + BATCH, 0)
                fill(5)

            for j in range(GH):
                step(0, j)
            add_output(0)
            with dve.Fori(1, NG - 1) as g:
                for j in range(GH):
                    step(g, j)
                add_output(g)
            for j in range(GH):
                step(NG - 1, j)
            add_output(NG - 1)


def expert_block(nc, ctx, d, keep, ps, out):
    def sb(name, shape, dt=F32):
        return ctx.enter_context(nc.sbuf_tensor(name, shape, dt))

    def sem(name):
        return ctx.enter_context(nc.semaphore(f"e_{name}"))

    def split(name, shape):
        return sb(f"e_{name}h", shape, F32R), sb(f"e_{name}l", shape, F32R)

    x1, hid, ident, identb, raw, own, gate_raw = (keep[k] for k in ("x1", "hid", "ident", "identb", "raw", "own", "gate"))
    ld_w = keep["ld_expert"]
    gate = split("gate", [P, DC, NE])
    w = split("w", [P, GM, FPACK])
    lgT = sb("e_lgT", [NE, T])
    lg, ex, gt, eq, cum = (sb(f"e_{n}", [P, TT, NE]) for n in ("lg", "ex", "gt", "eq", "cum"))
    top = sb("e_top", [P, TT, 8])
    cnt, tot = sb("e_cnt", [P, TT, 1]), sb("e_tot", [P, TT, 1])
    wf = sb("e_wf", [P, TT, NE])
    wr = sb("e_wr", [P, TT, NE])
    wp = sb("e_wp", [P, TT, P], BF16)
    wT = sb("e_wT", [P, T], BF16)
    sg = sb("e_sg", [P, 2, HALF])
    aw = sb("e_aw", [P, 2, HALF])
    a = split("a", [P, GM, T])

    rms_scalar, rms_vector, rms_tensor, xn, xn_done = rms_plan(nc, ctx, keep, ps, hid, keep["ln2"], "e_rms", 0,
                                                               squared=True)

    wh_done, w_done = sem("wh_done"), sem("w_done")
    dh_done, d_done = sem("dh_done"), sem("d_done")
    gh_done, gl_done = sem("gh_done"), sem("gl_done")
    lgT_ready, lgT_done = sem("lgT_ready"), sem("lgT_done")
    lg_ready, rt, ex_done = sem("lg_ready"), sem("rt"), sem("ex_done")
    wp_clear, wp_done, wT_ready, wT_done = sem("wp_clear"), sem("wp_done"), sem("wT_ready"), sem("wT_done")
    g_ready, u_ready = sem("g_ready"), sem("u_ready")
    sg_done, up_done, aw_done = sem("sg_done"), sem("up_done"), sem("aw_done")
    ah_done, al_done = sem("ah_done"), sem("al_done")
    dn_ready, dn_free = sem("dn_ready"), sem("dn_free")
    x_added = sem("x_added")
    st, ag, sq, rc, nw, ln, stored = (sem(n) for n in ("stat", "aggr", "sqrt", "rec", "newton", "ln", "stored"))

    N_SH = 2 * SH_TILES
    LN_PARTS = 2
    DOWN_AT = [[k] for k in range(GM - 2)] + [[GM - 2, GM - 1], []]

    with nc.Block() as block:
        @block.sync
        def _(sp):
            with sp.Fori(1, NMG + 1) as g:
                for j in range(GM):
                    sp.wait_ge(w_done, g * GM + (j + 1 - GM))
                    sp.dma_start(raw[:, j, 0:FPACK], d["expert_w"][bass.ds(g * GM + j, 1)].rearrange(
                        "a p n -> (a p) n")).then_inc(ld_w[j], 16)
            for i in range(TT):
                sp.wait_ge(ln, i + 1)
                sp.dma_start(out[:, i, :], hid[:, i, :]).then_inc(stored, 16)
            sp.wait_ge(stored, 16 * TT)

        @block.gpsimd
        def _(pool):
            pool.wait_ge(gh_done, 1)
            nc.gpsimd.tensor_tensor(gate[1][:], gate_raw[:], gate[0][:].bitcast(F32), ALU.subtract).then_inc(gl_done, 1)

            def rest(j, k, cols, high, low):
                pool.wait_ge(high, j + 1)
                nc.gpsimd.tensor_tensor(w[1][:, k, cols], raw[:, k, cols], w[0][:, k, cols].bitcast(F32),
                                        ALU.subtract).then_inc(low, 1)

            for k in range(GM):
                rest(k, k, slice(0, 2 * D), wh_done, w_done)
                if k == 0:
                    nc.gpsimd.memset(wp[:], 0.0).then_inc(wp_clear, 1)
            pool.wait_ge(xn_done, 2 * DC)
            nc.gpsimd.tensor_tensor(hid[:], hid[:], x1[:], ALU.add).then_inc(x_added, 1)
            with pool.Fori(0, NMG) as g:
                for k in range(GM):
                    for kd in DOWN_AT[k]:
                        rest(g * GM + kd, kd, slice(2 * D, 3 * D), dh_done, d_done)
                    rest(g * GM + (k + GM), k, slice(0, 2 * D), wh_done, w_done)

        @block.tensor
        def _(pe):
            rms_tensor(pe)
            pe.wait_ge(gl_done, 1)
            for c in range(DC):
                for th in range(2):
                    pe.wait_ge(xn_done, 2 * c + th + 1)
                    mm = three_passes(nc, ps[0:NE, 4 + th, :], [x[:, c, :] for x in gate],
                                      [x[:, c, th * HALF:(th + 1) * HALF] for x in xn], c == 0, c == DC - 1)
            mm.then_inc(lgT_ready, 1)

            def gate_up(g, k, th):
                n = g * (2 * GM) + (2 * k + th)
                toks = slice(th * HALF, (th + 1) * HALF)
                known = isinstance(n, int)
                shared = known and n < N_SH
                if th == 0:
                    pe.wait_ge(w_done, g * GM + (k + 1))
                for o, ready in enumerate((g_ready, u_ready)):
                    if not (known and n < 2):
                        if o == 0:
                            pe.wait_ge(sg_done, n - 1)
                        elif known and n - 2 < N_SH:
                            pe.wait_ge(aw_done, n - 1)
                        else:
                            pe.wait_ge(up_done, n - (1 + N_SH))
                    for c in range(DC):
                        at = o * D + c * P
                        mm = three_passes(nc, ps[:, 2 * o + th, :], [x[:, k, at:at + P] for x in w],
                                          [x[:, c, toks] for x in xn], c == 0, c == DC - 1)
                    if o == 0 or shared:
                        mm.then_inc(ready, 1)
                if not shared:
                    if known and n == N_SH:
                        pe.wait_ge(wT_done, 1)
                    pe.wait_ge(aw_done, n - 1)
                    rows = own[:, bass.ds(g * GM + (k - SH_TILES), 1), :].rearrange("p a n -> p (a n)")
                    nc.tensor.matmul(ps[:, 4 + th, :], rows, wT[:, toks], start=True, stop=True).then_inc(u_ready, 1)

            def turn_logits():
                pe.wait_ge(lgT_done, 2)
                for i in range(TT):
                    mm = nc.tensor.transpose(ps[:, 6, i * NE:(i + 1) * NE], lgT[:, i * P:(i + 1) * P],
                                             ident[0:NE, 0:NE])
                mm.then_inc(lg_ready, 1)

            def turn_weights():
                pe.wait_ge(wp_done, 1)
                turned = ps[:, 6, :].bitcast(BF16)
                for i in range(TT):
                    mm = nc.tensor.transpose(turned[:, i * P:(i + 1) * P], wp[:, i, :], identb[:])
                mm.then_inc(wT_ready, 1)

            def down(g, i):
                n = g * TT + i
                if not (isinstance(g, int) and g == 0 and i < 2):
                    pe.wait_ge(dn_free, n - 1)
                for k in range(GM):
                    if i in (0, TT // 2):
                        pe.wait_ge(al_done, g * (2 * GM) + (2 * k + (i > 0) + 1))
                    mm = three_passes(nc, ps[:, 6 + i % 2, 0:D], [x[:, k, i * P:(i + 1) * P] for x in a],
                                      [x[:, k, 2 * D:3 * D] for x in w], k == 0, k == GM - 1)
                mm.then_inc(dn_ready, 1)

            def group(g):
                for k in range(GM):
                    first = isinstance(g, int) and g == 0
                    gate_up(g, k, 0)
                    if first and k == 0:
                        turn_logits()
                    gate_up(g, k, 1)
                    if first and k == SH_TILES - 1:
                        turn_weights()
                pe.wait_ge(d_done, g * GM + GM)
                for i in range(TT):
                    down(g, i)

            group(0)
            with pe.Fori(1, NMG) as g:
                group(g)

        @block.scalar
        def _(act):
            act.wait_ge(keep["ld_small"], 32)
            nc.scalar.activation(gate[0][:], gate_raw[:], ACT.Copy).then_inc(gh_done, 1)

            def high_w(k, loads):
                act.wait_ge(ld_w[k], loads)
                nc.scalar.activation(w[0][:, k, 0:2 * D], raw[:, k, 0:2 * D], ACT.Copy).then_inc(wh_done, 1)

            def high_d(g, k):
                act.wait_ge(ld_w[k], g * 16 + 32)
                if k == 0 and not (isinstance(g, int) and g == 0):
                    act.wait_ge(dn_ready, g * TT)
                nc.scalar.activation(w[0][:, k, 2 * D:3 * D], raw[:, k, 2 * D:3 * D], ACT.Copy).then_inc(dh_done, 1)

            high_w(0, 16)
            rms_scalar(act)
            for k in range(1, GM):
                high_w(k, 16)
            act.wait_ge(rt, 2)
            nc.scalar.activation(ex[:], ex[:], ACT.Exp).then_inc(ex_done, 1)

            def silu(n, th):
                act.wait_ge(g_ready, n + 1)
                if not (isinstance(n, int) and n < 2):
                    act.wait_ge(aw_done, n - 1)
                nc.scalar.activation(sg[:, th, :], ps[:, th, :], ACT.Silu).then_inc(sg_done, 1)

            def high(n, k, th):
                act.wait_ge(aw_done, n + 1)
                nc.scalar.activation(a[0][:, k, th * HALF:(th + 1) * HALF], aw[:, th, :], ACT.Copy).then_inc(ah_done, 1)

            def group(g):
                for k in range(GM):
                    n = g * (2 * GM) + 2 * k
                    silu(n, 0)
                    if k == GM - 1:
                        high(n, k, 0)
                    silu(n + 1, 1)
                    for kd in DOWN_AT[k]:
                        high_d(g, kd)
                    if k < GM - 1:
                        high(n, k, 0)
                    high(n + 1, k, 1)
                    high_w(k, g * 16 + 32)

            group(0)
            with act.Fori(1, NMG) as g:
                group(g)
            for part in range(LN_PARTS):
                tiles = slice(part * TT // LN_PARTS, (part + 1) * TT // LN_PARTS)
                act.wait_ge(ag, tiles.stop)
                nc.scalar.activation(keep["stats"][:, tiles, 2], keep["stats"][:, tiles, 1], ACT.Sqrt,
                                     bias=keep["eps"][:, 0:1]).then_inc(sq, 1)

        @block.vector
        def _(dve):
            rms_vector(dve)
            step = [0]

            def chain(ins):
                step[0] += 1
                ins.then_inc(rt, 1)
                dve.wait_ge(rt, step[0])

            for th in range(2):
                dve.wait_ge(lgT_ready, 1)
                nc.vector.tensor_copy(lgT[:, th * HALF:(th + 1) * HALF], ps[0:NE, 4 + th, :]).then_inc(lgT_done, 1)
            fourth = top[:, :, TOPK - 1:TOPK].to_broadcast([P, TT, NE])

            def top_logits():
                dve.wait_ge(lg_ready, 1)
                chain(nc.vector.tensor_copy(lg[:], ps[:, 6, 0:TT * NE].rearrange("p (t e) -> p t e", e=NE)))
                for i in range(TT):
                    m = nc.vector.max(top[:, i, :], lg[:, i, :])
                m.then_inc(ex_done, 1)
                dve.wait_ge(ex_done, 1)
                chain(nc.vector.tensor_tensor(ex[:], lg[:], top[:, :, 0:1].to_broadcast([P, TT, NE]), ALU.subtract))

            def chosen():
                chain(nc.vector.tensor_tensor(gt[:], lg[:], fourth, ALU.is_gt))
                chain(nc.vector.tensor_tensor(eq[:], lg[:], fourth, ALU.is_equal))
                chain(nc.vector.tensor_reduce(cnt[:, :, 0], gt[:], AX.X, ALU.add))
                for i in range(TT):
                    m = nc.vector.tensor_tensor_scan(cum[:, i, :], eq[:, i, :], eq[:, i, :], cnt[:, i, 0:1],
                                                     ALU.bypass, ALU.add)
                chain(m)
                chain(nc.vector.tensor_scalar(cum[:], cum[:], float(TOPK), None, ALU.is_le))
                chain(nc.vector.tensor_tensor(eq[:], eq[:], cum[:], ALU.mult))
                chain(nc.vector.tensor_tensor(gt[:], gt[:], eq[:], ALU.add))

            def routing_weights():
                dve.wait_ge(ex_done, 2)
                chain(nc.vector.tensor_tensor(ex[:], ex[:], gt[:], ALU.mult))
                chain(nc.vector.tensor_reduce(tot[:, :, 0], ex[:], AX.X, ALU.add))
                chain(nc.vector.reciprocal(tot[:], tot[:]))
                chain(nc.vector.tensor_tensor(wf[:], ex[:], tot[:].to_broadcast([P, TT, NE]), ALU.mult))
                dve.wait_ge(wp_clear, 1)
                chain(nc.vector.tensor_copy(wp[:, :, 0:NE], wf[:]))
                chain(nc.vector.tensor_tensor(wr[:], wf[:], wp[:, :, 0:NE], ALU.subtract))
                chain(nc.vector.tensor_copy(wp[:, :, NW:NW + NE], wr[:]))
                chain(nc.vector.tensor_tensor(wr[:], wr[:], wp[:, :, NW:NW + NE], ALU.subtract))
                nc.vector.tensor_copy(wp[:, :, 2 * NW:2 * NW + NE], wr[:]).then_inc(wp_done, 1)

            def products(n, th):
                dve.wait_ge(u_ready, n + 1)
                dve.wait_ge(sg_done, n + 1)
                if isinstance(n, int) and n < N_SH:
                    if n >= 2:
                        dve.wait_ge(ah_done, n - 1)
                        dve.wait_ge(al_done, n - 1)
                    nc.vector.tensor_tensor(aw[:, th, :], sg[:, th, :], ps[:, 2 + th, :], ALU.mult).then_inc(aw_done, 1)
                    return
                nc.vector.tensor_tensor(sg[:, th, :], sg[:, th, :], ps[:, 2 + th, :], ALU.mult).then_inc(up_done, 1)
                dve.wait_ge(up_done, n + (1 - N_SH))
                dve.wait_ge(ah_done, n - 1)
                dve.wait_ge(al_done, n - 1)
                nc.vector.tensor_tensor(aw[:, th, :], sg[:, th, :], ps[:, 4 + th, :], ALU.mult).then_inc(aw_done, 1)

            def low(n, k, th):
                toks = slice(th * HALF, (th + 1) * HALF)
                dve.wait_ge(ah_done, n + 1)
                nc.vector.tensor_tensor(a[1][:, k, toks], aw[:, th, :], a[0][:, k, toks].bitcast(F32),
                                        ALU.subtract).then_inc(al_done, 1)

            def add_down(g, i):
                dve.wait_ge(dn_ready, g * TT + (i + 1))
                nc.vector.tensor_tensor(hid[:, i, :], hid[:, i, :], ps[:, 6 + i % 2, 0:D], ALU.add).then_inc(dn_free, 1)

            def tiles(g):
                for k in range(GM):
                    n = g * (2 * GM) + 2 * k
                    first = isinstance(g, int) and g == 0
                    if first and k == 0:
                        top_logits()
                    if first and k == 1:
                        chosen()
                    if first and k == 2:
                        routing_weights()
                    products(n, 0)
                    if k == GM - 1:
                        low(n, k, 0)
                    products(n + 1, 1)
                    if k < GM - 1:
                        low(n, k, 0)
                    low(n + 1, k, 1)
                    if first and k == SH_TILES - 1:
                        dve.wait_ge(wT_ready, 1)
                        nc.vector.tensor_copy(wT[:], ps[:, 6, :].bitcast(BF16)).then_inc(wT_done, 1)

            tiles(0)
            dve.wait_ge(x_added, 1)
            for i in range(TT):
                add_down(0, i)
            with dve.Fori(1, NMG - 1) as g:
                tiles(g)
                for i in range(TT):
                    add_down(g, i)
            tiles(NMG - 1)

            def last_sum(i):
                add_down(NMG - 1, i)
                dve.wait_ge(dn_free, (NMG - 1) * TT + i + 1)

            layernorm(nc, dve, hid, hid, keep, last_sum, st, ag, sq, rc, nw, ln, LN_PARTS)


def constants(nc, ctx):
    def sb(name, shape, dt=F32):
        return ctx.enter_context(nc.sbuf_tensor(name, shape, dt))

    keep = {
        "x1": sb("x1", [P, TT, D]),
        "hid": sb("hid", [P, TT, D]),
        "ident": sb("ident", [P, P]),
        "identb": sb("identb", [P, P], BF16),
        "mask": sb("mask", [P, 3 * P], BF16),
        "bn": sb("bn", [P, TT, 6]),
        "stats": sb("stats", [P, TT, 6]),
        "eps": sb("eps", [P, 2]),
        "raw": sb("raw", [P, GM, PACK]),
        "ln1": sb("ln1", [P, DC]),
    }
    keep["ld_attn"] = [ctx.enter_context(nc.semaphore(f"ld_attn{j}")) for j in range(GH)]
    keep["ld_ln1"] = ctx.enter_context(nc.semaphore("ld_ln1"))
    made, shaped = ctx.enter_context(nc.semaphore("c_made")), ctx.enter_context(nc.semaphore("c_shaped"))
    with nc.Block() as block:
        @block.gpsimd
        def _(pool):
            nc.gpsimd.memset(keep["ident"][:], 0.0).then_inc(made, 1)
            nc.gpsimd.memset(keep["eps"][:, 0:1], LN_EPS).then_inc(made, 1)
            nc.gpsimd.memset(keep["eps"][:, 1:2], RMS_EPS).then_inc(made, 1)
            pool.wait_ge(made, 3)
            nc.gpsimd.affine_select(out=keep["ident"][:], in_=keep["ident"][:], compare_op=ALU.not_equal, fill=1.0,
                                    base=0, pattern=[[-1, P]], channel_multiplier=1).then_inc(shaped, 1)
            pool.wait_ge(shaped, 1)
    return keep


def program(nc, d, out):
    with ExitStack() as ctx:
        ps = ctx.enter_context(nc.psum_tensor("ps", [P, 8, 512], F32))
        keep = constants(nc, ctx)
        with ExitStack() as part:
            mamba_block(nc, part, d, keep, ps)
        shared_buffers(nc, ctx, keep)
        with ExitStack() as part:
            attention_block(nc, part, d, keep, ps)
        with ExitStack() as part:
            expert_block(nc, part, d, keep, ps, out)


def layouts(i):
    f = {k: np.asarray(v) for k, v in i.items()}
    x = f["L0_attn_x"].reshape(T, D)

    def t_chunks(w):
        return w.T.reshape(-1, P, w.shape[0]).transpose(1, 0, 2)

    def per_channel(v):
        return v.reshape(EC, P, -1).transpose(1, 0, 2)

    w_x = f["L0_attn_W_x"]
    bc = w_x[DT_RANK:]
    q_w = f["L0_ffn_q_w"].reshape(NH, HD + ROPE, D)[:, :HD]
    kv = f["L0_ffn_kv_w"]
    k_w, v_w = kv[:NH * HD].reshape(NH, HD, D), kv[NH * HD:2 * NH * HD].reshape(NH // 2, 2 * HD, D)
    o_w = f["L0_ffn_o_w"].reshape(D, NH, HD)
    attn_w = np.zeros((NH + GH, P, PACK), np.float32)
    for h in range(NH):
        attn_w[h, :, 0:256] = t_chunks(q_w[h]).reshape(P, -1)
        attn_w[h, :, 256:512] = t_chunks(k_w[h]).reshape(P, -1)
        attn_w[h, :, 512:768] = t_chunks(v_w[h // 2])[:, h % 2]
        attn_w[h + GH, :, 768:1024] = o_w[:, h].T
    w1, sh = f["L0_ffn_w1"], f["L0_ffn_sh_gu_w"]
    rows = np.zeros((3, NM * P, D), np.float32)
    routed = SH_TILES * P
    for n in range(2):
        rows[n, :SHI] = sh[n * SHI:(n + 1) * SHI]
        rows[n, routed:] = w1[:, n * EI:(n + 1) * EI].reshape(-1, D)
    rows[2, :SHI] = f["L0_ffn_sh_down_w"].T
    rows[2, routed:] = f["L0_ffn_w2"].transpose(0, 2, 1).reshape(-1, D)
    expert_w = np.zeros((NM + GM, P, FPACK), np.float32)
    for m in range(NM):
        for n in range(2):
            expert_w[m, :, n * D:(n + 1) * D] = t_chunks(rows[n, m * P:(m + 1) * P]).reshape(P, -1)
        expert_w[m + GM, :, 2 * D:] = rows[2, m * P:(m + 1) * P]
    a = {
        "attn_w": attn_w, "expert_w": expert_w,
        "ln1": f["L0_ffn_ln1_w"].reshape(DC, P).T, "ln2": f["L0_ffn_ln2_w"].reshape(DC, P).T,
        "gate": t_chunks(f["L0_ffn_gate_w"]),
        "xT": t_chunks(x),
        "x_tok": x.reshape(TT, P, D).transpose(1, 0, 2),
        "w_in": t_chunks(f["L0_attn_W_in"]),
        "chan": np.concatenate([per_channel(f[k]) for k in (
            "L0_attn_conv_w", "L0_attn_conv_b", "L0_attn_b_dt", "L0_attn_Dp", "L0_attn_A_log")], axis=2),
        "w_x": t_chunks(np.concatenate([w_x[:DT_RANK], bc, bc, bc, bc])),
        "w_dt": f["L0_attn_W_dt"].T,
        "w_out": t_chunks(f["L0_attn_W_out"]),
    }
    return {k: np.ascontiguousarray(v) for k, v in a.items()}


def kernel(**inputs):
    import concourse.bacc as bacc
    from concourse.bass_utils import run_bass_kernel_spmd

    arrays = layouts(inputs)
    nc = bacc.Bacc("TRN2", target_bir_lowering=False, num_devices=1)
    d = {k: nc.dram_tensor(f"in_{k}", v.shape, mybir.dt.from_np(v.dtype), kind="ExternalInput").ap()
         for k, v in arrays.items()}
    out = nc.dram_tensor("out", (P, TT, D), F32, kind="ExternalOutput").ap()
    program(nc, d, out)
    r = run_bass_kernel_spmd(nc, [{f"in_{k}": v for k, v in arrays.items()}], core_ids=[0])
    got = r.results[0]["out"]
    return got.transpose(1, 0, 2).reshape(BATCH, SEQ, D)
```
